# Optimizing a Trainium2 kernel written in Bass

```python
import numpy as np
import jax
import jax.numpy as jnp

def _softmax(x, axis=-1):
    return jax.nn.softmax(x, axis=axis)

def _gelu(x):
    return jax.nn.gelu(x, approximate=True)

def _silu(x):
    return jax.nn.silu(x)

def _sigmoid(x):
    return jax.nn.sigmoid(x)

def _layernorm(x, axis=-1, eps=1e-05):
    m = jnp.mean(x, axis=axis, keepdims=True)
    v = jnp.var(x, axis=axis, keepdims=True)
    return (x - m) / jnp.sqrt(v + eps)

def _scatter_add(tgt, idx, src, axis=0):
    return tgt.at[idx].add(src)

def _segment_sum(src, seg, n):
    return jax.ops.segment_sum(src, seg, n)
kernel_name = 'mk_vit_tower_postln_d1_tok_img256_r4_991035'

def setup_inputs(seed: int=0):
    np.random.seed(seed)
    _w = jnp.asarray

    def _rec_inputs():
        import jax
        import jax.numpy as jnp
        _rk = jax.random.key(seed)
        x = -0.000222058 + 0.999998 * jax.random.normal(jax.random.fold_in(_rk, 1), (16, 3, 128, 128), jnp.float32)
        return x
    x = _rec_inputs()

    def _L0_tok_setup():
        import jax, jax.numpy as jnp
        import numpy as np
        P = 16
        NUM_HEADS = 8
        WINDOW = 64

        def _layer_norm(x, w, b, eps=1e-05):
            mu = jnp.mean(x, axis=-1, keepdims=True)
            var = jnp.var(x, axis=-1, keepdims=True)
            return (x - mu) * jax.lax.rsqrt(var + eps) * w + b

        def _sinusoidal_pe(num_patches, num_features, dtype):
            pos = jnp.arange(num_patches, dtype=jnp.float32)[:, None]
            i = jnp.arange(0, num_features, 2, dtype=jnp.float32)
            div = jnp.exp(-jnp.log(10000.0) * i / num_features)
            ang = pos * div
            pe = jnp.stack([jnp.sin(ang), jnp.cos(ang)], axis=-1).reshape(num_patches, num_features)
            return pe.astype(dtype)

        def _ffn(x, w1, b1, w2, b2):
            h = jax.nn.gelu(jnp.einsum('bnd,hd->bnh', x, w1) + b1)
            return jnp.einsum('bnh,dh->bnd', h, w2) + b2

        def _windowed_attention(x, qkv_w, qkv_b, proj_w, proj_b):
            B, N, D = x.shape
            hd = D // NUM_HEADS
            qkv = jnp.einsum('bnd,ed->bne', x, qkv_w) + qkv_b
            qkv = qkv.reshape(B, N, 3, NUM_HEADS, hd)
            q, k, v = (qkv[:, :, 0], qkv[:, :, 1], qkv[:, :, 2])
            nw = N // WINDOW
            q = q.reshape(B, nw, WINDOW, NUM_HEADS, hd).transpose(0, 3, 1, 2, 4)
            k = k.reshape(B, nw, WINDOW, NUM_HEADS, hd).transpose(0, 3, 1, 2, 4)
            v = v.reshape(B, nw, WINDOW, NUM_HEADS, hd).transpose(0, 3, 1, 2, 4)
            scale = 1.0 / jnp.sqrt(jnp.asarray(hd, x.dtype))
            scores = jnp.einsum('bhwqd,bhwkd->bhwqk', q, k) * scale
            attn = jax.nn.softmax(scores, axis=-1)
            out = jnp.einsum('bhwqk,bhwkd->bhwqd', attn, v)
            out = out.transpose(0, 2, 3, 1, 4).reshape(B, N, D)
            return jnp.einsum('bnd,ed->bne', out, proj_w) + proj_b
        key = jax.random.key(seed)
        ks = jax.random.split(key, 8)
        D, HF = (64, 256)
        s = lambda fan: 1.0 / np.sqrt(fan)
        return {'x': jax.random.normal(ks[0], (32, 3, 128, 128), jnp.float32), 'conv_w': jax.random.normal(ks[1], (D, 3, P, P), jnp.float32) * s(3 * P * P), 'conv_b': jnp.zeros((D,), jnp.float32), 'ln_w': jnp.ones((D,), jnp.float32), 'ln_b': jnp.zeros((D,), jnp.float32), 'qkv_w': jax.random.normal(ks[2], (3 * D, D), jnp.float32) * s(D), 'qkv_b': jnp.zeros((3 * D,), jnp.float32), 'proj_w': jax.random.normal(ks[3], (D, D), jnp.float32) * s(D), 'proj_b': jnp.zeros((D,), jnp.float32), 'ff_w1': jax.random.normal(ks[4], (HF, D), jnp.float32) * s(D), 'ff_b1': jnp.zeros((HF,), jnp.float32), 'ff_w2': jax.random.normal(ks[5], (D, HF), jnp.float32) * s(HF), 'ff_b2': jnp.zeros((D,), jnp.float32)}
    _L0_tok_all = _L0_tok_setup()
    _L0_tok_in = {k: v for k, v in _L0_tok_all.items() if k in ('conv_w', 'conv_b', 'ln_w', 'ln_b', 'qkv_w', 'qkv_b', 'proj_w', 'proj_b', 'ff_w1', 'ff_b1', 'ff_w2', 'ff_b2')}
    del _L0_tok_all

    def _L0_attn_setup():
        import jax, jax.numpy as jnp
        import numpy as np
        import math
        EMBED_DIM = 64
        SEQ_LEN = 1024
        BATCH = 4
        NUM_SCALES = (24.0, 720.0)
        key = jax.random.key(seed)
        ks = jax.random.split(key, 8)
        d = EMBED_DIM
        x = jax.random.normal(ks[0], (BATCH, SEQ_LEN, d), dtype=jnp.float32)
        s = 1.0 / math.sqrt(d)
        Wq = jax.random.uniform(ks[1], (d, d), jnp.float32, -s, s)
        bq = jax.random.uniform(ks[2], (d,), jnp.float32, -s, s)
        Wk = jax.random.uniform(ks[3], (d, d), jnp.float32, -s, s)
        bk = jax.random.uniform(ks[4], (d,), jnp.float32, -s, s)
        Wv = jax.random.uniform(ks[5], (d, d), jnp.float32, -s, s)
        bv = jax.random.uniform(ks[6], (d,), jnp.float32, -s, s)
        beta = jnp.ones((len(NUM_SCALES),), dtype=jnp.float32)
        return {'x': x, 'Wq': Wq, 'bq': bq, 'Wk': Wk, 'bk': bk, 'Wv': Wv, 'bv': bv, 'beta': beta}
    _L0_attn_all = _L0_attn_setup()
    _L0_attn_in = {k: v for k, v in _L0_attn_all.items() if k in ('Wq', 'bq', 'Wk', 'bk', 'Wv', 'bv', 'beta')}
    del _L0_attn_all

    def _L0_ffn_setup():
        import jax, jax.numpy as jnp
        import numpy as np
        B, T, C = (64, 96, 64)
        NH, NKV = (4, 2)
        HD = C // NH
        NREP = NH // NKV
        NE, TOPK = (8, 2)
        HID = int(8 / 3 * C)
        EPS_RMS = 1e-06

        def _rope_tables(t_len):
            inv_freq = 1.0 / 10000.0 ** (np.arange(0, HD, 2, dtype=np.float32) / HD)
            t = np.arange(t_len, dtype=np.float32)
            freqs = np.outer(t, inv_freq)
            emb = np.concatenate([freqs, freqs], axis=-1)
            return (jnp.asarray(np.cos(emb)), jnp.asarray(np.sin(emb)))

        def _rotate_half(x):
            h = x.shape[-1] // 2
            return jnp.concatenate([-x[..., h:], x[..., :h]], axis=-1)

        def _rmsnorm(v, w):
            return v * jax.lax.rsqrt(jnp.mean(v * v, axis=-1, keepdims=True) + EPS_RMS) * w
        key = jax.random.key(seed)
        ks = jax.random.split(key, 10)
        s = lambda k, shape: jax.random.normal(k, shape, jnp.float32) * 0.02
        return {'x': jax.random.normal(ks[0], (B, T, C), jnp.float32), 'ln1_w': jnp.ones((C,), jnp.float32), 'ln2_w': jnp.ones((C,), jnp.float32), 'wq': s(ks[1], (NH * HD, C)), 'wk': s(ks[2], (NKV * HD, C)), 'wv': s(ks[3], (NKV * HD, C)), 'wo': s(ks[4], (C, C)), 'router_w': s(ks[5], (NE, C)), 'w1': s(ks[6], (NE, HID, C)), 'w2': s(ks[7], (NE, C, HID)), 'w3': s(ks[8], (NE, HID, C))}
    _L0_ffn_all = _L0_ffn_setup()
    _L0_ffn_in = {k: v for k, v in _L0_ffn_all.items() if k in ('ln1_w', 'ln2_w', 'wq', 'wk', 'wv', 'wo', 'router_w', 'w1', 'w2', 'w3')}
    del _L0_ffn_all
    return {'x': x, 'L0_tok_conv_w': _L0_tok_in['conv_w'], 'L0_tok_conv_b': _L0_tok_in['conv_b'], 'L0_tok_ln_w': _L0_tok_in['ln_w'], 'L0_tok_ln_b': _L0_tok_in['ln_b'], 'L0_tok_qkv_w': _L0_tok_in['qkv_w'], 'L0_tok_qkv_b': _L0_tok_in['qkv_b'], 'L0_tok_proj_w': _L0_tok_in['proj_w'], 'L0_tok_proj_b': _L0_tok_in['proj_b'], 'L0_tok_ff_w1': _L0_tok_in['ff_w1'], 'L0_tok_ff_b1': _L0_tok_in['ff_b1'], 'L0_tok_ff_w2': _L0_tok_in['ff_w2'], 'L0_tok_ff_b2': _L0_tok_in['ff_b2'], 'L0_attn_Wq': _L0_attn_in['Wq'], 'L0_attn_bq': _L0_attn_in['bq'], 'L0_attn_Wk': _L0_attn_in['Wk'], 'L0_attn_bk': _L0_attn_in['bk'], 'L0_attn_Wv': _L0_attn_in['Wv'], 'L0_attn_bv': _L0_attn_in['bv'], 'L0_attn_beta': _L0_attn_in['beta'], 'L0_ffn_ln1_w': _L0_ffn_in['ln1_w'], 'L0_ffn_ln2_w': _L0_ffn_in['ln2_w'], 'L0_ffn_wq': _L0_ffn_in['wq'], 'L0_ffn_wk': _L0_ffn_in['wk'], 'L0_ffn_wv': _L0_ffn_in['wv'], 'L0_ffn_wo': _L0_ffn_in['wo'], 'L0_ffn_router_w': _L0_ffn_in['router_w'], 'L0_ffn_w1': _L0_ffn_in['w1'], 'L0_ffn_w2': _L0_ffn_in['w2'], 'L0_ffn_w3': _L0_ffn_in['w3']}

def reference(x, L0_tok_conv_w, L0_tok_conv_b, L0_tok_ln_w, L0_tok_ln_b, L0_tok_qkv_w, L0_tok_qkv_b, L0_tok_proj_w, L0_tok_proj_b, L0_tok_ff_w1, L0_tok_ff_b1, L0_tok_ff_w2, L0_tok_ff_b2, L0_attn_Wq, L0_attn_bq, L0_attn_Wk, L0_attn_bk, L0_attn_Wv, L0_attn_bv, L0_attn_beta, L0_ffn_ln1_w, L0_ffn_ln2_w, L0_ffn_wq, L0_ffn_wk, L0_ffn_wv, L0_ffn_wo, L0_ffn_router_w, L0_ffn_w1, L0_ffn_w2, L0_ffn_w3):
    import jax
    import jax.numpy as jnp

    def _L0_tok_ref(x, conv_w, conv_b, ln_w, ln_b, qkv_w, qkv_b, proj_w, proj_b, ff_w1, ff_b1, ff_w2, ff_b2):
        import jax, jax.numpy as jnp
        import numpy as np
        P = 16
        NUM_HEADS = 8
        WINDOW = 64

        def _layer_norm(x, w, b, eps=1e-05):
            mu = jnp.mean(x, axis=-1, keepdims=True)
            var = jnp.var(x, axis=-1, keepdims=True)
            return (x - mu) * jax.lax.rsqrt(var + eps) * w + b

        def _sinusoidal_pe(num_patches, num_features, dtype):
            pos = jnp.arange(num_patches, dtype=jnp.float32)[:, None]
            i = jnp.arange(0, num_features, 2, dtype=jnp.float32)
            div = jnp.exp(-jnp.log(10000.0) * i / num_features)
            ang = pos * div
            pe = jnp.stack([jnp.sin(ang), jnp.cos(ang)], axis=-1).reshape(num_patches, num_features)
            return pe.astype(dtype)

        def _ffn(x, w1, b1, w2, b2):
            h = jax.nn.gelu(jnp.einsum('bnd,hd->bnh', x, w1) + b1)
            return jnp.einsum('bnh,dh->bnd', h, w2) + b2

        def _windowed_attention(x, qkv_w, qkv_b, proj_w, proj_b):
            B, N, D = x.shape
            hd = D // NUM_HEADS
            qkv = jnp.einsum('bnd,ed->bne', x, qkv_w) + qkv_b
            qkv = qkv.reshape(B, N, 3, NUM_HEADS, hd)
            q, k, v = (qkv[:, :, 0], qkv[:, :, 1], qkv[:, :, 2])
            nw = N // WINDOW
            q = q.reshape(B, nw, WINDOW, NUM_HEADS, hd).transpose(0, 3, 1, 2, 4)
            k = k.reshape(B, nw, WINDOW, NUM_HEADS, hd).transpose(0, 3, 1, 2, 4)
            v = v.reshape(B, nw, WINDOW, NUM_HEADS, hd).transpose(0, 3, 1, 2, 4)
            scale = 1.0 / jnp.sqrt(jnp.asarray(hd, x.dtype))
            scores = jnp.einsum('bhwqd,bhwkd->bhwqk', q, k) * scale
            attn = jax.nn.softmax(scores, axis=-1)
            out = jnp.einsum('bhwqk,bhwkd->bhwqd', attn, v)
            out = out.transpose(0, 2, 3, 1, 4).reshape(B, N, D)
            return jnp.einsum('bnd,ed->bne', out, proj_w) + proj_b
        B, C, H, W = x.shape
        D = conv_w.shape[0]
        nH, nW = (H // P, W // P)
        patches = x.reshape(B, C, nH, P, nW, P).transpose(0, 2, 4, 1, 3, 5).reshape(B, nH * nW, C * P * P)
        h = jnp.einsum('bnp,dp->bnd', patches, conv_w.reshape(D, -1)) + conv_b
        h = _layer_norm(h, ln_w, ln_b)
        h = h + _sinusoidal_pe(h.shape[1], D, h.dtype)
        identity = h
        h = _ffn(h, ff_w1, ff_b1, ff_w2, ff_b2)
        h = _windowed_attention(h, qkv_w, qkv_b, proj_w, proj_b)
        h = h + identity
        identity = h
        h = _ffn(h, ff_w1, ff_b1, ff_w2, ff_b2)
        return h + identity

    def _L0_attn_ref(x, Wq, bq, Wk, bk, Wv, bv, beta):
        import jax, jax.numpy as jnp
        import numpy as np
        import math
        EMBED_DIM = 64
        SEQ_LEN = 1024
        BATCH = 4
        NUM_SCALES = (24.0, 720.0)
        d = x.shape[-1]
        seq_len = x.shape[1]
        sqrt_d = jnp.asarray(math.sqrt(d), x.dtype)
        Q = jnp.einsum('bsd,ed->bse', x, Wq) + bq
        K = jnp.einsum('bsd,ed->bse', x, Wk) + bk
        V = jnp.einsum('bsd,ed->bse', x, Wv) + bv
        attn = jnp.einsum('bse,bte->bst', Q, K) / sqrt_d
        idx = jnp.arange(seq_len, dtype=jnp.float32)
        absdiff = jnp.abs(idx[:, None] - idx[None, :])
        two_pi = jnp.asarray(2.0 * math.pi, jnp.float32)
        bias = jnp.zeros((seq_len, seq_len), dtype=jnp.float32)
        for n, T in enumerate(NUM_SCALES):
            bias = bias + beta[n] * jnp.cos(two_pi * absdiff / T)
        scores = jax.nn.softmax(attn + bias[None, :, :], axis=-1)
        return jnp.einsum('bst,bte->bse', scores, V)

    def _L0_ffn_ref(x, ln1_w, ln2_w, wq, wk, wv, wo, router_w, w1, w2, w3):
        import jax, jax.numpy as jnp
        import numpy as np
        B, T, C = (64, 96, 64)
        NH, NKV = (4, 2)
        HD = C // NH
        NREP = NH // NKV
        NE, TOPK = (8, 2)
        HID = int(8 / 3 * C)
        EPS_RMS = 1e-06

        def _rope_tables(t_len):
            inv_freq = 1.0 / 10000.0 ** (np.arange(0, HD, 2, dtype=np.float32) / HD)
            t = np.arange(t_len, dtype=np.float32)
            freqs = np.outer(t, inv_freq)
            emb = np.concatenate([freqs, freqs], axis=-1)
            return (jnp.asarray(np.cos(emb)), jnp.asarray(np.sin(emb)))

        def _rotate_half(x):
            h = x.shape[-1] // 2
            return jnp.concatenate([-x[..., h:], x[..., :h]], axis=-1)

        def _rmsnorm(v, w):
            return v * jax.lax.rsqrt(jnp.mean(v * v, axis=-1, keepdims=True) + EPS_RMS) * w
        Bx, Tx, Cx = x.shape
        h = _rmsnorm(x, ln1_w)
        q = (h @ wq.T).reshape(Bx, Tx, NH, HD).transpose(0, 2, 1, 3)
        k = (h @ wk.T).reshape(Bx, Tx, NKV, HD).transpose(0, 2, 1, 3)
        v = (h @ wv.T).reshape(Bx, Tx, NKV, HD).transpose(0, 2, 1, 3)
        cos, sin = _rope_tables(Tx)
        cos, sin = (cos[None, None], sin[None, None])
        q = q * cos + _rotate_half(q) * sin
        k = k * cos + _rotate_half(k) * sin
        k = jnp.repeat(k, NREP, axis=1)
        v = jnp.repeat(v, NREP, axis=1)
        scores = jnp.einsum('bhtd,bhsd->bhts', q, k) / jnp.sqrt(jnp.float32(HD))
        causal = jnp.tril(jnp.ones((Tx, Tx), dtype=bool))
        scores = jnp.where(causal[None, None], scores, jnp.float32(-1e+30))
        att = jax.nn.softmax(scores, axis=-1)
        y = jnp.einsum('bhts,bhsd->bhtd', att, v).transpose(0, 2, 1, 3).reshape(Bx, Tx, Cx)
        x = x + y @ wo.T
        flat = _rmsnorm(x, ln2_w).reshape(-1, Cx)
        probs = jax.nn.softmax(flat @ router_w.T, axis=-1)
        tp, ti = jax.lax.top_k(probs, TOPK)
        tp = tp / (jnp.sum(tp, axis=-1, keepdims=True) + 1e-09)
        weights = jnp.sum(tp[..., None] * jax.nn.one_hot(ti, NE, dtype=flat.dtype), axis=1)
        out = jnp.zeros_like(flat)
        for e in range(NE):
            hh = jax.nn.silu(flat @ w1[e].T) * (flat @ w3[e].T)
            out = out + weights[:, e:e + 1] * (hh @ w2[e].T)
        return x + out.reshape(Bx, Tx, Cx)
    h = _L0_tok_ref(x, L0_tok_conv_w, L0_tok_conv_b, L0_tok_ln_w, L0_tok_ln_b, L0_tok_qkv_w, L0_tok_qkv_b, L0_tok_proj_w, L0_tok_proj_b, L0_tok_ff_w1, L0_tok_ff_b1, L0_tok_ff_w2, L0_tok_ff_b2)
    h = _layernorm(h + _L0_attn_ref(h, L0_attn_Wq, L0_attn_bq, L0_attn_Wk, L0_attn_bk, L0_attn_Wv, L0_attn_bv, L0_attn_beta), axis=-1)
    h = _layernorm(h + _L0_ffn_ref(h, L0_ffn_ln1_w, L0_ffn_ln2_w, L0_ffn_wq, L0_ffn_wk, L0_ffn_wv, L0_ffn_wo, L0_ffn_router_w, L0_ffn_w1, L0_ffn_w2, L0_ffn_w3), axis=-1)
    return h

_drawn_inputs = setup_inputs


def setup_inputs(seed=0):
    import zlib

    import numpy as np

    out = dict(_drawn_inputs(seed))
    spreads = {'L0_tok_conv_b': (0.0, 0.1),
     'L0_tok_ln_w': (1.0, 0.2),
     'L0_tok_ln_b': (0.0, 0.1),
     'L0_tok_qkv_b': (0.0, 0.1),
     'L0_tok_proj_b': (0.0, 0.1),
     'L0_tok_ff_b1': (0.0, 0.1),
     'L0_tok_ff_b2': (0.0, 0.1),
     'L0_attn_beta': (1.0, 0.6),
     'L0_ffn_ln1_w': (1.0, 0.6),
     'L0_ffn_ln2_w': (1.0, 0.6)}
    factors = {'L0_attn_bq': 8.0,
     'L0_attn_bk': 8.0,
     'L0_ffn_wq': 8.0,
     'L0_ffn_wk': 8.0,
     'L0_ffn_wv': 6.651,
     'L0_ffn_wo': 6.716,
     'L0_ffn_router_w': 8.0,
     'L0_ffn_w1': 8.0,
     'L0_ffn_w2': 8.0,
     'L0_ffn_w3': 8.0}
    for name, (base, spread) in spreads.items():
        noise = np.random.default_rng([zlib.crc32(name.encode()), seed]).standard_normal(out[name].shape)
        drawn = base * np.exp(spread * noise) if base else spread * noise
        out[name] = jnp.asarray(drawn.astype(out[name].dtype))
    for name, factor in factors.items():
        out[name] = (out[name] * factor).astype(out[name].dtype)
    return out
```

```python
from contextlib import ExitStack

import concourse.bass as bass
from concourse import mybir

ALU = mybir.AluOpType
ACT = mybir.ActivationFunctionType
AX = mybir.AxisListType.X
F32 = mybir.dt.float32
F32R = mybir.dt.float32r
BF16 = mybir.dt.bfloat16

P = 128
B, C, IMG, PATCH = 16, 3, 128, 16
GRID = IMG // PATCH
N = GRID * GRID
D = 64
HALF = 64
COLS = B * N * D // P
HC = COLS // 2
KCH = C * PATCH * PATCH // P
W8 = B // 2
HEADS, HD = 8, 8
FF = 256
FH, FHD, FKV = 4, 16, 2
NE, HID = 8, 170
CH = -(-NE * HID // P)
UPBUF = 3


def experts_of(chunk):
    return range(chunk * P // HID, min((chunk * P + P - 1) // HID, NE - 1) + 1)


DOWN_AT = [D * sum(len(experts_of(ch)) for ch in range(n)) for n in range(CH + 1)]
EPS = 1e-5
EPS_RMS = 1e-6

PACK_A = dict(ident=P, conv=KCH * D, conv_b=D, pos=N, ln_w=1, ln_b=1)
PACK_B = dict(ff1=FF, ff1_b=2, ff2=2 * D, ff2_b=1, wq=P, wk=P, wv=P, proj=P, bq=1, bk=1, bv=1, bp=1,
              head_mask=HEADS)
PACK_C = dict(aq=P, ak=P, av=P, abq=1, abk=1, abv=D, beta=2, cosines=2 * N,
              fq=P, fq_turned=P, fk=P, fk_turned=P, fv=2 * FKV * FHD, fo=P, router=NE, rope_cos=N, rope_sin=N,
              causal=FH * N, fhead_mask=FH, rank=NE, ln1=1, ln2=1)
PACK_D = dict(up=2 * CH * P)
PACK_E = dict(down=DOWN_AT[CH])


def width(pack):
    return sum(pack.values())


def columns(pack, name):
    at = 0
    for key, n in pack.items():
        if key == name:
            return slice(at, at + n)
        at += n
    raise KeyError(name)


def build(nc, x, pack_a, pack_b, pack_c, pack_d, pack_e, out):
    with ExitStack() as ctx:
        def sb(name, shape, dt=F32):
            return ctx.enter_context(nc.sbuf_tensor(name, shape, dt))

        made = {}

        def sem(name):
            if name not in made:
                made[name] = ctx.enter_context(nc.semaphore(name))
            return made[name]

        PS = ctx.enter_context(nc.psum_tensor("PS", [P, 8, 512], F32))

        A = sb("pack_a_sb", [P, width(PACK_A)])
        Bp = sb("pack_b_sb", [P, width(PACK_B)])
        Cp = sb("pack_c_sb", [P, width(PACK_C)])
        up_w = sb("up_w", [P, 2 * CH * P])
        up_hi = sb("up_hi", [P, 2 * CH * P], F32R)
        up_lo = sb("up_lo", [P, 2 * CH * P], F32R)
        down_w = sb("down_w", [P, DOWN_AT[CH]])

        def a(name):
            return A[:, columns(PACK_A, name)]

        def b(name):
            return Bp[:, columns(PACK_B, name)]

        def c(name):
            return Cp[:, columns(PACK_C, name)]

        shared_x = sb("shared_x", [P, KCH * 1024])
        shared_p = sb("shared_p", [P, 4 * COLS])
        shared_f = sb("shared_f", [P, 4 * COLS])
        shared_h = sb("shared_h", [P, CH * 2 * COLS])
        x_sb = shared_x[:, :].rearrange("q (k c) -> q k c", k=KCH)
        patches = shared_p[:, :].rearrange("q (k c) -> q k c", k=2)
        x_patches = shared_f[:, :].rearrange("q (k c) -> q k c", k=2)
        emb = sb("emb", [P, COLS])
        centred = sb("centred", [P, COLS])
        squares = sb("squares", [P, COLS])
        normed = sb("normed", [P, COLS])
        sums = sb("sums", [P, 8])
        sq_sums = sb("sq_sums", [P, 8])
        var = sb("var", [P, 8])
        rstd = sb("rstd", [P, 8])
        spare = sb("spare", [P, 1])
        minus_half = sb("minus_half", [P, 8])
        pos_b = sb("pos_b", [P, N])
        proj_bias = sb("proj_bias", [P, 1])
        h0 = sb("h0", [P, COLS])
        hidden = shared_f[:, :].rearrange("q (m s c) -> q m s c", m=2, s=2)
        f1 = sb("f1", [P, COLS])
        h2 = sb("h2", [P, COLS])
        h3 = sb("h3", [P, COLS])
        q_diag = sb("q_diag", [P, W8, 2, N])
        kf = sb("kf", [P, COLS])
        k_heads = shared_h[:, 0:W8 * HEADS * N].rearrange("q (w h n) -> q w h n", w=W8, h=HEADS)
        vo = sb("vo", [P, 2, W8, 4, 2, HD + 1])
        r1 = sb("r1", [P, W8, HEADS])
        top = sb("top", [P, 2, HEADS])
        shifted = sb("shifted", [P, 2, COLS])
        probs = sb("probs", [P, 2, COLS])
        attended = sb("attended", [P, COLS])
        bias = sb("bias", [P, N])
        q2_diag = sb("q2_diag", [P, W8, 2, N])
        k2 = sb("k2", [P, COLS])
        v2 = sb("v2", [P, W8, D + 1])
        s2 = sb("s2", [P, COLS])
        on = s2[:, :].rearrange("q (w d) -> q w d", d=D)
        s2_top = sb("s2_top", [P, W8])
        s2_shift = sb("s2_shift", [P, COLS])
        p2 = sb("p2", [P, 4, P])
        r2 = sb("r2", [P, W8])
        o2 = attended
        sum2 = h2
        h4 = sb("h4", [P, COLS])
        h4n = emb
        h4f = h0
        rope = shared_f[:, :].rearrange("q (k c) -> q k c", k=4)
        kr = sb("kr", [P, COLS])
        q3_diag = sb("q3_diag", [P, W8, 2, N])
        vo3 = sb("vo3", [P, 2, W8, FKV, 2, FHD + 1])
        k3_heads = shared_x[:, 0:W8 * FH * N].rearrange("q (w h n) -> q w h n", w=W8, h=FH)
        causal_bf = sb("causal_bf", [P, FH * N], BF16)
        ident_bf = sb("ident_bf", [P, P], BF16)
        attended3 = attended
        h5 = f1
        h45 = emb
        h5n = normed
        parts = q_diag
        xf = sb("xf", [P, 2, COLS], F32R)
        router_s = sb("router_s", [P, NE])
        router_hi = sb("router_hi", [P, NE], F32R)
        router_lo = sb("router_lo", [P, NE], F32R)
        gate = shared_f[:, 0:UPBUF * COLS].rearrange("q (k c) -> q k c", k=UPBUF)
        hh = shared_h[:, 0:CH * 2 * COLS].rearrange("q (c s t) -> q c s t", c=CH, s=2)
        small = {k: sb("r_" + k, [P, 8, NE]) for k in
                 ("shift", "exp", "prob", "same1", "rank1", "one1", "prob2", "same2", "rank2", "one2",
                  "part1", "part2", "both", "weights")}
        few = {k: sb("r_" + k, [P, 8]) for k in
               ("top", "sum", "rsum", "first", "first_rank", "second", "second_rank", "total", "total_eps", "rtotal")}
        weighted = shared_p[:, 2 * COLS:].rearrange("q (k e d) -> q k e d", k=2, e=NE)
        mixed = s2[:, :].rearrange("q (u s d) -> q u s d", u=4, s=2)
        h6 = s2_shift[:, :].rearrange("q (u s d) -> q u s d", u=4, s=2)
        out_sb = k2[:, :].rearrange("q (s u d) -> q s u d", s=2, u=4)

        def tiles(t):
            return t[:, :].rearrange("q (t d) -> q t d", d=D)

        def half(t, g):
            return t[:, g * HC:(g + 1) * HC]

        def vo_part(h2, p, g):
            return vo[HALF * h2:HALF * h2 + HALF, p, 4 * g:4 * g + 4, :, h2, 0:HD]

        def vo3_part(h2, p, g):
            return vo3[HALF * h2:HALF * h2 + HALF, p, 4 * g:4 * g + 4, :, h2, 0:FHD]

        UP_BANKS = (3, 6, 0)
        DOWN_BANKS = (5, 2, 3, 4)

        block = ctx.enter_context(nc.Block())

        @block.sync
        def _(sp):
            def load_x(k):
                ch, ph = k // 2, k % 2
                rows = x[:, ch].rearrange("b (i r) w -> b i (r w)", i=GRID)[:, :, ph * 1024:(ph + 1) * 1024]
                sp.dma_start(x_sb[:, k, :], rows).then_inc(sem(f"x_loaded{k}"), 16)

            sp.dma_start(A[:, :], pack_a).then_inc(sem("pack_a_loaded"), 16)
            for k in range(KCH):
                load_x(k)
            sp.dma_start(Bp[:, :], pack_b).then_inc(sem("pack_b_loaded"), 16)
            sp.dma_start(up_w[:, :], pack_d).then_inc(sem("up_w_loaded"), 16)
            sp.dma_start(Cp[:, :], pack_c).then_inc(sem("pack_c_loaded"), 16)
            sp.dma_start(down_w[:, :], pack_e).then_inc(sem("down_w_loaded"), 16)
            for s in range(2):
                sp.wait_ge(sem("out_normed"), s + 1)
                dst = out.rearrange("(s u p) n d -> s u (p n) d", s=2, p=2)[s].rearrange("u q d -> q u d")
                sp.dma_start(dst, out_sb[:, s]).then_inc(sem("stored"), 16)
            sp.wait_ge(sem("stored"), 32)

        @block.tensor
        def _(pe):
            mm, tp = nc.tensor.matmul, nc.tensor.transpose
            ident = a("ident")

            def conv_transposes(k):
                pe.wait_ge(sem("x_grouped"), k + 1)
                if k >= 2:
                    pe.wait_ge(sem("patches_copied_act"), k - 1)
                    pe.wait_ge(sem("patches_copied_dve"), k - 1)
                for j in range(GRID):
                    t = tp(PS[:, 2 * (k % 2) + j // 4, (j % 4) * P:(j % 4 + 1) * P], x_patches[:, k % 2, j * P:(j + 1) * P], ident)
                    if j % 4 == 3:
                        t.then_inc(sem("patches_turned"), 1)

            def conv_products(k):
                pe.wait_ge(sem("patches_copied_act"), k + 1)
                pe.wait_ge(sem("patches_copied_dve"), k + 1)
                w = a("conv")[:, k * D:(k + 1) * D]
                for j in range(GRID):
                    m = mm(PS[:, 4, j * D:(j + 1) * D], patches[:, k % 2, j * P:(j + 1) * P], w,
                           start=(k == 0 and j == 0), stop=(k == KCH - 1), skip_group_check=True)
                m.then_inc(sem("conv_summed"), 1)

            def ffn(name, src, u_banks):
                for g in range(2):
                    pe.wait_ge(sem(name + "_in"), g + 1)
                    for m in range(2):
                        for s in range(2):
                            r = slice(HALF * s, HALF * s + HALF)
                            t = mm(PS[:, u_banks[g] + s, m * HC:(m + 1) * HC], b("ff1")[r, m * P:(m + 1) * P],
                                   src[r, g * HC:(g + 1) * HC], start=True, stop=True)
                    t.then_inc(sem(name + "_up"), 1)
                for g in range(2):
                    pe.wait_ge(sem(name + "_gelu"), 2 * g + 2)
                    for s in range(2):
                        r = slice(HALF * s, HALF * s + HALF)
                        for m in range(2):
                            t = mm(PS[r, 6 + g, 0:HC], b("ff2")[:, m * D:(m + 1) * D],
                                   hidden[:, m, s, g * HC:(g + 1) * HC], start=(m == 0), stop=(m == 1))
                    t.then_inc(sem(name + "_down"), 1)

            def values(src, w, wide, bank, g):
                for u in (2 * g, 2 * g + 1):
                    at = (u % 2) * 2 * wide
                    t = mm(PS[:, bank, at:at + 2 * wide], src[:, u * P:(u + 1) * P], w, start=True, stop=True)
                return t

            pe.wait_ge(sem("pack_a_loaded"), 16)
            for k in range(KCH):
                conv_transposes(k)
                if k:
                    conv_products(k - 1)
            conv_products(KCH - 1)

            for g in range(2):
                pe.wait_ge(sem("ln0_normed"), g + 1)
                for j in range(4 * g, 4 * g + 4):
                    for s in range(2):
                        r = slice(HALF * s, HALF * s + HALF)
                        t = mm(PS[r, 5, j * D:(j + 1) * D], normed[r, j * D:(j + 1) * D], ident[r, r],
                               start=True, stop=True)
            t.then_inc(sem("emb_turned"), 1)
            pe.wait_ge(sem("pack_b_loaded"), 16)
            mm(PS[:, 6, 0:1], b("proj"), b("bv"), start=True, stop=True).then_inc(sem("proj_bv"), 1)

            ffn("ffn1", h0, (0, 2))

            for g in range(2):
                pe.wait_ge(sem("f1_ready"), g + 1)
                cols = slice(g * HC, (g + 1) * HC)
                mm(PS[:, 2 * g, 0:HC], b("wq"), f1[:, cols], start=True, stop=True).then_inc(sem("q1_mm"), 1)
                mm(PS[:, 2 * g + 1, 0:HC], b("wk"), f1[:, cols], start=True, stop=True).then_inc(sem("k1_mm"), 1)
                values(f1, b("wv"), D, 4 + g, g).then_inc(sem("v1_mm"), 1)

            def scores1(w):
                if w % 4 == 0:
                    pe.wait_ge(sem("q1_act"), w // 4 + 1)
                    pe.wait_ge(sem("q1_dve"), w // 4 + 1)
                    pe.wait_ge(sem("k1_act"), w // 4 + 1)
                    pe.wait_ge(sem("k1_dve"), w // 4 + 1)
                if w >= 2:
                    pe.wait_ge(sem("att1_shifted"), w - 1)
                mm(PS[:, 6 + w % 2, :], q_diag[:, w].rearrange("q s n -> q (s n)"),
                   k_heads[:, w].rearrange("q h n -> q (h n)"), start=True, stop=True).then_inc(sem("att1_scores"), 1)

            def turn1(w):
                pe.wait_ge(sem("att1_shifted"), w + 1)
                if w >= 2:
                    pe.wait_ge(sem("att1_probs"), w - 1)
                for ch in range(4):
                    t = tp(PS[:, w % 2, ch * P:(ch + 1) * P], shifted[:, w % 2, ch * P:(ch + 1) * P], ident)
                t.then_inc(sem("att1_turned"), 1)

            def mix1(w):
                if w % 4 == 0:
                    pe.wait_ge(sem("v1_act"), w // 4 + 1)
                    pe.wait_ge(sem("v1_dve"), w // 4 + 1)
                pe.wait_ge(sem("att1_probs"), w + 1)
                wide = 2 * (HD + 1)
                for s in range(2):
                    r = slice(HALF * s, HALF * s + HALF)
                    for ch in range(4):
                        at = ((w % 4) * 4 + ch) * wide
                        t = mm(PS[r, 4 + w // 4, at:at + wide], probs[:, w % 2, ch * P + s * HALF:ch * P + (s + 1) * HALF],
                               vo[:, w % 2, (w // 2) * 2 + s, ch].rearrange("q e d -> q (e d)"), start=True, stop=True)
                t.then_inc(sem("att1_mixed"), 1)

            pe.wait_ge(sem("vo_made"), 1)
            for w in range(W8 + 2):
                if w < W8:
                    scores1(w)
                if 1 <= w <= W8:
                    turn1(w - 1)
                if w >= 2:
                    mix1(w - 2)

            def mixed_to_features(name, bank, g):
                pe.wait_ge(sem(name + "_divided"), g + 1)
                for w in range(4 * g, 4 * g + 4):
                    for s in range(2):
                        r = slice(HALF * s, HALF * s + HALF)
                        t = mm(PS[r, bank, (w % 4) * N:(w % 4 + 1) * N], on[r, w, :], ident[r, r], start=True, stop=True)
                t.then_inc(sem(name + "_back"), 1)

            def project1(g):
                pe.wait_ge(sem("att1_ready"), g + 1)
                mm(PS[:, 2 + g, 0:HC], b("proj"), half(attended, g),
                   start=True, stop=True).then_inc(sem("proj_mm"), 1)

            for g in range(2):
                mixed_to_features("att1", g, g)
            for g in range(2):
                project1(g)
            ffn("ffn2", h2, (0, 4))

            pe.wait_ge(sem("pack_c_loaded"), 16)
            for g in range(2):
                pe.wait_ge(sem("h3_ready"), g + 1)
                cols = slice(g * HC, (g + 1) * HC)
                mm(PS[:, 4 * g, 0:HC], c("aq"), h3[:, cols], start=True, stop=True).then_inc(sem("q2_mm"), 1)
                mm(PS[:, 4 * g + 1, 0:HC], c("ak"), h3[:, cols], start=True, stop=True).then_inc(sem("k2_mm"), 1)
                values(h3, c("av"), D, 4 * g + 2, g).then_inc(sem("v2_mm"), 1)
                for u in (2 * g, 2 * g + 1):
                    t = tp(PS[:, 4 * g + 3, (u % 2) * P:(u % 2 + 1) * P], h3[:, u * P:(u + 1) * P], ident)
                t.then_inc(sem("h3_turned"), 1)
            for g in range(2):
                pe.wait_ge(sem("q2_act"), g + 1)
                pe.wait_ge(sem("k2_dve"), g + 1)
                for w in range(4 * g, 4 * g + 4):
                    t = mm(PS[:, 4 * g, (w % 4) * N:(w % 4 + 1) * N], q2_diag[:, w].rearrange("q s n -> q (s n)"),
                           k2[:, w * N:(w + 1) * N], start=True, stop=True)
                t.then_inc(sem("att2_scores"), 1)
            for g in range(2):
                pe.wait_ge(sem("att2_shifted"), g + 1)
                for u in (2 * g, 2 * g + 1):
                    t = tp(PS[:, 4 * g + 1, (u % 2) * P:(u % 2 + 1) * P], s2_shift[:, u * P:(u + 1) * P], ident)
                t.then_inc(sem("att2_turned"), 1)
            for g in range(2):
                pe.wait_ge(sem("v2_ready"), g + 1)
                pe.wait_ge(sem("att2_probs"), g + 1)
                for u in (2 * g, 2 * g + 1):
                    for s in range(2):
                        for p in range(2):
                            r = slice(HALF * p, HALF * p + HALF)
                            at = ((u % 2) * 2 + s) * (D + 1)
                            t = mm(PS[r, 4 * g + 2, at:at + D + 1], p2[r, u, s * HALF:(s + 1) * HALF],
                                   v2[r, 2 * u + s, :], start=True, stop=True)
                t.then_inc(sem("att2_mixed"), 1)

            for g in range(2):
                pe.wait_ge(sem("rms1_normed"), g + 1)
                for u in (2 * g, 2 * g + 1):
                    t = tp(PS[:, 4 * g, (u % 2) * P:(u % 2 + 1) * P], h4n[:, u * P:(u + 1) * P], ident)
                t.then_inc(sem("h4_turned"), 1)
            for g in range(2):
                pe.wait_ge(sem("h4f_ready"), g + 1)
                cols = slice(g * HC, (g + 1) * HC)
                for n, name in enumerate(("fq", "fq_turned", "fk", "fk_turned")):
                    t = mm(PS[:, 1 + 4 * g + n // 2, (n % 2) * HC:(n % 2 + 1) * HC], c(name), h4f[:, cols],
                           start=True, stop=True)
                    if n % 2:
                        t.then_inc(sem("qk3_mm"), 1)
                values(h4f, c("fv"), FKV * FHD, 3 + 4 * g, g).then_inc(sem("v3_mm"), 1)

            score_banks = (0, 4, 1, 5)

            def scores3(i):
                if i % 2 == 0:
                    pe.wait_ge(sem("q3_ready"), i + 2)
                    pe.wait_ge(sem("k3_ready"), i // 2 + 1)
                for w in (2 * i, 2 * i + 1):
                    at = PS[:, score_banks[i], (w % 2) * HC:(w % 2 + 1) * HC]
                    mm(at, ident_bf[:, :], causal_bf[:, :], start=True, stop=False)
                    t = mm(at, q3_diag[:, w].rearrange("q s n -> q (s n)"), k3_heads[:, w].rearrange("q h n -> q (h n)"),
                           start=False, stop=True)
                t.then_inc(sem("att3_scores"), 1)

            def turn3(i):
                pe.wait_ge(sem("att3_shifted"), i + 1)
                if i >= 2:
                    pe.wait_ge(sem("att3_probs"), i - 1)
                for n in range(4):
                    t = tp(PS[:, 2 + 4 * (i % 2), n * P:(n + 1) * P], shifted[:, i % 2, n * P:(n + 1) * P], ident)
                t.then_inc(sem("att3_turned"), 1)

            def mix3(i):
                if i % 2 == 0:
                    pe.wait_ge(sem("v3_ready"), i // 2 + 1)
                pe.wait_ge(sem("att3_probs"), i + 1)
                wide = 2 * (FHD + 1)
                for w in (2 * i, 2 * i + 1):
                    for s in range(2):
                        r = slice(HALF * s, HALF * s + HALF)
                        for ch in range(FKV):
                            n = (w % 2) * FKV + ch
                            at = ((w % 4) * FKV + ch) * wide
                            t = mm(PS[r, 3 + 4 * (w // 4), at:at + wide],
                                   probs[:, i % 2, n * P + s * HALF:n * P + (s + 1) * HALF],
                                   vo3[:, w % 2, (w // 2) * 2 + s, ch].rearrange("q e d -> q (e d)"), start=True, stop=True)
                t.then_inc(sem("att3_mixed"), 1)

            pe.wait_ge(sem("causal_made"), 1)
            pe.wait_ge(sem("ident_bf_made"), 1)
            for i in range(4):
                scores3(i)
            for i in range(5):
                if i < 4:
                    turn3(i)
                if i >= 1:
                    mix3(i - 1)
            for g in range(2):
                mixed_to_features("att3", 2 + 4 * g, g)
            for g in range(2):
                pe.wait_ge(sem("att3_ready"), g + 1)
                values(attended3, c("fo"), D, 4 * g, g).then_inc(sem("fo_mm"), 1)

            for g in range(2):
                pe.wait_ge(sem("parts_ready"), g + 1)
                for s in range(2):
                    for u in (2 * g, 2 * g + 1):
                        t = tp(PS[:, 1 + 4 * s, u * P:(u + 1) * P], parts[:, 2 * u + s].rearrange("q l d -> q (l d)"), ident)
            t.then_inc(sem("parts_turned"), 1)
            pe.wait_ge(sem("router_made"), 1)
            pe.wait_ge(sem("xf_ready"), 2)
            for t8 in range(8):
                u, s = t8 // 2, t8 % 2
                for n, w in enumerate((router_hi, router_lo)):
                    t = mm(PS[:, 2, t8 * NE:(t8 + 1) * NE], xf[:, s, u * P:(u + 1) * P], w[:, :],
                           start=(n == 0), stop=(n == 1))
            t.then_inc(sem("logits_mm"), 1)

            pe.wait_ge(sem("up_split"), 1)
            for s in range(2):
                for ch in range(CH):
                    n = s * CH + ch
                    if n >= UPBUF:
                        pe.wait_ge(sem("hh_ready"), n - UPBUF + 1)
                    for v in range(2):
                        at = (2 * ch + v) * P
                        mm(PS[:, UP_BANKS[n % UPBUF] + v, :], up_hi[:, at:at + P], xf[:, s, :], start=True, stop=False)
                        t = mm(PS[:, UP_BANKS[n % UPBUF] + v, :], up_lo[:, at:at + P], xf[:, s, :], start=False, stop=True)
                        t.then_inc(sem("up_mm"), 1)
            pe.wait_ge(sem("down_w_loaded"), 16)
            for n in range(8):
                s, u = n // 4, n % 4
                if n % 4 == 0:
                    pe.wait_ge(sem("hh_ready"), CH * (s + 1))
                if n == 1:
                    pe.wait_ge(sem("logits_read"), 1)
                if n == 2:
                    pe.wait_ge(sem("hh_ready"), 2 * CH)
                if n >= 4:
                    pe.wait_ge(sem("tile_weighted"), n - 3)
                bank = DOWN_BANKS[n % 4]
                tok = slice(u * P, (u + 1) * P)
                for ch in range(CH):
                    ex = experts_of(ch)
                    t = mm(PS[:, bank, ex[0] * D:(ex[-1] + 1) * D], hh[:, ch, s, tok],
                           down_w[:, DOWN_AT[ch]:DOWN_AT[ch + 1]],
                           start=(ch == 0), stop=(ch == CH - 1), skip_group_check=True)
                t.then_inc(sem("down_mm"), 1)

        @block.scalar
        def _(act):
            f = nc.scalar.activation

            for k in range(KCH):
                act.wait_ge(sem("patches_turned"), 2 * k + 1)
                if k >= 2:
                    act.wait_ge(sem("conv_summed"), k - 1)
                f(patches[:, k % 2, 0:512], PS[:, 2 * (k % 2), :], ACT.Copy).then_inc(sem("patches_copied_act"), 1)

            def squares_of(name, src):
                for g in range(2):
                    act.wait_ge(sem(name + "_centred"), g + 1)
                    f(half(squares, g), half(src, g), ACT.Square).then_inc(sem(name + "_squared"), 1)

            def gelus(name, u_banks):
                for g in range(2):
                    act.wait_ge(sem(name + "_up"), g + 1)
                    for m in range(2):
                        f(hidden[:, m, :, g * HC:(g + 1) * HC],
                          PS[:, u_banks[g]:u_banks[g] + 2, m * HC:(m + 1) * HC],
                          ACT.Gelu_apprx_tanh, bias=b("ff1_b")[:, m:m + 1]).then_inc(sem(name + "_gelu"), 1)

            squares_of("ln0", centred)
            act.wait_ge(sem("pack_b_loaded"), 16)
            gelus("ffn1", (0, 2))
            for g in range(2):
                act.wait_ge(sem("ffn1_down"), g + 1)
                f(half(f1, g), PS[:, 6 + g, 0:HC], ACT.Identity, bias=b("ff2_b")).then_inc(sem("f1_ready"), 1)

            act.wait_ge(sem("zeros_made"), 1)
            for g in range(2):
                ws = slice(4 * g, 4 * g + 4)
                cols = slice(g * HC, (g + 1) * HC)
                act.wait_ge(sem("q1_mm"), g + 1)
                f(q_diag[HALF:P, ws, 1, :], PS[HALF:P, 2 * g, 0:HC].rearrange("q (w n) -> q w n", n=N), ACT.Identity,
                  bias=b("bq")[HALF:P]).then_inc(sem("q1_act"), 1)
                act.wait_ge(sem("kf_ready"), g + 1)
                for h in range(5, 8):
                    t = f(k_heads[:, ws, h, :], half(kf, g).rearrange("q (w n) -> q w n", n=N), ACT.Copy,
                          scale=b("head_mask")[:, h:h + 1])
                t.then_inc(sem("k1_act"), 1)
                if g == 0:
                    act.wait_ge(sem("vo_made"), 1)
                act.wait_ge(sem("v1_mm"), g + 1)
                src = PS[HALF:P, 4 + g, 0:HC].rearrange("q (t c e d) -> q t c e d", t=4, c=4, e=2)
                for h2_ in range(2):
                    t = f(vo_part(h2_, 1, g), src[:, :, :, h2_, :], ACT.Copy)
                t.then_inc(sem("v1_act"), 1)

            scale1 = float(HD) ** -0.5
            for w in range(W8):
                act.wait_ge(sem("att1_turned"), w + 1)
                if w >= 2:
                    act.wait_ge(sem("att1_mixed"), w - 1)
                f(probs[:, w % 2, :], PS[:, w % 2, :], ACT.Exp, scale=scale1).then_inc(sem("att1_probs"), 1)

            for g in range(2):
                act.wait_ge(sem("att1_back"), g + 1)
                f(half(attended, g), PS[:, g, 0:HC], ACT.Copy).then_inc(sem("att1_ready"), 1)
            gelus("ffn2", (0, 4))

            act.wait_ge(sem("pack_c_loaded"), 16)
            for g in range(2):
                ws = slice(4 * g, 4 * g + 4)
                cols = slice(g * HC, (g + 1) * HC)
                act.wait_ge(sem("q2_mm"), g + 1)
                for s in range(2):
                    r = slice(HALF * s, HALF * s + HALF)
                    t = f(q2_diag[r, ws, s, :], PS[r, 4 * g, 0:HC].rearrange("q (w n) -> q w n", n=N), ACT.Identity,
                          bias=c("abq")[r])
                t.then_inc(sem("q2_act"), 1)
            for g in range(2):
                act.wait_ge(sem("att2_turned"), g + 1)
                f(p2[:, 2 * g:2 * g + 2, :], PS[:, 4 * g + 1, 0:HC].rearrange("q (u n) -> q u n", n=P),
                  ACT.Exp).then_inc(sem("att2_probs"), 1)

            squares_of("ln1", centred)
            squares_of("rms1", h4)

            for g in range(2):
                act.wait_ge(sem("h4_turned"), g + 1)
                f(half(h4f, g), PS[:, 4 * g, 0:HC], ACT.Copy, scale=c("ln1")).then_inc(sem("h4f_ready"), 1)
            act.wait_ge(sem("zeros_made"), 1)
            for g in range(2):
                act.wait_ge(sem("v3_mm"), g + 1)
                if g == 0:
                    act.wait_ge(sem("vo3_made"), 1)
                for h2_ in range(2):
                    for p in range(2):
                        src = PS[HALF * p:HALF * (p + 1), 3 + 4 * g, 0:P].rearrange(
                            "q (t c d) -> q t c d", t=4, c=FKV)
                        t = f(vo3_part(h2_, p, g), src, ACT.Copy)
                t.then_inc(sem("v3_ready"), 1)
                act.wait_ge(sem("kr_ready"), g + 1)
                for h in range(FH):
                    t = f(k3_heads[:, 4 * g:4 * g + 4, h, :], half(kr, g).rearrange("q (w n) -> q w n", n=N),
                          ACT.Copy, scale=c("fhead_mask")[:, h:h + 1])
                t.then_inc(sem("k3_ready"), 1)
            scale3 = float(FHD) ** -0.5
            for i in range(4):
                act.wait_ge(sem("att3_turned"), i + 1)
                if i >= 2:
                    act.wait_ge(sem("att3_mixed"), i - 1)
                f(probs[:, i % 2, :], PS[:, 2 + 4 * (i % 2), :], ACT.Exp, scale=scale3).then_inc(sem("att3_probs"), 1)

            for g in range(2):
                act.wait_ge(sem("att3_back"), g + 1)
                f(half(attended3, g), PS[:, 2 + 4 * g, 0:HC], ACT.Copy).then_inc(sem("att3_ready"), 1)
            squares_of("rms2", h5)
            act.wait_ge(sem("parts_turned"), 1)
            f(xf[:, 0, :], PS[:, 1, :], ACT.Copy).then_inc(sem("xf_ready"), 1)
            act.wait_ge(sem("logits_read"), 1)
            f(small["exp"][:, :, :], small["shift"][:, :, :], ACT.Exp).then_inc(sem("router_exp"), 1)
            for n in range(2 * CH):
                act.wait_ge(sem("up_mm"), 2 * n + 1)
                if n >= UPBUF:
                    act.wait_ge(sem("hh_ready"), n - UPBUF + 1)
                f(gate[:, n % UPBUF, :], PS[:, UP_BANKS[n % UPBUF], :], ACT.Silu).then_inc(sem("gated"), 1)
            for s in range(2):
                act.wait_ge(sem("lnf_centred"), s + 1)
                f(half(squares, s), half(centred, s), ACT.Square).then_inc(sem("lnf_squared"), 1)

        @block.gpsimd
        def _(pool):
            g_ = nc.gpsimd
            g_.memset(minus_half[:, :], -0.5).then_inc(sem("minus_half_made"), 1)
            g_.memset(q_diag[:, :, :, :], 0.0)
            g_.memset(q2_diag[:, :, :, :], 0.0)
            g_.memset(q3_diag[:, :, :, :], 0.0)
            g_.memset(v2[:, :, D:D + 1], 1.0).then_inc(sem("zeros_made"), 1)
            g_.memset(vo[:, :, :, :, :, :], 0.0).then_inc(sem("vo_zero"), 1)
            for h2_ in range(2):
                pool.wait_ge(sem("vo_zero"), h2_ + 1)
                g_.memset(vo[HALF * h2_:HALF * h2_ + HALF, :, :, :, h2_, HD:HD + 1], 1.0).then_inc(sem("vo_zero"), 1)
            pool.wait_ge(sem("vo_zero"), 3)
            g_.memset(spare[:, 0:1], 0.0).then_inc(sem("vo_made"), 1)

            def powers(name):
                for g in range(2):
                    pool.wait_ge(sem(name + "_var"), g + 1)
                    g_.tensor_tensor(rstd[:, 4 * g:4 * g + 4], var[:, 4 * g:4 * g + 4],
                                     minus_half[:, 4 * g:4 * g + 4], ALU.pow).then_inc(sem(name + "_rstd"), 1)

            pool.wait_ge(sem("minus_half_made"), 1)
            powers("ln0")
            g_.memset(vo3[:, :, :, :, :, :], 0.0).then_inc(sem("vo3_zero"), 1)
            for h2_ in range(2):
                pool.wait_ge(sem("vo3_zero"), h2_ + 1)
                g_.memset(vo3[HALF * h2_:HALF * h2_ + HALF, :, :, :, h2_, FHD:FHD + 1], 1.0).then_inc(sem("vo3_zero"), 1)
            pool.wait_ge(sem("vo3_zero"), 3)
            g_.memset(spare[:, 0:1], 0.0).then_inc(sem("vo3_made"), 1)

            pool.wait_ge(sem("pack_c_loaded"), 16)
            g_.tensor_scalar(router_s[:, :], c("router"), c("ln2"), None, ALU.mult).then_inc(sem("router_s"), 1)
            pool.wait_ge(sem("router_s"), 1)
            g_.tensor_copy(router_hi[:, :], router_s[:, :]).then_inc(sem("router_h"), 1)
            pool.wait_ge(sem("router_h"), 1)
            g_.tensor_tensor(router_lo[:, :], router_s[:, :], router_hi[:, :].bitcast(F32),
                             ALU.subtract).then_inc(sem("router_made"), 1)
            g_.tensor_copy(causal_bf[:, :], c("causal")).then_inc(sem("causal_made"), 1)
            g_.tensor_copy(ident_bf[:, :], a("ident")).then_inc(sem("ident_bf_made"), 1)
            pool.wait_ge(sem("up_w_loaded"), 16)
            g_.tensor_scalar(up_w[:, :], up_w[:, :], c("ln2"), None, ALU.mult).then_inc(sem("up_scaled"), 1)
            pool.wait_ge(sem("up_scaled"), 1)
            g_.tensor_copy(up_hi[:, :], up_w[:, :]).then_inc(sem("up_h"), 1)
            pool.wait_ge(sem("up_h"), 1)
            g_.tensor_tensor(up_lo[:, :], up_w[:, :], up_hi[:, :].bitcast(F32), ALU.subtract).then_inc(sem("up_split"), 1)

            powers("ln1")
            powers("rms1")
            for g in range(2):
                pool.wait_ge(sem("rope_q"), g + 1)
                for s in range(2):
                    r = slice(HALF * s, HALF * s + HALF)
                    cols = slice(g * HC, (g + 1) * HC)
                    if g or s:
                        pool.wait_ge(sem("q3_ready"), 2 * g + s)
                    g_.tensor_tensor(q3_diag[r, 4 * g:4 * g + 4, s, :],
                                     rope[r, 0, cols].rearrange("q (w n) -> q w n", n=N),
                                     rope[r, 1, cols].rearrange("q (w n) -> q w n", n=N), ALU.add)\
                        .then_inc(sem("q3_ready"), 1)
            pool.wait_ge(sem("q3_ready"), 4)
            powers("rms2")
            pool.wait_ge(sem("rms2_centred"), 2)
            g_.tensor_tensor(h45[:, :], h4[:, :], h5[:, :], ALU.add).then_inc(sem("h45_ready"), 1)
            powers("lnf")

        @block.vector
        def _(ve):
            v = nc.vector

            def centre(name, src):
                for g in range(2):
                    ve.wait_ge(sem(name + "_in"), g + 1)
                    v.reduce_sum(sums[:, 4 * g:4 * g + 4], tiles(src)[:, 4 * g:4 * g + 4], AX).then_inc(sem(name + "_sum"), 1)
                for g in range(2):
                    ts = slice(4 * g, 4 * g + 4)
                    ve.wait_ge(sem(name + "_sum"), g + 1)
                    v.scalar_tensor_tensor(out=tiles(centred)[:, ts], in0=sums[:, ts].unsqueeze(2).to_broadcast([P, 4, D]),
                                           scalar=-1.0 / D, in1=tiles(src)[:, ts], op0=ALU.mult, op1=ALU.add)\
                        .then_inc(sem(name + "_centred"), 1)

            def normalise(name, src, dst, eps):
                for g in range(2):
                    ve.wait_ge(sem(name + "_squared"), g + 1)
                    v.reduce_sum(sq_sums[:, 4 * g:4 * g + 4], tiles(squares)[:, 4 * g:4 * g + 4], AX)\
                        .then_inc(sem(name + "_sq_sum"), 1)
                for g in range(2):
                    ts = slice(4 * g, 4 * g + 4)
                    ve.wait_ge(sem(name + "_sq_sum"), g + 1)
                    v.tensor_scalar(var[:, ts], sq_sums[:, ts], 1.0 / D, eps, ALU.mult, ALU.add).then_inc(sem(name + "_var"), 1)
                for g in range(2):
                    ts = slice(4 * g, 4 * g + 4)
                    ve.wait_ge(sem(name + "_rstd"), g + 1)
                    v.tensor_tensor(dst(g), tiles(src)[:, ts], rstd[:, ts].unsqueeze(2).to_broadcast([P, 4, D]),
                                    ALU.mult).then_inc(sem(name + "_normed"), 1)

            def group(k):
                ve.wait_ge(sem(f"x_loaded{k}"), 16)
                if k >= 2:
                    ve.wait_ge(sem("patches_turned"), 2 * k - 2)
                v.tensor_copy(x_patches[:, k % 2, :].rearrange("q (j r w) -> q j r w", j=GRID, r=8),
                              x_sb[:, k, :].rearrange("q (r j w) -> q j r w", r=8, j=GRID)).then_inc(sem("x_grouped"), 1)

            group(0)
            for k in range(KCH):
                if k + 1 < KCH:
                    group(k + 1)
                ve.wait_ge(sem("patches_turned"), 2 * k + 2)
                if k >= 2:
                    ve.wait_ge(sem("conv_summed"), k - 1)
                v.tensor_copy(patches[:, k % 2, 512:1024], PS[:, 2 * (k % 2) + 1, :]).then_inc(sem("patches_copied_dve"), 1)

            ve.wait_ge(sem("pack_a_loaded"), 16)
            v.tensor_scalar(pos_b[:, :], a("pos"), a("ln_b"), None, ALU.add).then_inc(sem("pos_b_made"), 1)
            ve.wait_ge(sem("conv_summed"), KCH)
            for g in range(2):
                v.tensor_tensor(tiles(emb)[:, 4 * g:4 * g + 4], PS[:, 4, g * HC:(g + 1) * HC].rearrange("q (j d) -> q j d", d=D),
                                a("conv_b").unsqueeze(1).to_broadcast([P, 4, D]), ALU.add).then_inc(sem("ln0_in"), 1)
            centre("ln0", emb)
            normalise("ln0", centred, lambda g: tiles(normed)[:, 4 * g:4 * g + 4], EPS)
            ve.wait_ge(sem("pack_b_loaded"), 16)
            ve.wait_ge(sem("proj_bv"), 1)
            v.tensor_tensor(proj_bias[:, :], PS[:, 6, 0:1], b("bp"), ALU.add).then_inc(sem("proj_bias_made"), 1)
            ve.wait_ge(sem("emb_turned"), 1)
            ve.wait_ge(sem("pos_b_made"), 1)
            turned = PS[:, 5, :].rearrange("q (j w i) -> q w i j", j=GRID, w=W8)
            grid = pos_b[:, :].rearrange("q (i j) -> q i j", j=GRID)
            for w in range(W8):
                t = v.scalar_tensor_tensor(out=h0[:, w * N:(w + 1) * N].rearrange("q (i j) -> q i j", j=GRID),
                                           in0=turned[:, w], scalar=a("ln_w"), in1=grid, op0=ALU.mult, op1=ALU.add)
                if w % 4 == 3:
                    t.then_inc(sem("ffn1_in"), 1)

            ve.wait_ge(sem("zeros_made"), 1)
            for g in range(2):
                ws = slice(4 * g, 4 * g + 4)
                cols = slice(g * HC, (g + 1) * HC)
                ve.wait_ge(sem("q1_mm"), g + 1)
                v.tensor_scalar(q_diag[0:HALF, ws, 0, :], PS[0:HALF, 2 * g, 0:HC].rearrange("q (w n) -> q w n", n=N),
                                b("bq")[0:HALF], None, ALU.add).then_inc(sem("q1_dve"), 1)
                ve.wait_ge(sem("k1_mm"), g + 1)
                v.tensor_scalar(half(kf, g), PS[:, 2 * g + 1, 0:HC], b("bk"), None, ALU.add).then_inc(sem("kf_ready"), 1)
                ve.wait_ge(sem("kf_ready"), g + 1)
                for h in range(5):
                    t = v.tensor_scalar(k_heads[:, ws, h, :], half(kf, g).rearrange("q (w n) -> q w n", n=N),
                                        b("head_mask")[:, h:h + 1], None, ALU.mult)
                t.then_inc(sem("k1_dve"), 1)
                if g == 0:
                    ve.wait_ge(sem("vo_made"), 1)
                ve.wait_ge(sem("v1_mm"), g + 1)
                src = PS[0:HALF, 4 + g, 0:HC].rearrange("q (t c e d) -> q t c e d", t=4, c=4, e=2)
                for h2_ in range(2):
                    t = v.tensor_copy(vo_part(h2_, 0, g), src[:, :, :, h2_, :])
                t.then_inc(sem("v1_dve"), 1)

            def shift(name, bank, n):
                ve.wait_ge(sem(name + "_scores"), n + 1)
                if n >= 2:
                    ve.wait_ge(sem(name + "_turned"), n - 1)
                rows = PS[:, bank, :].rearrange("q (h n) -> q h n", n=N)
                v.reduce_max(top[:, n % 2, :], rows, AX).then_inc(sem(name + "_top"), 1)
                ve.wait_ge(sem(name + "_top"), n + 1)
                v.tensor_tensor(shifted[:, n % 2, :].rearrange("q (h n) -> q h n", n=N), rows,
                                top[:, n % 2, :].unsqueeze(2).to_broadcast([P, 8, N]), ALU.subtract)\
                    .then_inc(sem(name + "_shifted"), 1)

            def divide(name, bank, g, heads, size):
                ve.wait_ge(sem(name + "_mixed"), (4 if name == "att1" else 2) * (g + 1))
                mix = PS[:, bank, 0:4 * heads * (size + 1)].rearrange("q (w h d) -> q w h d", w=4, h=heads)
                rec = r1[:, 4 * g:4 * g + 4, 0:heads]
                v.reciprocal(rec, mix[:, :, :, size]).then_inc(sem(name + "_recip"), 1)
                ve.wait_ge(sem(name + "_recip"), g + 1)
                v.tensor_tensor(on[:, 4 * g:4 * g + 4, :].rearrange("q w (h d) -> q w h d", h=heads), mix[:, :, :, 0:size],
                                rec.unsqueeze(3).to_broadcast([P, 4, heads, size]), ALU.mult)\
                    .then_inc(sem(name + "_divided"), 1)

            for w in range(W8):
                shift("att1", 6 + w % 2, w)
                if w == 6:
                    divide("att1", 4, 0, HEADS, HD)
            divide("att1", 5, 1, HEADS, HD)

            ve.wait_ge(sem("proj_bias_made"), 1)
            for g in range(2):
                ve.wait_ge(sem("proj_mm"), g + 1)
                v.scalar_tensor_tensor(out=half(h2, g), in0=PS[:, 2 + g, 0:HC], scalar=proj_bias[:, 0:1],
                                       in1=half(h0, g), op0=ALU.add, op1=ALU.add).then_inc(sem("ffn2_in"), 1)
            ve.wait_ge(sem("pack_c_loaded"), 16)
            v.tensor_scalar(bias[:, :], c("cosines")[:, N:2 * N], c("beta")[:, 1:2], None, ALU.mult).then_inc(sem("bias_part"), 1)
            ve.wait_ge(sem("bias_part"), 1)
            v.scalar_tensor_tensor(out=bias[:, :], in0=c("cosines")[:, 0:N], scalar=c("beta")[:, 0:1], in1=bias[:, :],
                                   op0=ALU.mult, op1=ALU.add).then_inc(sem("bias_made"), 1)
            for g in range(2):
                ve.wait_ge(sem("ffn2_down"), g + 1)
                v.scalar_tensor_tensor(out=half(h3, g), in0=PS[:, 6 + g, 0:HC], scalar=b("ff2_b"),
                                       in1=half(h2, g), op0=ALU.add, op1=ALU.add).then_inc(sem("h3_ready"), 1)

            for g in range(2):
                cols = slice(g * HC, (g + 1) * HC)
                ve.wait_ge(sem("k2_mm"), g + 1)
                v.tensor_scalar(half(k2, g), PS[:, 4 * g + 1, 0:HC], c("abk"), None, ALU.add).then_inc(sem("k2_dve"), 1)
                ve.wait_ge(sem("v2_mm"), g + 1)
                v.tensor_tensor(v2[:, 4 * g:4 * g + 4, 0:D], PS[:, 4 * g + 2, 0:HC].rearrange("q (t d) -> q t d", d=D),
                                c("abv").unsqueeze(1).to_broadcast([P, 4, D]), ALU.add).then_inc(sem("v2_ready"), 1)
            ve.wait_ge(sem("bias_made"), 1)
            for g in range(2):
                ts = slice(4 * g, 4 * g + 4)
                ve.wait_ge(sem("att2_scores"), g + 1)
                v.scalar_tensor_tensor(out=tiles(s2)[:, ts], in0=PS[:, 4 * g, 0:HC].rearrange("q (w n) -> q w n", n=N),
                                       scalar=float(D) ** -0.5, in1=bias[:, :].unsqueeze(1).to_broadcast([P, 4, N]),
                                       op0=ALU.mult, op1=ALU.add).then_inc(sem("att2_biased"), 1)
            for g in range(2):
                ts = slice(4 * g, 4 * g + 4)
                ve.wait_ge(sem("att2_biased"), g + 1)
                v.reduce_max(s2_top[:, ts], tiles(s2)[:, ts], AX).then_inc(sem("att2_top"), 1)
            for g in range(2):
                ts = slice(4 * g, 4 * g + 4)
                ve.wait_ge(sem("att2_top"), g + 1)
                v.tensor_tensor(tiles(s2_shift)[:, ts], tiles(s2)[:, ts], s2_top[:, ts].unsqueeze(2).to_broadcast([P, 4, N]),
                                ALU.subtract).then_inc(sem("att2_shifted"), 1)
            for g in range(2):
                mixed2 = PS[:, 4 * g + 2, 0:4 * (D + 1)].rearrange("q (t d) -> q t d", d=D + 1)
                ve.wait_ge(sem("att2_mixed"), g + 1)
                v.reciprocal(r2[:, 4 * g:4 * g + 4], mixed2[:, :, D]).then_inc(sem("att2_recip"), 1)
            for g in range(2):
                ts = slice(4 * g, 4 * g + 4)
                mixed2 = PS[:, 4 * g + 2, 0:4 * (D + 1)].rearrange("q (t d) -> q t d", d=D + 1)
                ve.wait_ge(sem("att2_recip"), g + 1)
                v.tensor_tensor(tiles(o2)[:, ts], mixed2[:, :, 0:D], r2[:, ts].unsqueeze(2).to_broadcast([P, 4, D]),
                                ALU.mult).then_inc(sem("o2_ready"), 1)
            for g in range(2):
                ve.wait_ge(sem("h3_turned"), g + 1)
                ve.wait_ge(sem("o2_ready"), g + 1)
                v.tensor_tensor(half(sum2, g), PS[:, 4 * g + 3, 0:HC], half(o2, g), ALU.add).then_inc(sem("ln1_in"), 1)
            centre("ln1", sum2)
            normalise("ln1", centred, lambda g: tiles(h4)[:, 4 * g:4 * g + 4], EPS)

            for g in range(2):
                ve.wait_ge(sem("ln1_normed"), g + 1)
                v.tensor_copy(sums[:, g:g + 1], h4[:, g * HC:g * HC + 1]).then_inc(sem("rms1_centred"), 1)
            normalise("rms1", h4, lambda g: tiles(h4n)[:, 4 * g:4 * g + 4], EPS_RMS)
            cos = c("rope_cos").unsqueeze(1).to_broadcast([P, 4, N])
            sin = c("rope_sin").unsqueeze(1).to_broadcast([P, 4, N])
            for g in range(2):
                cols = slice(g * HC, (g + 1) * HC)
                for n in range(4):
                    ve.wait_ge(sem("qk3_mm"), 2 * g + n // 2 + 1)
                    t = v.tensor_tensor(rope[:, n, cols].rearrange("q (w n) -> q w n", n=N),
                                        PS[:, 1 + 4 * g + n // 2, (n % 2) * HC:(n % 2 + 1) * HC].rearrange(
                                            "q (w n) -> q w n", n=N),
                                        sin if n % 2 else cos, ALU.mult)
                    if n == 1:
                        t.then_inc(sem("rope_q"), 1)
                t.then_inc(sem("rope_k"), 1)
                ve.wait_ge(sem("rope_k"), g + 1)
                v.tensor_tensor(half(kr, g), rope[:, 2, cols], rope[:, 3, cols], ALU.add).then_inc(sem("kr_ready"), 1)
            for i in range(4):
                shift("att3", (0, 4, 1, 5)[i], i)
            divide("att3", 3, 0, FH, FHD)
            divide("att3", 7, 1, FH, FHD)
            for g in range(2):
                ve.wait_ge(sem("fo_mm"), g + 1)
                v.tensor_tensor(half(h5, g), PS[:, 4 * g, 0:HC], half(h4, g), ALU.add).then_inc(sem("rms2_centred"), 1)

            normalise("rms2", h5, lambda g: tiles(h5n)[:, 4 * g:4 * g + 4], EPS_RMS)
            for g in range(2):
                ts = slice(4 * g, 4 * g + 4)
                ve.wait_ge(sem("rms2_normed"), g + 1)
                v.tensor_copy(parts[:, ts, 0, :].bitcast(F32R), tiles(h5n)[:, ts]).then_inc(sem("high_ready"), 1)
            for g in range(2):
                ts = slice(4 * g, 4 * g + 4)
                ve.wait_ge(sem("high_ready"), g + 1)
                v.tensor_tensor(parts[:, ts, 1, :], tiles(h5n)[:, ts], parts[:, ts, 0, :], ALU.subtract)\
                    .then_inc(sem("parts_ready"), 1)
            ve.wait_ge(sem("parts_turned"), 1)
            v.tensor_copy(xf[:, 1, :], PS[:, 5, :]).then_inc(sem("xf_ready"), 1)

            def spread(name):
                return few[name][:, :].unsqueeze(2).to_broadcast([P, 8, NE])

            rank = c("rank").unsqueeze(1).to_broadcast([P, 8, NE])
            logits = PS[:, 2, 0:8 * NE].rearrange("q (t e) -> q t e", e=NE)
            routed = sem("router_step")
            ve.wait_ge(sem("logits_mm"), 1)
            v.reduce_max(few["top"][:, :], logits, AX).then_inc(routed, 1)
            ve.wait_ge(routed, 1)
            v.tensor_tensor(small["shift"][:, :, :], logits, spread("top"), ALU.subtract).then_inc(sem("logits_read"), 1)

            def top_of(dst, src):
                return lambda: v.reduce_max(few[dst][:, :], small[src][:, :, :], AX)

            def pair(dst, x0, x1, op):
                return lambda: v.tensor_tensor(small[dst][:, :, :], small[x0][:, :, :], x1, op)

            def few_pair(dst, x0, x1, op):
                return lambda: v.tensor_tensor(few[dst][:, :], few[x0][:, :], few[x1][:, :], op)

            router_steps = [
                lambda: v.reduce_sum(few["sum"][:, :], small["exp"][:, :, :], AX),
                lambda: v.reciprocal(few["rsum"][:, :], few["sum"][:, :]),
                pair("prob", "exp", spread("rsum"), ALU.mult),
                top_of("first", "prob"),
                pair("same1", "prob", spread("first"), ALU.is_equal),
                pair("rank1", "same1", rank, ALU.mult),
                top_of("first_rank", "rank1"),
                pair("one1", "rank1", spread("first_rank"), ALU.is_equal),
                lambda: v.scalar_tensor_tensor(out=small["prob2"][:, :, :], in0=small["one1"][:, :, :], scalar=-2.0,
                                               in1=small["prob"][:, :, :], op0=ALU.mult, op1=ALU.add),
                top_of("second", "prob2"),
                pair("same2", "prob2", spread("second"), ALU.is_equal),
                pair("rank2", "same2", rank, ALU.mult),
                top_of("second_rank", "rank2"),
                pair("one2", "rank2", spread("second_rank"), ALU.is_equal),
                pair("part1", "one1", spread("first"), ALU.mult),
                pair("part2", "one2", spread("second"), ALU.mult),
                pair("both", "part1", small["part2"][:, :, :], ALU.add),
                few_pair("total", "first", "second", ALU.add),
                lambda: v.tensor_scalar(few["total_eps"][:, :], few["total"][:, :], 1e-9, None, ALU.add),
                lambda: v.reciprocal(few["rtotal"][:, :], few["total_eps"][:, :]),
                pair("weights", "both", spread("rtotal"), ALU.mult),
            ]
            for n in range(2 * CH):
                s, ch = n // CH, n % CH
                ve.wait_ge(sem("gated"), n + 1)
                ve.wait_ge(sem("up_mm"), 2 * n + 2)
                v.tensor_tensor(hh[:, ch, s, :], PS[:, UP_BANKS[n % UPBUF] + 1, :], gate[:, n % UPBUF, :], ALU.mult)\
                    .then_inc(sem("hh_ready"), 1)
                if n < len(router_steps):
                    if n == 0:
                        ve.wait_ge(sem("router_exp"), 1)
                    else:
                        ve.wait_ge(routed, n + 1)
                    router_steps[n]().then_inc(routed, 1)

            ve.wait_ge(routed, len(router_steps) + 1)
            for s in range(2):
                for u in range(4):
                    n = 4 * s + u
                    ve.wait_ge(sem("down_mm"), n + 1)
                    v.tensor_tensor(weighted[:, n % 2], PS[:, DOWN_BANKS[n % 4], :].rearrange("q (e d) -> q e d", d=D),
                                    small["weights"][:, 2 * u + s, :].unsqueeze(2).to_broadcast([P, NE, D]), ALU.mult)\
                        .then_inc(sem("tile_weighted"), 1)
                    ve.wait_ge(sem("tile_weighted"), n + 1)
                    v.reduce_sum(mixed[:, u, s, :], weighted[:, n % 2].rearrange("q e d -> q d e"), AX)\
                        .then_inc(sem("tile_mixed"), 1)
                ts = slice(4 * s, 4 * s + 4)
                h45u = h45[:, :].rearrange("q (u s d) -> q u s d", s=2, d=D)
                ve.wait_ge(sem("tile_mixed"), 4 * s + 4)
                ve.wait_ge(sem("h45_ready"), 1)
                v.tensor_tensor(h6[:, :, s, :], mixed[:, :, s, :], h45u[:, :, s, :], ALU.add).then_inc(sem("h6_ready"), 1)
                ve.wait_ge(sem("h6_ready"), s + 1)
                v.reduce_sum(sums[:, ts], h6[:, :, s, :], AX).then_inc(sem("lnf_sum"), 1)
                ve.wait_ge(sem("lnf_sum"), s + 1)
                v.scalar_tensor_tensor(out=tiles(centred)[:, ts], in0=sums[:, ts].unsqueeze(2).to_broadcast([P, 4, D]),
                                       scalar=-1.0 / D, in1=h6[:, :, s, :], op0=ALU.mult, op1=ALU.add)\
                    .then_inc(sem("lnf_centred"), 1)
                ve.wait_ge(sem("lnf_squared"), s + 1)
                v.reduce_sum(sq_sums[:, ts], tiles(squares)[:, ts], AX).then_inc(sem("lnf_sq_sum"), 1)
                ve.wait_ge(sem("lnf_sq_sum"), s + 1)
                v.tensor_scalar(var[:, ts], sq_sums[:, ts], 1.0 / D, EPS, ALU.mult, ALU.add).then_inc(sem("lnf_var"), 1)
                ve.wait_ge(sem("lnf_rstd"), s + 1)
                v.tensor_tensor(out_sb[:, s], tiles(centred)[:, ts], rstd[:, ts].unsqueeze(2).to_broadcast([P, 4, D]),
                                ALU.mult).then_inc(sem("out_normed"), 1)


def layouts(np, t):
    def w(name):
        return np.asarray(t[name])

    def both(m):
        return np.concatenate([m, m], axis=0)

    def diag(m):
        n = m.shape[1]
        z = np.zeros((P, 2 * n), np.float32)
        z[:D, :n] = m
        z[D:, n:] = m
        return z

    def col(vec):
        return both(vec.reshape(D, 1))

    def row(vec):
        return np.broadcast_to(vec.reshape(1, -1), (P, vec.size))

    def pack(names, parts):
        assert {k: v.shape[1] for k, v in parts.items()} == names, \
            {k: v.shape for k, v in parts.items() if v.shape[1] != names.get(k)}
        return np.ascontiguousarray(np.concatenate([parts[k] for k in names], axis=1))

    pos = np.arange(N, dtype=np.float32)[:, None]
    i = np.arange(0, D, 2, dtype=np.float32)
    ang = pos * np.exp(-np.log(np.float32(10000.0)) * i / np.float32(D)).astype(np.float32)
    pe = np.stack([np.sin(ang), np.cos(ang)], axis=-1).reshape(N, D).astype(np.float32)
    conv = w("L0_tok_conv_w").reshape(D, KCH, P).transpose(2, 1, 0).reshape(P, KCH * D)
    pack_a = pack(PACK_A, dict(
        ident=np.eye(P, dtype=np.float32), conv=conv, conv_b=row(w("L0_tok_conv_b")), pos=both(pe.T),
        ln_w=col(w("L0_tok_ln_w")), ln_b=col(w("L0_tok_ln_b"))))

    qkv, qkv_b = w("L0_tok_qkv_w"), w("L0_tok_qkv_b")
    feature = np.arange(P)[:, None] % D
    pack_b = pack(PACK_B, dict(
        ff1=both(w("L0_tok_ff_w1").T), ff1_b=w("L0_tok_ff_b1").reshape(2, P).T,
        ff2=w("L0_tok_ff_w2").T.reshape(2, P, D).transpose(1, 0, 2).reshape(P, 2 * D), ff2_b=col(w("L0_tok_ff_b2")),
        wq=diag(qkv[0:D].T), wk=diag(qkv[D:2 * D].T), wv=diag(qkv[2 * D:].T), proj=diag(w("L0_tok_proj_w").T),
        bq=col(qkv_b[0:D]), bk=col(qkv_b[D:2 * D]), bv=col(qkv_b[2 * D:]), bp=col(w("L0_tok_proj_b")),
        head_mask=(feature // HD == np.arange(HEADS)[None, :]).astype(np.float32)))

    n = np.arange(N, dtype=np.float32)
    dist = np.abs(n[:, None] - n[None, :])
    two_pi = np.float32(2.0 * np.pi)
    cosines = np.concatenate([np.cos(two_pi * dist / np.float32(period)) for period in (24.0, 720.0)], axis=1)
    inv_freq = 1.0 / 10000.0 ** (np.arange(0, FHD, 2, dtype=np.float32) / FHD)
    freqs = np.outer(n, inv_freq)
    emb = np.concatenate([freqs, freqs], axis=-1)
    cos, sin = np.cos(emb).T.astype(np.float32), np.sin(emb).T.astype(np.float32)
    sign = np.where(np.arange(FHD) < FHD // 2, -1.0, 1.0)[:, None].astype(np.float32)
    turned = (np.arange(FHD) + FHD // 2) % FHD
    wq = w("L0_ffn_wq").reshape(FH, FHD, D)
    wk = w("L0_ffn_wk").reshape(FKV, FHD, D)[[h // (FH // FKV) for h in range(FH)]]
    causal = np.where(n[:, None] >= n[None, :], 0.0, -1e30).astype(np.float32)
    pack_c = pack(PACK_C, dict(
        aq=diag(w("L0_attn_Wq").T), ak=diag(w("L0_attn_Wk").T), av=diag(w("L0_attn_Wv").T),
        abq=col(w("L0_attn_bq")), abk=col(w("L0_attn_bk")), abv=row(w("L0_attn_bv")), beta=row(w("L0_attn_beta")),
        cosines=both(cosines.astype(np.float32)),
        fq=diag(wq.reshape(D, D).T), fq_turned=diag(wq[:, turned].reshape(D, D).T),
        fk=diag(wk.reshape(D, D).T), fk_turned=diag(wk[:, turned].reshape(D, D).T),
        fv=diag(w("L0_ffn_wv").T), fo=diag(w("L0_ffn_wo").T), router=both(w("L0_ffn_router_w").T),
        rope_cos=both(np.tile(cos, (FH, 1))), rope_sin=both(np.tile(sign * sin, (FH, 1))),
        causal=both(np.tile(causal, (1, FH))),
        fhead_mask=(feature // FHD == np.arange(FH)[None, :]).astype(np.float32),
        rank=row(np.arange(NE, 0, -1).astype(np.float32)), ln1=col(w("L0_ffn_ln1_w")), ln2=col(w("L0_ffn_ln2_w"))))

    up = np.zeros((2, CH * P, D), np.float32)
    down = np.zeros((P, DOWN_AT[CH]), np.float32)
    w2 = w("L0_ffn_w2").transpose(0, 2, 1)
    for v, name in enumerate(("L0_ffn_w1", "L0_ffn_w3")):
        up[v, :NE * HID] = w(name).reshape(NE * HID, D)
    up = up.reshape(2, CH, P, D).transpose(1, 0, 2, 3)
    for ch in range(CH):
        for n, ex in enumerate(experts_of(ch)):
            r0, r1 = max(ch * P, ex * HID), min((ch + 1) * P, (ex + 1) * HID)
            down[r0 - ch * P:r1 - ch * P, DOWN_AT[ch] + n * D:DOWN_AT[ch] + (n + 1) * D] = w2[ex, r0 - ex * HID:r1 - ex * HID]
    pack_d = np.ascontiguousarray(both(up.reshape(2 * CH * P, D).T))
    return dict(x=np.ascontiguousarray(w("x")), pack_a=pack_a, pack_b=pack_b, pack_c=pack_c, pack_d=pack_d, pack_e=down)


def kernel(**inputs):
    import numpy as np
    import concourse.bacc as bacc
    from concourse.bass_utils import run_bass_kernel_spmd

    nc = bacc.Bacc("TRN2", target_bir_lowering=False, num_devices=1)
    arrays, args = {}, []
    for name, arr in layouts(np, inputs).items():
        arrays[name + "_dram"] = arr
        args.append(nc.dram_tensor(name + "_dram", arr.shape, mybir.dt.from_np(arr.dtype), kind="ExternalInput").ap())
    args.append(nc.dram_tensor("out_dram", (B, N, D), F32, kind="ExternalOutput").ap())
    build(nc, *args)
    r = run_bass_kernel_spmd(nc, [arrays], core_ids=[0])
    return r.results[0]["out_dram"]
```

```python
from contextlib import ExitStack

import concourse.bass as bass
from concourse import mybir

ALU = mybir.AluOpType
ACT = mybir.ActivationFunctionType
AX = mybir.AxisListType.X
F32 = mybir.dt.float32
F32R = mybir.dt.float32r
BF16 = mybir.dt.bfloat16

P = 128
B, C, IMG, PATCH = 16, 3, 128, 16
GRID = IMG // PATCH
N = GRID * GRID
D = 64
HALF = 64
COLS = B * N * D // P
HC = COLS // 2
KCH = C * PATCH * PATCH // P
W8 = B // 2
HEADS, HD = 8, 8
FF = 256
FH, FHD, FKV = 4, 16, 2
NE, HID = 8, 170
CH = -(-NE * HID // P)
UPBUF = 3


def experts_of(chunk):
    return range(chunk * P // HID, min((chunk * P + P - 1) // HID, NE - 1) + 1)


DOWN_AT = [D * sum(len(experts_of(ch)) for ch in range(n)) for n in range(CH + 1)]
EPS = 1e-5
EPS_RMS = 1e-6

PACK_A = dict(ident=P, conv=KCH * D, conv_b=D, ones=P, pos=N, ln_w=1, ln_b=1)
PACK_B = dict(ff1=FF, ff1_b=2, ff2=2 * D, ff2_b=1, wq=P, wk=P, wv=P, proj=P, bq=1, bk=1, bv=1, bp=1,
              head_mask=HEADS // 2)
PACK_C = dict(aq=P, ak=P, av=P, abq=1, abk=1, abv=D, beta=2, cosines=2 * N,
              fq=P, fq_turned=P, fk=P, fk_turned=P, fv=2 * FKV * FHD, fo=P, router=NE, rope_cos=N, rope_sin=N,
              causal=2 * N, fhead_mask=FH // 2, rank=NE, ln1=1, ln2=1, centring=P)
PACK_D = dict(up=2 * CH * P)
PACK_E = dict(down=DOWN_AT[CH])


def width(pack):
    return sum(pack.values())


def columns(pack, name):
    at = 0
    for key, n in pack.items():
        if key == name:
            return slice(at, at + n)
        at += n
    raise KeyError(name)


def build(nc, x, pack_a, pack_b, pack_c, pack_d, pack_e, out):
    with ExitStack() as ctx:
        def sb(name, shape, dt=F32):
            return ctx.enter_context(nc.sbuf_tensor(name, shape, dt))

        made = {}

        def sem(name):
            if name not in made:
                made[name] = ctx.enter_context(nc.semaphore(name))
            return made[name]

        idle_bf = sb("idle_bf", [P, 512], BF16)
        PS = ctx.enter_context(nc.psum_tensor("PS", [P, 8, 512], F32))

        A = sb("pack_a_sb", [P, width(PACK_A)])
        Bp = sb("pack_b_sb", [P, width(PACK_B)])
        Cp = sb("pack_c_sb", [P, width(PACK_C)])
        up_w = sb("up_w", [P, 2 * CH * P])
        up_hi = sb("up_hi", [P, 2 * CH * P], F32R)
        up_lo = sb("up_lo", [P, 2 * CH * P], F32R)
        down_w = sb("down_w", [P, DOWN_AT[CH]])

        def a(name):
            return A[:, columns(PACK_A, name)]

        def b(name):
            return Bp[:, columns(PACK_B, name)]

        def c(name):
            return Cp[:, columns(PACK_C, name)]

        shared_x = sb("shared_x", [P, KCH * 1024])
        shared_p = sb("shared_p", [P, 4 * COLS])
        shared_f = sb("shared_f", [P, 4 * COLS])
        shared_h = sb("shared_h", [P, CH * 2 * COLS])
        x_sb = shared_x[:, :].rearrange("q (k c) -> q k c", k=KCH)
        patches = shared_p[:, :].rearrange("q (k c) -> q k c", k=2)
        x_patches = shared_f[:, :].rearrange("q (k c) -> q k c", k=2)
        means = sb("means", [P, DOWN_AT[CH] // D])
        squares = sb("squares", [P, COLS])
        normed = sb("normed", [P, COLS])
        sq_sums = sb("sq_sums", [P, 8])
        var = sb("var", [P, 8])
        rstd = sb("rstd", [P, 8])
        var_rms = sb("var_rms", [P, 8])
        rstd_rms = sb("rstd_rms", [P, 8])
        spare = sb("spare", [P, 1])
        minus_half = sb("minus_half", [P, 8])
        pos_b = sb("pos_b", [P, N])
        proj_bias = sb("proj_bias", [P, 1])
        h0 = sb("h0", [P, COLS])
        hidden = shared_f[:, :].rearrange("q (m s c) -> q m s c", m=2, s=2)
        f1 = sb("f1", [P, COLS])
        h2 = sb("h2", [P, COLS])
        h3 = sb("h3", [P, COLS])
        qf = sb("qf", [P, COLS])
        kf = sb("kf", [P, COLS])
        k_heads = shared_h[:, 0:W8 * 4 * N].rearrange("q (w h n) -> q w h n", w=W8, h=4)
        vo = sb("vo", [P, 2, W8, 4, 2, HD + 1])
        r1 = sb("r1", [P, W8, HEADS])
        top = sb("top", [P, 2, HEADS])
        shifted = sb("shifted", [P, 2, COLS])
        probs = sb("probs", [P, 2, COLS])
        attended = sb("attended", [P, COLS])
        bias = sb("bias", [P, N])
        q2 = qf
        k2 = sb("k2", [P, COLS])
        v2 = sb("v2", [P, W8, D + 1])
        s2 = sb("s2", [P, COLS])
        on = s2[:, :].rearrange("q (w d) -> q w d", d=D)
        s2_top = sb("s2_top", [P, W8])
        s2_shift = sb("s2_shift", [P, COLS])
        p2 = sb("p2", [P, 4, P])
        r2 = sb("r2", [P, W8])
        o2 = attended
        sum2 = h2
        h4 = sb("h4", [P, COLS])
        h4n = kf
        h4f = h0
        rope = shared_f[:, :].rearrange("q (k c) -> q k c", k=4)
        kr = sb("kr", [P, COLS])
        q3 = qf
        vo3 = sb("vo3", [P, 2, W8, FKV, 2, FHD + 1])
        k3_heads = shared_x[:, 0:W8 * 2 * N].rearrange("q (w h n) -> q w h n", w=W8, h=2)
        causal_bf = sb("causal_bf", [P, 2 * N], BF16)
        ident_bf = sb("ident_bf", [P, P], BF16)
        attended3 = attended
        h5 = f1
        h45 = attended
        h5n = normed
        parts = sb("parts", [P, W8, 2, N])
        xf = sb("xf", [P, 2, COLS], F32R)
        router_s = sb("router_s", [P, NE])
        router_hi = sb("router_hi", [P, NE], F32R)
        router_lo = sb("router_lo", [P, NE], F32R)
        gate = shared_f[:, 0:UPBUF * COLS].rearrange("q (k c) -> q k c", k=UPBUF)
        hh = shared_h[:, 0:CH * 2 * COLS].rearrange("q (c s t) -> q c s t", c=CH, s=2)
        small = {k: sb("r_" + k, [P, 8, NE]) for k in
                 ("shift", "exp", "prob", "same1", "rank1", "one1", "prob2", "same2", "rank2", "one2",
                  "part1", "part2", "both", "weights")}
        few = {k: sb("r_" + k, [P, 8]) for k in
               ("top", "sum", "rsum", "first", "first_rank", "second", "second_rank", "total", "total_eps", "rtotal")}
        weighted = shared_p[:, 2 * COLS:].rearrange("q (k e d) -> q k e d", k=2, e=NE)
        mixed = s2[:, :].rearrange("q (u s d) -> q u s d", u=4, s=2)
        h6 = s2_shift[:, :].rearrange("q (u s d) -> q u s d", u=4, s=2)
        out_sb = k2[:, :].rearrange("q (s u d) -> q s u d", s=2, u=4)

        def tiles(t):
            return t[:, :].rearrange("q (t d) -> q t d", d=D)

        def half(t, g):
            return t[:, g * HC:(g + 1) * HC]

        def vo_part(h2, p, g):
            return vo[HALF * h2:HALF * h2 + HALF, p, 4 * g:4 * g + 4, :, h2, 0:HD]

        def vo3_part(h2, p, g):
            return vo3[HALF * h2:HALF * h2 + HALF, p, 4 * g:4 * g + 4, :, h2, 0:FHD]

        SCORE_BANKS1 = (6, 2)
        UP_BANKS = (3, 6, 0)
        DOWN_BANKS = (5, 2, 3, 4)

        block = ctx.enter_context(nc.Block())

        @block.sync
        def _(sp):
            def load_x(k):
                ch, ph = k // 2, k % 2
                rows = x[:, ch].rearrange("b (i r) w -> b i (r w)", i=GRID)[:, :, ph * 1024:(ph + 1) * 1024]
                sp.dma_start(x_sb[:, k, :], rows).then_inc(sem(f"x_loaded{k}"), 16)

            sp.dma_start(A[:, :], pack_a).then_inc(sem("pack_a_loaded"), 16)
            for k in range(KCH):
                load_x(k)
            sp.dma_start(Bp[:, :], pack_b).then_inc(sem("pack_b_loaded"), 16)
            sp.dma_start(up_w[:, :], pack_d).then_inc(sem("up_w_loaded"), 16)
            sp.dma_start(Cp[:, :], pack_c).then_inc(sem("pack_c_loaded"), 16)
            sp.dma_start(down_w[:, :], pack_e).then_inc(sem("down_w_loaded"), 16)
            for s in range(2):
                sp.wait_ge(sem("out_normed"), s + 1)
                dst = out.rearrange("(s u p) n d -> s u (p n) d", s=2, p=2)[s].rearrange("u q d -> q u d")
                sp.dma_start(dst, out_sb[:, s]).then_inc(sem("stored"), 16)
            sp.wait_ge(sem("stored"), 32)

        @block.tensor
        def _(pe):
            mm, tp = nc.tensor.matmul, nc.tensor.transpose
            ident = a("ident")

            def stay_awake(n, bank):
                for _ in range(n):
                    mm(PS[:, bank, :], idle_bf[:, 0:P], idle_bf[:, :], start=True, stop=True)

            def conv_transposes(k):
                pe.wait_ge(sem("x_grouped"), k + 1)
                if k >= 2:
                    pe.wait_ge(sem("patches_copied_act"), k - 1)
                    pe.wait_ge(sem("patches_copied_dve"), k - 1)
                for j in range(GRID):
                    t = tp(PS[:, 2 * (k % 2) + j // 4, (j % 4) * P:(j % 4 + 1) * P], x_patches[:, k % 2, j * P:(j + 1) * P], ident)
                    if j % 4 == 3:
                        t.then_inc(sem("patches_turned"), 1)

            def conv_products(k):
                pe.wait_ge(sem("patches_copied_act"), k + 1)
                pe.wait_ge(sem("patches_copied_dve"), k + 1)
                w = a("conv")[:, k * D:(k + 1) * D]
                if k == 0:
                    pe.wait_ge(sem("conv_centred"), 1)
                    mm(PS[:, 4, :].rearrange("q (j d) -> q j d", d=D), a("ones")[0:1, :],
                       a("conv_b")[0:1].unsqueeze(1).to_broadcast([1, GRID, D]), start=True, stop=False, skip_group_check=True)
                for j in range(GRID):
                    m = mm(PS[:, 4, j * D:(j + 1) * D], patches[:, k % 2, j * P:(j + 1) * P], w,
                           start=False, stop=(k == KCH - 1), skip_group_check=True)
                m.then_inc(sem("conv_summed"), 1)

            def ffn(name, src, u_banks):
                for g in range(2):
                    pe.wait_ge(sem(name + "_in"), g + 1)
                    for m in range(2):
                        for s in range(2):
                            r = slice(HALF * s, HALF * s + HALF)
                            t = mm(PS[:, u_banks[g] + s, m * HC:(m + 1) * HC], b("ff1")[r, m * P:(m + 1) * P],
                                   src[r, g * HC:(g + 1) * HC], start=True, stop=True)
                    t.then_inc(sem(name + "_up"), 1)
                for g in range(2):
                    pe.wait_ge(sem(name + "_gelu"), 2 * g + 2)
                    for s in range(2):
                        r = slice(HALF * s, HALF * s + HALF)
                        for m in range(2):
                            t = mm(PS[r, 6 + g, 0:HC], b("ff2")[:, m * D:(m + 1) * D],
                                   hidden[:, m, s, g * HC:(g + 1) * HC], start=(m == 0), stop=(m == 1))
                    t.then_inc(sem(name + "_down"), 1)

            def values(src, w, wide, bank, g):
                for u in (2 * g, 2 * g + 1):
                    at = (u % 2) * 2 * wide
                    t = mm(PS[:, bank, at:at + 2 * wide], src[:, u * P:(u + 1) * P], w, start=True, stop=True)
                return t

            pe.wait_ge(sem("idle_made"), 1)
            stay_awake(10, 7)
            pe.wait_ge(sem("pack_a_loaded"), 16)
            for k in range(KCH):
                conv_transposes(k)
                if k:
                    conv_products(k - 1)
            conv_products(KCH - 1)

            stay_awake(12, 7)
            for g in range(2):
                pe.wait_ge(sem("ln0_normed"), g + 1)
                for j in range(4 * g, 4 * g + 4):
                    for s in range(2):
                        r = slice(HALF * s, HALF * s + HALF)
                        t = mm(PS[r, 5, j * D:(j + 1) * D], normed[r, j * D:(j + 1) * D], ident[r, r],
                               start=True, stop=True)
            t.then_inc(sem("emb_turned"), 1)
            pe.wait_ge(sem("pack_b_loaded"), 16)
            mm(PS[:, 4, 0:1], b("proj"), b("bv"), start=True, stop=True).then_inc(sem("proj_bv"), 1)

            stay_awake(3, 7)
            ffn("ffn1", h0, (0, 2))

            for g in range(2):
                pe.wait_ge(sem("f1_ready"), g + 1)
                cols = slice(g * HC, (g + 1) * HC)
                mm(PS[:, 2 * g, 0:HC], b("wq"), f1[:, cols], start=True, stop=True).then_inc(sem("q1_mm"), 1)
                mm(PS[:, 2 * g + 1, 0:HC], b("wk"), f1[:, cols], start=True, stop=True).then_inc(sem("k1_mm"), 1)
                if g == 0:
                    pe.wait_ge(sem("proj_bias_made"), 1)
                values(f1, b("wv"), D, 4 + g, g).then_inc(sem("v1_mm"), 1)

            def scores1(w):
                if w % 4 == 0:
                    pe.wait_ge(sem("q1_act"), w // 4 + 1)
                    pe.wait_ge(sem("k1_act"), w // 4 + 1)
                    pe.wait_ge(sem("k1_dve"), w // 4 + 1)
                if w == 1:
                    pe.wait_ge(sem("q1_act"), 2)
                    pe.wait_ge(sem("kf_ready"), 2)
                if w >= 2:
                    pe.wait_ge(sem("att1_shifted"), w - 1)
                stay_awake(1, SCORE_BANKS1[w % 2])
                for s in range(2):
                    for hg in range(2):
                        rows = slice(HALF * s + 32 * hg, HALF * s + 32 * hg + 32)
                        t = mm(PS[HALF * s:HALF * s + HALF, SCORE_BANKS1[w % 2] + hg, 0:HC], qf[rows, w * N:(w + 1) * N],
                               k_heads[rows, w].rearrange("q h n -> q (h n)"), start=True, stop=True)
                t.then_inc(sem("att1_scores"), 1)

            def turn1(w):
                pe.wait_ge(sem("att1_shifted"), w + 1)
                if w >= 2:
                    pe.wait_ge(sem("att1_probs"), w - 1)
                for ch in range(4):
                    t = tp(PS[:, w % 2, ch * P:(ch + 1) * P], shifted[:, w % 2, ch * P:(ch + 1) * P], ident)
                t.then_inc(sem("att1_turned"), 1)

            def mix1(w):
                if w % 4 == 0:
                    pe.wait_ge(sem("v1_act"), w // 4 + 1)
                    pe.wait_ge(sem("v1_dve"), w // 4 + 1)
                pe.wait_ge(sem("att1_probs"), w + 1)
                wide = 2 * (HD + 1)
                for s in range(2):
                    r = slice(HALF * s, HALF * s + HALF)
                    for ch in range(4):
                        at = ((w % 4) * 4 + ch) * wide
                        t = mm(PS[r, 4 + w // 4, at:at + wide], probs[:, w % 2, ch * P + s * HALF:ch * P + (s + 1) * HALF],
                               vo[:, w % 2, (w // 2) * 2 + s, ch].rearrange("q e d -> q (e d)"), start=True, stop=True)
                t.then_inc(sem("att1_mixed"), 1)

            pe.wait_ge(sem("vo_made"), 1)
            for w in range(W8 + 2):
                if w < W8:
                    scores1(w)
                if 1 <= w <= W8:
                    turn1(w - 1)
                if w >= W8:
                    stay_awake(2, 6)
                if w >= 2:
                    mix1(w - 2)

            def mixed_to_features(name, bank, g):
                pe.wait_ge(sem(name + "_divided"), g + 1)
                for w in range(4 * g, 4 * g + 4):
                    for s in range(2):
                        r = slice(HALF * s, HALF * s + HALF)
                        t = mm(PS[r, bank, (w % 4) * N:(w % 4 + 1) * N], on[r, w, :], ident[r, r], start=True, stop=True)
                t.then_inc(sem(name + "_back"), 1)

            def project1(g):
                pe.wait_ge(sem("att1_ready"), g + 1)
                mm(PS[:, 2 + g, 0:HC], b("proj"), half(attended, g),
                   start=True, stop=True).then_inc(sem("proj_mm"), 1)

            for g in range(2):
                stay_awake(1 + g, 6)
                mixed_to_features("att1", g, g)
            for g in range(2):
                stay_awake(1, 6)
                project1(g)
            stay_awake(1, 6)
            ffn("ffn2", h2, (0, 4))

            pe.wait_ge(sem("pack_c_loaded"), 16)
            for g in range(2):
                pe.wait_ge(sem("h3_ready"), g + 1)
                cols = slice(g * HC, (g + 1) * HC)
                mm(PS[:, 4 * g, 0:HC], c("aq"), h3[:, cols], start=True, stop=True).then_inc(sem("q2_mm"), 1)
                mm(PS[:, 4 * g + 1, 0:HC], c("ak"), h3[:, cols], start=True, stop=True).then_inc(sem("k2_mm"), 1)
                pe.wait_ge(sem("v2_centred"), 2)
                values(h3, c("av"), D, 4 * g + 2, g).then_inc(sem("v2_mm"), 1)
                for u in (2 * g, 2 * g + 1):
                    t = mm(PS[:, 4 * g + 3, (u % 2) * P:(u % 2 + 1) * P], h3[:, u * P:(u + 1) * P], c("centring"),
                           start=True, stop=True)
                t.then_inc(sem("h3_turned"), 1)
            for g in range(2):
                pe.wait_ge(sem("q2_act"), g + 1)
                pe.wait_ge(sem("k2_dve"), g + 1)
                for w in range(4 * g, 4 * g + 4):
                    for s in range(2):
                        r = slice(HALF * s, HALF * s + HALF)
                        t = mm(PS[r, 4 * g, (w % 4) * N:(w % 4 + 1) * N], q2[r, w * N:(w + 1) * N],
                               k2[r, w * N:(w + 1) * N], start=True, stop=True)
                t.then_inc(sem("att2_scores"), 1)
            stay_awake(6, 1)
            for g in range(2):
                pe.wait_ge(sem("att2_shifted"), g + 1)
                for u in (2 * g, 2 * g + 1):
                    t = tp(PS[:, 4 * g + 1, (u % 2) * P:(u % 2 + 1) * P], s2_shift[:, u * P:(u + 1) * P], ident)
                t.then_inc(sem("att2_turned"), 1)
            for g in range(2):
                pe.wait_ge(sem("v2_ready"), g + 1)
                pe.wait_ge(sem("att2_probs"), g + 1)
                for u in (2 * g, 2 * g + 1):
                    for s in range(2):
                        for p in range(2):
                            r = slice(HALF * p, HALF * p + HALF)
                            at = ((u % 2) * 2 + s) * (D + 1)
                            t = mm(PS[r, 4 * g + 2, at:at + D + 1], p2[r, u, s * HALF:(s + 1) * HALF],
                                   v2[r, 2 * u + s, :], start=True, stop=True)
                t.then_inc(sem("att2_mixed"), 1)

            stay_awake(17, 1)
            for g in range(2):
                pe.wait_ge(sem("h4n_ready"), g + 1)
                for u in (2 * g, 2 * g + 1):
                    t = tp(PS[:, 4 * g, (u % 2) * P:(u % 2 + 1) * P], h4n[:, u * P:(u + 1) * P], ident)
                t.then_inc(sem("h4_turned"), 1)
            for g in range(2):
                pe.wait_ge(sem("h4f_ready"), g + 1)
                cols = slice(g * HC, (g + 1) * HC)
                for n, name in enumerate(("fq", "fq_turned", "fk", "fk_turned")):
                    t = mm(PS[:, 1 + 4 * g + n // 2, (n % 2) * HC:(n % 2 + 1) * HC], c(name), h4f[:, cols],
                           start=True, stop=True)
                    if n % 2:
                        t.then_inc(sem("qk3_mm"), 1)
                values(h4f, c("fv"), FKV * FHD, 3 + 4 * g, g).then_inc(sem("v3_mm"), 1)

            def scores3(g):
                stay_awake(2, 4 * g)
                pe.wait_ge(sem("q3_ready"), g + 1)
                pe.wait_ge(sem("k3_ready"), g + 1)
                for w in range(4 * g, 4 * g + 4):
                    for s in range(2):
                        r = slice(HALF * s, HALF * s + HALF)
                        for hg in range(2):
                            rows = slice(HALF * s + 32 * hg, HALF * s + 32 * hg + 32)
                            at = PS[r, 4 * g + hg, (w % 4) * P:(w % 4 + 1) * P]
                            mm(at, ident_bf[:, r], causal_bf[:, :], start=True, stop=False)
                            t = mm(at, q3[rows, w * N:(w + 1) * N], k3_heads[rows, w].rearrange("q h n -> q (h n)"),
                                   start=False, stop=True)
                t.then_inc(sem("att3_scores"), 1)

            def turn3(i):
                if i >= 2:
                    pe.wait_ge(sem("att3_probs"), i - 1)
                    stay_awake(1, 2 + 4 * (i % 2))
                pe.wait_ge(sem("att3_shifted"), i + 1)
                for n in range(4):
                    t = tp(PS[:, 2 + 4 * (i % 2), n * P:(n + 1) * P], shifted[:, i % 2, n * P:(n + 1) * P], ident)
                t.then_inc(sem("att3_turned"), 1)

            def mix3(i):
                g, ch = i // 2, i % 2
                if ch == 0:
                    pe.wait_ge(sem("v3_ready"), g + 1)
                pe.wait_ge(sem("att3_probs"), i + 1)
                wide = 2 * (FHD + 1)
                for w in range(4 * g, 4 * g + 4):
                    for s in range(2):
                        r = slice(HALF * s, HALF * s + HALF)
                        at = ((w % 4) * FKV + ch) * wide
                        t = mm(PS[r, 3 + 4 * g, at:at + wide],
                               probs[:, i % 2, (w % 4) * P + s * HALF:(w % 4) * P + (s + 1) * HALF],
                               vo3[:, w % 2, (w // 2) * 2 + s, ch].rearrange("q e d -> q (e d)"), start=True, stop=True)
                t.then_inc(sem("att3_mixed"), 1)

            pe.wait_ge(sem("causal_made"), 1)
            pe.wait_ge(sem("ident_bf_made"), 1)
            for g in range(2):
                scores3(g)
            for i in range(5):
                if i < 4:
                    turn3(i)
                if i >= 1:
                    mix3(i - 1)
            for g in range(2):
                stay_awake(1, 0)
                mixed_to_features("att3", 2 + 4 * g, g)
            for g in range(2):
                pe.wait_ge(sem("att3_ready"), g + 1)
                values(attended3, c("fo"), D, 4 * g, g).then_inc(sem("fo_mm"), 1)

            stay_awake(20, 3)
            for g in range(2):
                pe.wait_ge(sem("parts_ready"), g + 1)
                for s in range(2):
                    for u in (2 * g, 2 * g + 1):
                        t = tp(PS[:, 1 + 4 * s, u * P:(u + 1) * P], parts[:, 2 * u + s].rearrange("q l d -> q (l d)"), ident)
            t.then_inc(sem("parts_turned"), 1)
            stay_awake(4, 3)
            pe.wait_ge(sem("router_made"), 1)
            pe.wait_ge(sem("xf_ready"), 2)
            for t8 in range(8):
                u, s = t8 // 2, t8 % 2
                for n, w in enumerate((router_hi, router_lo)):
                    t = mm(PS[:, 2, t8 * NE:(t8 + 1) * NE], xf[:, s, u * P:(u + 1) * P], w[:, :],
                           start=(n == 0), stop=(n == 1))
            t.then_inc(sem("logits_mm"), 1)

            pe.wait_ge(sem("up_split"), 1)
            for s in range(2):
                for ch in range(CH):
                    n = s * CH + ch
                    if n >= UPBUF:
                        pe.wait_ge(sem("hh_ready"), n - UPBUF + 1)
                    for v in range(2):
                        at = (2 * ch + v) * P
                        mm(PS[:, UP_BANKS[n % UPBUF] + v, :], up_hi[:, at:at + P], xf[:, s, :], start=True, stop=False)
                        t = mm(PS[:, UP_BANKS[n % UPBUF] + v, :], up_lo[:, at:at + P], xf[:, s, :], start=False, stop=True)
                        t.then_inc(sem("up_mm"), 1)
            pe.wait_ge(sem("down_centred"), 1)
            for n in range(8):
                s, u = n // 4, n % 4
                if n % 4 == 0:
                    pe.wait_ge(sem("hh_ready"), CH * (s + 1))
                if n == 1:
                    pe.wait_ge(sem("logits_read"), 1)
                if n == 2:
                    pe.wait_ge(sem("hh_ready"), 2 * CH)
                if n >= 4:
                    pe.wait_ge(sem("tile_weighted"), n - 3)
                bank = DOWN_BANKS[n % 4]
                tok = slice(u * P, (u + 1) * P)
                for ch in range(CH):
                    ex = experts_of(ch)
                    t = mm(PS[:, bank, ex[0] * D:(ex[-1] + 1) * D], hh[:, ch, s, tok],
                           down_w[:, DOWN_AT[ch]:DOWN_AT[ch + 1]],
                           start=(ch == 0), stop=(ch == CH - 1), skip_group_check=True)
                t.then_inc(sem("down_mm"), 1)

        @block.scalar
        def _(act):
            f = nc.scalar.activation

            for k in range(KCH):
                act.wait_ge(sem("patches_turned"), 2 * k + 1)
                if k >= 2:
                    act.wait_ge(sem("conv_summed"), k - 1)
                f(patches[:, k % 2, 0:512], PS[:, 2 * (k % 2), :], ACT.Copy).then_inc(sem("patches_copied_act"), 1)

            def squares_of(name, ready, count, src):
                for g in range(2):
                    act.wait_ge(sem(ready), count[g])
                    f(half(squares, g), half(src, g), ACT.Square).then_inc(sem(name + "_squared"), 1)

            def gelus(name, u_banks):
                for g in range(2):
                    act.wait_ge(sem(name + "_up"), g + 1)
                    for m in range(2):
                        f(hidden[:, m, :, g * HC:(g + 1) * HC],
                          PS[:, u_banks[g]:u_banks[g] + 2, m * HC:(m + 1) * HC],
                          ACT.Gelu_apprx_tanh, bias=b("ff1_b")[:, m:m + 1]).then_inc(sem(name + "_gelu"), 1)

            squares_of("ln0", "conv_summed", (KCH, KCH), PS[:, 4, :])
            act.wait_ge(sem("pack_b_loaded"), 16)
            gelus("ffn1", (0, 2))
            for g in range(2):
                act.wait_ge(sem("ffn1_down"), g + 1)
                f(half(f1, g), PS[:, 6 + g, 0:HC], ACT.Identity, bias=b("ff2_b")).then_inc(sem("f1_ready"), 1)

            for g in range(2):
                ws = slice(4 * g, 4 * g + 4)
                cols = slice(g * HC, (g + 1) * HC)
                act.wait_ge(sem("q1_mm"), g + 1)
                f(half(qf, g), PS[:, 2 * g, 0:HC], ACT.Identity, bias=b("bq")).then_inc(sem("q1_act"), 1)
                act.wait_ge(sem("kf_ready"), g + 1)
                for h in (2, 3):
                    t = f(k_heads[:, ws, h, :], half(kf, g).rearrange("q (w n) -> q w n", n=N), ACT.Copy,
                          scale=b("head_mask")[:, h:h + 1])
                t.then_inc(sem("k1_act"), 1)
                if g == 0:
                    act.wait_ge(sem("vo_made"), 1)
                act.wait_ge(sem("v1_mm"), g + 1)
                src = PS[HALF:P, 4 + g, 0:HC].rearrange("q (t c e d) -> q t c e d", t=4, c=4, e=2)
                for h2_ in range(2):
                    t = f(vo_part(h2_, 1, g), src[:, :, :, h2_, :], ACT.Copy)
                t.then_inc(sem("v1_act"), 1)

            scale1 = float(HD) ** -0.5
            for w in range(W8):
                act.wait_ge(sem("att1_turned"), w + 1)
                if w >= 2:
                    act.wait_ge(sem("att1_mixed"), w - 1)
                f(probs[:, w % 2, :], PS[:, w % 2, :], ACT.Exp, scale=scale1).then_inc(sem("att1_probs"), 1)

            for g in range(2):
                act.wait_ge(sem("att1_back"), g + 1)
                f(half(attended, g), PS[:, g, 0:HC], ACT.Copy).then_inc(sem("att1_ready"), 1)
            gelus("ffn2", (0, 4))

            act.wait_ge(sem("pack_c_loaded"), 16)
            for g in range(2):
                ws = slice(4 * g, 4 * g + 4)
                cols = slice(g * HC, (g + 1) * HC)
                act.wait_ge(sem("q2_mm"), g + 1)
                f(half(q2, g), PS[:, 4 * g, 0:HC], ACT.Identity, bias=c("abq")).then_inc(sem("q2_act"), 1)
            for g in range(2):
                act.wait_ge(sem("att2_turned"), g + 1)
                f(p2[:, 2 * g:2 * g + 2, :], PS[:, 4 * g + 1, 0:HC].rearrange("q (u n) -> q u n", n=P),
                  ACT.Exp).then_inc(sem("att2_probs"), 1)

            squares_of("ln1", "ln1_in", (1, 2), sum2)

            for g in range(2):
                act.wait_ge(sem("h4_turned"), g + 1)
                f(half(h4f, g), PS[:, 4 * g, 0:HC], ACT.Copy, scale=c("ln1")).then_inc(sem("h4f_ready"), 1)
            for g in range(2):
                act.wait_ge(sem("v3_mm"), g + 1)
                if g == 0:
                    act.wait_ge(sem("vo3_made"), 1)
                for h2_ in range(2):
                    for p in range(2):
                        src = PS[HALF * p:HALF * (p + 1), 3 + 4 * g, 0:P].rearrange(
                            "q (t c d) -> q t c d", t=4, c=FKV)
                        t = f(vo3_part(h2_, p, g), src, ACT.Copy)
                t.then_inc(sem("v3_ready"), 1)
                act.wait_ge(sem("kr_ready"), g + 1)
                for h in range(2):
                    t = f(k3_heads[:, 4 * g:4 * g + 4, h, :], half(kr, g).rearrange("q (w n) -> q w n", n=N),
                          ACT.Copy, scale=c("fhead_mask")[:, h:h + 1])
                t.then_inc(sem("k3_ready"), 1)
            scale3 = float(FHD) ** -0.5
            for i in range(4):
                act.wait_ge(sem("att3_turned"), i + 1)
                if i >= 2:
                    act.wait_ge(sem("att3_mixed"), i - 1)
                f(probs[:, i % 2, :], PS[:, 2 + 4 * (i % 2), :], ACT.Exp, scale=scale3).then_inc(sem("att3_probs"), 1)

            for g in range(2):
                act.wait_ge(sem("att3_back"), g + 1)
                f(half(attended3, g), PS[:, 2 + 4 * g, 0:HC], ACT.Copy).then_inc(sem("att3_ready"), 1)
            squares_of("rms2", "h5_ready", (1, 2), h5)
            act.wait_ge(sem("parts_turned"), 1)
            f(xf[:, 0, :], PS[:, 1, :], ACT.Copy).then_inc(sem("xf_ready"), 1)
            act.wait_ge(sem("logits_read"), 1)
            f(small["exp"][:, :, :], small["shift"][:, :, :], ACT.Exp).then_inc(sem("router_exp"), 1)
            for n in range(2 * CH):
                act.wait_ge(sem("up_mm"), 2 * n + 1)
                if n >= UPBUF:
                    act.wait_ge(sem("hh_ready"), n - UPBUF + 1)
                f(gate[:, n % UPBUF, :], PS[:, UP_BANKS[n % UPBUF], :], ACT.Silu).then_inc(sem("gated"), 1)
            for s in range(2):
                act.wait_ge(sem("h6_ready"), s + 1)
                f(half(squares, s).rearrange("q (u d) -> q u d", d=D), h6[:, :, s, :], ACT.Square).then_inc(sem("lnf_squared"), 1)

        @block.gpsimd
        def _(pool):
            g_ = nc.gpsimd
            g_.memset(idle_bf[:, :], 0.0).then_inc(sem("idle_made"), 1)
            g_.memset(minus_half[:, :], -0.5).then_inc(sem("minus_half_made"), 1)
            g_.memset(v2[:, :, D:D + 1], 1.0).then_inc(sem("v2_ones"), 1)
            g_.memset(vo[:, :, :, :, :, :], 0.0).then_inc(sem("vo_zero"), 1)
            for h2_ in range(2):
                pool.wait_ge(sem("vo_zero"), h2_ + 1)
                g_.memset(vo[HALF * h2_:HALF * h2_ + HALF, :, :, :, h2_, HD:HD + 1], 1.0).then_inc(sem("vo_zero"), 1)
            pool.wait_ge(sem("vo_zero"), 3)
            g_.memset(spare[:, 0:1], 0.0).then_inc(sem("vo_made"), 1)

            def powers(name, dst=rstd, src=var):
                for g in range(2):
                    pool.wait_ge(sem(name + "_var"), g + 1)
                    g_.tensor_tensor(dst[:, 4 * g:4 * g + 4], src[:, 4 * g:4 * g + 4],
                                     minus_half[:, 4 * g:4 * g + 4], ALU.pow).then_inc(sem(name + "_rstd"), 1)

            pool.wait_ge(sem("minus_half_made"), 1)
            powers("ln0")
            g_.memset(vo3[:, :, :, :, :, :], 0.0).then_inc(sem("vo3_zero"), 1)
            for h2_ in range(2):
                pool.wait_ge(sem("vo3_zero"), h2_ + 1)
                g_.memset(vo3[HALF * h2_:HALF * h2_ + HALF, :, :, :, h2_, FHD:FHD + 1], 1.0).then_inc(sem("vo3_zero"), 1)
            pool.wait_ge(sem("vo3_zero"), 3)
            g_.memset(spare[:, 0:1], 0.0).then_inc(sem("vo3_made"), 1)

            pool.wait_ge(sem("pack_c_loaded"), 16)
            g_.tensor_scalar(router_s[:, :], c("router"), c("ln2"), None, ALU.mult).then_inc(sem("router_s"), 1)
            pool.wait_ge(sem("router_s"), 1)
            g_.tensor_copy(router_hi[:, :], router_s[:, :]).then_inc(sem("router_h"), 1)
            pool.wait_ge(sem("router_h"), 1)
            g_.tensor_tensor(router_lo[:, :], router_s[:, :], router_hi[:, :].bitcast(F32),
                             ALU.subtract).then_inc(sem("router_made"), 1)
            g_.tensor_copy(causal_bf[:, :], c("causal")).then_inc(sem("causal_made"), 1)
            g_.tensor_copy(ident_bf[:, :], a("ident")).then_inc(sem("ident_bf_made"), 1)
            pool.wait_ge(sem("up_w_loaded"), 16)
            g_.tensor_scalar(up_w[:, :], up_w[:, :], c("ln2"), None, ALU.mult).then_inc(sem("up_scaled"), 1)
            pool.wait_ge(sem("up_scaled"), 1)
            g_.tensor_copy(up_hi[:, :], up_w[:, :]).then_inc(sem("up_h"), 1)
            pool.wait_ge(sem("up_h"), 1)
            g_.tensor_tensor(up_lo[:, :], up_w[:, :], up_hi[:, :].bitcast(F32), ALU.subtract).then_inc(sem("up_split"), 1)

            powers("rms1", rstd_rms, var_rms)
            powers("ln1")
            for g in range(2):
                pool.wait_ge(sem("rope_q"), g + 1)
                g_.tensor_tensor(half(q3, g), half(rope[:, 0], g), half(rope[:, 1], g), ALU.add).then_inc(sem("q3_ready"), 1)
            powers("rms2")
            pool.wait_ge(sem("h5_ready"), 2)
            g_.tensor_tensor(h45[:, :], h4[:, :], h5[:, :], ALU.add).then_inc(sem("h45_ready"), 1)
            powers("lnf")

        @block.vector
        def _(ve):
            v = nc.vector

            def centre(name, w, n):
                blocks = w.rearrange("q (n d) -> q n d", d=D)
                v.reduce_sum(means[:, 0:n], blocks, AX).then_inc(sem(name + "_sum"), 1)
                ve.wait_ge(sem(name + "_sum"), 1)
                return v.scalar_tensor_tensor(out=blocks, in0=means[:, 0:n].unsqueeze(2).to_broadcast([P, n, D]),
                                              scalar=-1.0 / D, in1=blocks, op0=ALU.mult, op1=ALU.add)

            def sum_squares(name, g):
                ve.wait_ge(sem(name + "_squared"), g + 1)
                v.reduce_sum(sq_sums[:, 4 * g:4 * g + 4], tiles(squares)[:, 4 * g:4 * g + 4], AX)\
                    .then_inc(sem(name + "_sq_sum"), 1)

            def variance(name, g, dst, factor, eps):
                ts = slice(4 * g, 4 * g + 4)
                v.tensor_scalar(dst[:, ts], sq_sums[:, ts], factor, eps, ALU.mult, ALU.add).then_inc(sem(name + "_var"), 1)

            def scale(name, g, dst, src, by):
                ts = slice(4 * g, 4 * g + 4)
                ve.wait_ge(sem(name + "_rstd"), g + 1)
                return v.tensor_tensor(tiles(dst)[:, ts], tiles(src)[:, ts], by[:, ts].unsqueeze(2).to_broadcast([P, 4, D]),
                                       ALU.mult)

            def normalise(name, src, dst, eps):
                for g in range(2):
                    sum_squares(name, g)
                for g in range(2):
                    ve.wait_ge(sem(name + "_sq_sum"), g + 1)
                    variance(name, g, var, 1.0 / D, eps)
                for g in range(2):
                    scale(name, g, dst, src, rstd).then_inc(sem(name + "_normed"), 1)

            def group(k):
                ve.wait_ge(sem(f"x_loaded{k}"), 16)
                if k >= 2:
                    ve.wait_ge(sem("patches_turned"), 2 * k - 2)
                v.tensor_copy(x_patches[:, k % 2, :].rearrange("q (j r w) -> q j r w", j=GRID, r=8),
                              x_sb[:, k, :].rearrange("q (r j w) -> q j r w", r=8, j=GRID)).then_inc(sem("x_grouped"), 1)

            ve.wait_ge(sem("pack_a_loaded"), 16)
            centre("conv", A[:, columns(PACK_A, "conv").start:columns(PACK_A, "conv_b").stop], KCH + 1)\
                .then_inc(sem("conv_centred"), 1)
            group(0)
            for k in range(KCH):
                if k + 1 < KCH:
                    group(k + 1)
                ve.wait_ge(sem("patches_turned"), 2 * k + 2)
                if k >= 2:
                    ve.wait_ge(sem("conv_summed"), k - 1)
                v.tensor_copy(patches[:, k % 2, 512:1024], PS[:, 2 * (k % 2) + 1, :]).then_inc(sem("patches_copied_dve"), 1)

            v.tensor_scalar(pos_b[:, :], a("pos"), a("ln_b"), None, ALU.add).then_inc(sem("pos_b_made"), 1)
            normalise("ln0", PS[:, 4, :], normed, EPS)
            ve.wait_ge(sem("emb_turned"), 1)
            ve.wait_ge(sem("pos_b_made"), 1)
            turned = PS[:, 5, :].rearrange("q (j w i) -> q w i j", j=GRID, w=W8)
            grid = pos_b[:, :].rearrange("q (i j) -> q i j", j=GRID).unsqueeze(1).to_broadcast([P, W8 // 2, GRID, GRID])
            for g in range(2):
                v.scalar_tensor_tensor(out=half(h0, g).rearrange("q (w i j) -> q w i j", i=GRID, j=GRID),
                                       in0=turned[:, 4 * g:4 * g + 4], scalar=a("ln_w"), in1=grid,
                                       op0=ALU.mult, op1=ALU.add).then_inc(sem("ffn1_in"), 1)
            ve.wait_ge(sem("pack_b_loaded"), 16)
            ve.wait_ge(sem("proj_bv"), 1)
            v.tensor_tensor(proj_bias[:, :], PS[:, 4, 0:1], b("bp"), ALU.add).then_inc(sem("proj_bias_made"), 1)
            ve.wait_ge(sem("pack_c_loaded"), 16)
            ve.wait_ge(sem("conv_centred"), 1)
            centre("av", c("av"), 2).then_inc(sem("v2_centred"), 1)
            ve.wait_ge(sem("v2_centred"), 1)
            centre("abv", c("abv"), 1).then_inc(sem("v2_centred"), 1)
            ve.wait_ge(sem("v2_centred"), 2)
            ve.wait_ge(sem("down_w_loaded"), 16)
            centre("down", down_w[:, :], DOWN_AT[CH] // D).then_inc(sem("down_centred"), 1)
            v.tensor_scalar(bias[:, :], c("cosines")[:, N:2 * N], c("beta")[:, 1:2], None, ALU.mult).then_inc(sem("bias_part"), 1)
            ve.wait_ge(sem("bias_part"), 1)
            v.scalar_tensor_tensor(out=bias[:, :], in0=c("cosines")[:, 0:N], scalar=c("beta")[:, 0:1], in1=bias[:, :],
                                   op0=ALU.mult, op1=ALU.add).then_inc(sem("bias_made"), 1)

            for g in range(2):
                ws = slice(4 * g, 4 * g + 4)
                cols = slice(g * HC, (g + 1) * HC)
                ve.wait_ge(sem("k1_mm"), g + 1)
                v.tensor_scalar(half(kf, g), PS[:, 2 * g + 1, 0:HC], b("bk"), None, ALU.add).then_inc(sem("kf_ready"), 1)
                ve.wait_ge(sem("kf_ready"), g + 1)
                for h in (0, 1):
                    t = v.tensor_scalar(k_heads[:, ws, h, :], half(kf, g).rearrange("q (w n) -> q w n", n=N),
                                        b("head_mask")[:, h:h + 1], None, ALU.mult)
                t.then_inc(sem("k1_dve"), 1)
                if g == 0:
                    ve.wait_ge(sem("vo_made"), 1)
                ve.wait_ge(sem("v1_mm"), g + 1)
                src = PS[0:HALF, 4 + g, 0:HC].rearrange("q (t c e d) -> q t c e d", t=4, c=4, e=2)
                for h2_ in range(2):
                    t = v.tensor_copy(vo_part(h2_, 0, g), src[:, :, :, h2_, :])
                t.then_inc(sem("v1_dve"), 1)

            def shift(name, rows, n):
                ve.wait_ge(sem(name + "_scores"), n + 1 if name == "att1" else n // 2 + 1)
                if n >= 2:
                    ve.wait_ge(sem(name + "_turned"), n - 1)
                tops = top[:, n % 2, :].rearrange("q (b h) -> q b h", b=2)
                v.reduce_max(tops, rows, AX).then_inc(sem(name + "_top"), 1)
                ve.wait_ge(sem(name + "_top"), n + 1)
                v.tensor_tensor(shifted[:, n % 2, :].rearrange("q (b h n) -> q b h n", b=2, n=N), rows,
                                tops.unsqueeze(3).to_broadcast([P, 2, 4, N]), ALU.subtract)\
                    .then_inc(sem(name + "_shifted"), 1)

            def divide(name, bank, g, heads, size):
                ve.wait_ge(sem(name + "_mixed"), (4 if name == "att1" else 2) * (g + 1))
                mix = PS[:, bank, 0:4 * heads * (size + 1)].rearrange("q (w h d) -> q w h d", w=4, h=heads)
                rec = r1[:, 4 * g:4 * g + 4, 0:heads]
                v.reciprocal(rec, mix[:, :, :, size]).then_inc(sem(name + "_recip"), 1)
                ve.wait_ge(sem(name + "_recip"), g + 1)
                v.tensor_tensor(on[:, 4 * g:4 * g + 4, :].rearrange("q w (h d) -> q w h d", h=heads), mix[:, :, :, 0:size],
                                rec.unsqueeze(3).to_broadcast([P, 4, heads, size]), ALU.mult)\
                    .then_inc(sem(name + "_divided"), 1)

            for w in range(W8):
                banks = SCORE_BANKS1[w % 2]
                shift("att1", PS[:, banks:banks + 2, 0:HC].rearrange("q b (h n) -> q b h n", n=N), w)
                if w == 6:
                    divide("att1", 4, 0, HEADS, HD)
            divide("att1", 5, 1, HEADS, HD)

            ve.wait_ge(sem("proj_bias_made"), 1)
            for g in range(2):
                ve.wait_ge(sem("proj_mm"), g + 1)
                v.scalar_tensor_tensor(out=half(h2, g), in0=PS[:, 2 + g, 0:HC], scalar=proj_bias[:, 0:1],
                                       in1=half(h0, g), op0=ALU.add, op1=ALU.add).then_inc(sem("ffn2_in"), 1)
            for g in range(2):
                ve.wait_ge(sem("ffn2_down"), g + 1)
                v.scalar_tensor_tensor(out=half(h3, g), in0=PS[:, 6 + g, 0:HC], scalar=b("ff2_b"),
                                       in1=half(h2, g), op0=ALU.add, op1=ALU.add).then_inc(sem("h3_ready"), 1)

            for g in range(2):
                cols = slice(g * HC, (g + 1) * HC)
                ve.wait_ge(sem("k2_mm"), g + 1)
                v.tensor_scalar(half(k2, g), PS[:, 4 * g + 1, 0:HC], c("abk"), None, ALU.add).then_inc(sem("k2_dve"), 1)
                ve.wait_ge(sem("v2_mm"), g + 1)
                v.tensor_tensor(v2[:, 4 * g:4 * g + 4, 0:D], PS[:, 4 * g + 2, 0:HC].rearrange("q (t d) -> q t d", d=D),
                                c("abv").unsqueeze(1).to_broadcast([P, 4, D]), ALU.add).then_inc(sem("v2_ready"), 1)
            ve.wait_ge(sem("bias_made"), 1)
            for g in range(2):
                ts = slice(4 * g, 4 * g + 4)
                ve.wait_ge(sem("att2_scores"), g + 1)
                v.scalar_tensor_tensor(out=tiles(s2)[:, ts], in0=PS[:, 4 * g, 0:HC].rearrange("q (w n) -> q w n", n=N),
                                       scalar=float(D) ** -0.5, in1=bias[:, :].unsqueeze(1).to_broadcast([P, 4, N]),
                                       op0=ALU.mult, op1=ALU.add).then_inc(sem("att2_biased"), 1)
            for g in range(2):
                ts = slice(4 * g, 4 * g + 4)
                ve.wait_ge(sem("att2_biased"), g + 1)
                v.reduce_max(s2_top[:, ts], tiles(s2)[:, ts], AX).then_inc(sem("att2_top"), 1)
            for g in range(2):
                ts = slice(4 * g, 4 * g + 4)
                ve.wait_ge(sem("att2_top"), g + 1)
                v.tensor_tensor(tiles(s2_shift)[:, ts], tiles(s2)[:, ts], s2_top[:, ts].unsqueeze(2).to_broadcast([P, 4, N]),
                                ALU.subtract).then_inc(sem("att2_shifted"), 1)
            for g in range(2):
                mixed2 = PS[:, 4 * g + 2, 0:4 * (D + 1)].rearrange("q (t d) -> q t d", d=D + 1)
                ve.wait_ge(sem("att2_mixed"), g + 1)
                v.reciprocal(r2[:, 4 * g:4 * g + 4], mixed2[:, :, D]).then_inc(sem("att2_recip"), 1)
            for g in range(2):
                ts = slice(4 * g, 4 * g + 4)
                mixed2 = PS[:, 4 * g + 2, 0:4 * (D + 1)].rearrange("q (t d) -> q t d", d=D + 1)
                ve.wait_ge(sem("att2_recip"), g + 1)
                v.tensor_tensor(tiles(o2)[:, ts], mixed2[:, :, 0:D], r2[:, ts].unsqueeze(2).to_broadcast([P, 4, D]),
                                ALU.mult).then_inc(sem("o2_ready"), 1)
            for g in range(2):
                ve.wait_ge(sem("h3_turned"), g + 1)
                ve.wait_ge(sem("o2_ready"), g + 1)
                v.tensor_tensor(half(sum2, g), PS[:, 4 * g + 3, 0:HC], half(o2, g), ALU.add).then_inc(sem("ln1_in"), 1)
            for g in range(2):
                sum_squares("ln1", g)
            for g in range(2):
                ve.wait_ge(sem("ln1_sq_sum"), g + 1)
                variance("rms1", g, var_rms, (1.0 + EPS_RMS) / D, EPS_RMS * EPS)
            for g in range(2):
                variance("ln1", g, var, 1.0 / D, EPS)
            for g in range(2):
                scale("rms1", g, h4n, sum2, rstd_rms).then_inc(sem("h4n_ready"), 1)
            for g in range(2):
                scale("ln1", g, h4, sum2, rstd).then_inc(sem("h4_ready"), 1)
            cos = c("rope_cos").unsqueeze(1).to_broadcast([P, 4, N])
            sin = c("rope_sin").unsqueeze(1).to_broadcast([P, 4, N])
            for g in range(2):
                cols = slice(g * HC, (g + 1) * HC)
                for n in range(4):
                    ve.wait_ge(sem("qk3_mm"), 2 * g + n // 2 + 1)
                    t = v.tensor_tensor(rope[:, n, cols].rearrange("q (w n) -> q w n", n=N),
                                        PS[:, 1 + 4 * g + n // 2, (n % 2) * HC:(n % 2 + 1) * HC].rearrange(
                                            "q (w n) -> q w n", n=N),
                                        sin if n % 2 else cos, ALU.mult)
                    if n == 1:
                        t.then_inc(sem("rope_q"), 1)
                t.then_inc(sem("rope_k"), 1)
                ve.wait_ge(sem("rope_k"), g + 1)
                v.tensor_tensor(half(kr, g), rope[:, 2, cols], rope[:, 3, cols], ALU.add).then_inc(sem("kr_ready"), 1)
            for i in range(4):
                g, hg = i // 2, i % 2
                shift("att3", PS[:, 4 * g + hg, :].rearrange("q (b h n) -> q b h n", b=2, n=N), i)
            divide("att3", 3, 0, FH, FHD)
            divide("att3", 7, 1, FH, FHD)
            for g in range(2):
                ve.wait_ge(sem("fo_mm"), g + 1)
                v.tensor_tensor(half(h5, g), PS[:, 4 * g, 0:HC], half(h4, g), ALU.add).then_inc(sem("h5_ready"), 1)

            normalise("rms2", h5, h5n, EPS_RMS)
            for g in range(2):
                ts = slice(4 * g, 4 * g + 4)
                ve.wait_ge(sem("rms2_normed"), g + 1)
                v.tensor_copy(parts[:, ts, 0, :].bitcast(F32R), tiles(h5n)[:, ts]).then_inc(sem("high_ready"), 1)
            for g in range(2):
                ts = slice(4 * g, 4 * g + 4)
                ve.wait_ge(sem("high_ready"), g + 1)
                v.tensor_tensor(parts[:, ts, 1, :], tiles(h5n)[:, ts], parts[:, ts, 0, :], ALU.subtract)\
                    .then_inc(sem("parts_ready"), 1)
            ve.wait_ge(sem("parts_turned"), 1)
            v.tensor_copy(xf[:, 1, :], PS[:, 5, :]).then_inc(sem("xf_ready"), 1)

            def spread(name):
                return few[name][:, :].unsqueeze(2).to_broadcast([P, 8, NE])

            rank = c("rank").unsqueeze(1).to_broadcast([P, 8, NE])
            logits = PS[:, 2, 0:8 * NE].rearrange("q (t e) -> q t e", e=NE)
            routed = sem("router_step")
            ve.wait_ge(sem("logits_mm"), 1)
            v.reduce_max(few["top"][:, :], logits, AX).then_inc(routed, 1)
            ve.wait_ge(routed, 1)
            v.tensor_tensor(small["shift"][:, :, :], logits, spread("top"), ALU.subtract).then_inc(sem("logits_read"), 1)

            def top_of(dst, src):
                return lambda: v.reduce_max(few[dst][:, :], small[src][:, :, :], AX)

            def pair(dst, x0, x1, op):
                return lambda: v.tensor_tensor(small[dst][:, :, :], small[x0][:, :, :], x1, op)

            def few_pair(dst, x0, x1, op):
                return lambda: v.tensor_tensor(few[dst][:, :], few[x0][:, :], few[x1][:, :], op)

            router_steps = [
                lambda: v.reduce_sum(few["sum"][:, :], small["exp"][:, :, :], AX),
                lambda: v.reciprocal(few["rsum"][:, :], few["sum"][:, :]),
                pair("prob", "exp", spread("rsum"), ALU.mult),
                top_of("first", "prob"),
                pair("same1", "prob", spread("first"), ALU.is_equal),
                pair("rank1", "same1", rank, ALU.mult),
                top_of("first_rank", "rank1"),
                pair("one1", "rank1", spread("first_rank"), ALU.is_equal),
                lambda: v.scalar_tensor_tensor(out=small["prob2"][:, :, :], in0=small["one1"][:, :, :], scalar=-2.0,
                                               in1=small["prob"][:, :, :], op0=ALU.mult, op1=ALU.add),
                top_of("second", "prob2"),
                pair("same2", "prob2", spread("second"), ALU.is_equal),
                pair("rank2", "same2", rank, ALU.mult),
                top_of("second_rank", "rank2"),
                pair("one2", "rank2", spread("second_rank"), ALU.is_equal),
                pair("part1", "one1", spread("first"), ALU.mult),
                pair("part2", "one2", spread("second"), ALU.mult),
                pair("both", "part1", small["part2"][:, :, :], ALU.add),
                few_pair("total", "first", "second", ALU.add),
                lambda: v.tensor_scalar(few["total_eps"][:, :], few["total"][:, :], 1e-9, None, ALU.add),
                lambda: v.reciprocal(few["rtotal"][:, :], few["total_eps"][:, :]),
                pair("weights", "both", spread("rtotal"), ALU.mult),
            ]
            for n in range(2 * CH):
                s, ch = n // CH, n % CH
                ve.wait_ge(sem("gated"), n + 1)
                ve.wait_ge(sem("up_mm"), 2 * n + 2)
                v.tensor_tensor(hh[:, ch, s, :], PS[:, UP_BANKS[n % UPBUF] + 1, :], gate[:, n % UPBUF, :], ALU.mult)\
                    .then_inc(sem("hh_ready"), 1)
                if n < len(router_steps):
                    if n == 0:
                        ve.wait_ge(sem("router_exp"), 1)
                    else:
                        ve.wait_ge(routed, n + 1)
                    router_steps[n]().then_inc(routed, 1)

            ve.wait_ge(sem("h45_ready"), 1)
            ve.wait_ge(sem("down_centred"), 1)
            centre("h45", h45[:, :], 8).then_inc(sem("h45_centred"), 1)

            ve.wait_ge(routed, len(router_steps) + 1)
            for s in range(2):
                for u in range(4):
                    n = 4 * s + u
                    ve.wait_ge(sem("down_mm"), n + 1)
                    v.tensor_tensor(weighted[:, n % 2], PS[:, DOWN_BANKS[n % 4], :].rearrange("q (e d) -> q e d", d=D),
                                    small["weights"][:, 2 * u + s, :].unsqueeze(2).to_broadcast([P, NE, D]), ALU.mult)\
                        .then_inc(sem("tile_weighted"), 1)
                    ve.wait_ge(sem("tile_weighted"), n + 1)
                    v.reduce_sum(mixed[:, u, s, :], weighted[:, n % 2].rearrange("q e d -> q d e"), AX)\
                        .then_inc(sem("tile_mixed"), 1)
                ts = slice(4 * s, 4 * s + 4)
                h45u = h45[:, :].rearrange("q (u s d) -> q u s d", s=2, d=D)
                ve.wait_ge(sem("tile_mixed"), 4 * s + 4)
                ve.wait_ge(sem("h45_centred"), 1)
                v.tensor_tensor(h6[:, :, s, :], mixed[:, :, s, :], h45u[:, :, s, :], ALU.add).then_inc(sem("h6_ready"), 1)
                ve.wait_ge(sem("lnf_squared"), s + 1)
                v.reduce_sum(sq_sums[:, ts], tiles(squares)[:, ts], AX).then_inc(sem("lnf_sq_sum"), 1)
                ve.wait_ge(sem("lnf_sq_sum"), s + 1)
                v.tensor_scalar(var[:, ts], sq_sums[:, ts], 1.0 / D, EPS, ALU.mult, ALU.add).then_inc(sem("lnf_var"), 1)
                ve.wait_ge(sem("lnf_rstd"), s + 1)
                v.tensor_tensor(out_sb[:, s], h6[:, :, s, :], rstd[:, ts].unsqueeze(2).to_broadcast([P, 4, D]),
                                ALU.mult).then_inc(sem("out_normed"), 1)


def layouts(np, t):
    def w(name):
        return np.asarray(t[name])

    def both(m):
        return np.concatenate([m, m], axis=0)

    def diag(m):
        n = m.shape[1]
        z = np.zeros((P, 2 * n), np.float32)
        z[:D, :n] = m
        z[D:, n:] = m
        return z

    def col(vec):
        return both(vec.reshape(D, 1))

    def row(vec):
        return np.broadcast_to(vec.reshape(1, -1), (P, vec.size))

    def pack(names, parts):
        assert {k: v.shape[1] for k, v in parts.items()} == names, \
            {k: v.shape for k, v in parts.items() if v.shape[1] != names.get(k)}
        return np.ascontiguousarray(np.concatenate([parts[k] for k in names], axis=1))

    pos = np.arange(N, dtype=np.float32)[:, None]
    i = np.arange(0, D, 2, dtype=np.float32)
    ang = pos * np.exp(-np.log(np.float32(10000.0)) * i / np.float32(D)).astype(np.float32)
    pe = np.stack([np.sin(ang), np.cos(ang)], axis=-1).reshape(N, D).astype(np.float32)
    conv = w("L0_tok_conv_w").reshape(D, KCH, P).transpose(2, 1, 0).reshape(P, KCH * D)
    pack_a = pack(PACK_A, dict(
        ident=np.eye(P, dtype=np.float32), conv=conv, conv_b=row(w("L0_tok_conv_b")),
        ones=np.ones((P, P), np.float32), pos=both(pe.T),
        ln_w=col(w("L0_tok_ln_w")), ln_b=col(w("L0_tok_ln_b"))))

    qkv, qkv_b = w("L0_tok_qkv_w"), w("L0_tok_qkv_b")
    feature = np.arange(P)[:, None] % D
    pack_b = pack(PACK_B, dict(
        ff1=both(w("L0_tok_ff_w1").T), ff1_b=w("L0_tok_ff_b1").reshape(2, P).T,
        ff2=w("L0_tok_ff_w2").T.reshape(2, P, D).transpose(1, 0, 2).reshape(P, 2 * D), ff2_b=col(w("L0_tok_ff_b2")),
        wq=diag(qkv[0:D].T), wk=diag(qkv[D:2 * D].T), wv=diag(qkv[2 * D:].T), proj=diag(w("L0_tok_proj_w").T),
        bq=col(qkv_b[0:D]), bk=col(qkv_b[D:2 * D]), bv=col(qkv_b[2 * D:]), bp=col(w("L0_tok_proj_b")),
        head_mask=(feature // HD % (HEADS // 2) == np.arange(HEADS // 2)[None, :]).astype(np.float32)))

    n = np.arange(N, dtype=np.float32)
    dist = np.abs(n[:, None] - n[None, :])
    two_pi = np.float32(2.0 * np.pi)
    cosines = np.concatenate([np.cos(two_pi * dist / np.float32(period)) for period in (24.0, 720.0)], axis=1)
    inv_freq = 1.0 / 10000.0 ** (np.arange(0, FHD, 2, dtype=np.float32) / FHD)
    freqs = np.outer(n, inv_freq)
    emb = np.concatenate([freqs, freqs], axis=-1)
    cos, sin = np.cos(emb).T.astype(np.float32), np.sin(emb).T.astype(np.float32)
    sign = np.where(np.arange(FHD) < FHD // 2, -1.0, 1.0)[:, None].astype(np.float32)
    turned = (np.arange(FHD) + FHD // 2) % FHD
    wq = w("L0_ffn_wq").reshape(FH, FHD, D)
    wk = w("L0_ffn_wk").reshape(FKV, FHD, D)[[h // (FH // FKV) for h in range(FH)]]
    causal = np.where(n[:, None] >= n[None, :], 0.0, -1e30).astype(np.float32)
    pack_c = pack(PACK_C, dict(
        aq=diag(w("L0_attn_Wq").T), ak=diag(w("L0_attn_Wk").T), av=diag(w("L0_attn_Wv").T),
        abq=col(w("L0_attn_bq")), abk=col(w("L0_attn_bk")), abv=row(w("L0_attn_bv")), beta=row(w("L0_attn_beta")),
        cosines=both(cosines.astype(np.float32)),
        fq=diag(wq.reshape(D, D).T), fq_turned=diag(wq[:, turned].reshape(D, D).T),
        fk=diag(wk.reshape(D, D).T), fk_turned=diag(wk[:, turned].reshape(D, D).T),
        fv=diag(w("L0_ffn_wv").T), fo=diag(w("L0_ffn_wo").T), router=both(w("L0_ffn_router_w").T),
        rope_cos=both(np.tile(cos, (FH, 1))), rope_sin=both(np.tile(sign * sin, (FH, 1))),
        causal=both(np.tile(causal, (1, 2))),
        fhead_mask=(feature // FHD % (FH // 2) == np.arange(FH // 2)[None, :]).astype(np.float32),
        rank=row(np.arange(NE, 0, -1).astype(np.float32)), ln1=col(w("L0_ffn_ln1_w")), ln2=col(w("L0_ffn_ln2_w")),
        centring=np.kron(np.eye(2), np.eye(D) - 1.0 / D).astype(np.float32)))

    up = np.zeros((2, CH * P, D), np.float32)
    down = np.zeros((P, DOWN_AT[CH]), np.float32)
    w2 = w("L0_ffn_w2").transpose(0, 2, 1)
    for v, name in enumerate(("L0_ffn_w1", "L0_ffn_w3")):
        up[v, :NE * HID] = w(name).reshape(NE * HID, D)
    up = up.reshape(2, CH, P, D).transpose(1, 0, 2, 3)
    for ch in range(CH):
        for n, ex in enumerate(experts_of(ch)):
            r0, r1 = max(ch * P, ex * HID), min((ch + 1) * P, (ex + 1) * HID)
            down[r0 - ch * P:r1 - ch * P, DOWN_AT[ch] + n * D:DOWN_AT[ch] + (n + 1) * D] = w2[ex, r0 - ex * HID:r1 - ex * HID]
    pack_d = np.ascontiguousarray(both(up.reshape(2 * CH * P, D).T))
    return dict(x=np.ascontiguousarray(w("x")), pack_a=pack_a, pack_b=pack_b, pack_c=pack_c, pack_d=pack_d, pack_e=down)


def kernel(**inputs):
    import numpy as np
    import concourse.bacc as bacc
    from concourse.bass_utils import run_bass_kernel_spmd

    nc = bacc.Bacc("TRN2", target_bir_lowering=False, num_devices=1)
    arrays, args = {}, []
    for name, arr in layouts(np, inputs).items():
        arrays[name + "_dram"] = arr
        args.append(nc.dram_tensor(name + "_dram", arr.shape, mybir.dt.from_np(arr.dtype), kind="ExternalInput").ap())
    args.append(nc.dram_tensor("out_dram", (B, N, D), F32, kind="ExternalOutput").ap())
    build(nc, *args)
    r = run_bass_kernel_spmd(nc, [arrays], core_ids=[0])
    return r.results[0]["out_dram"]
```

```python
import math
from contextlib import ExitStack

import concourse.bass as bass
from concourse import mybir

ALU = mybir.AluOpType
ACT = mybir.ActivationFunctionType
AX = mybir.AxisListType.X
F32 = mybir.dt.float32
F32R = mybir.dt.float32r
BF16 = mybir.dt.bfloat16

P = 128
B, C, IMG, PATCH = 16, 3, 128, 16
GRID = IMG // PATCH
N = GRID * GRID
D = 64
HALF = 64
COLS = B * N * D // P
HC = COLS // 2
KCH = C * PATCH * PATCH // P
W8 = B // 2
HEADS, HD = 8, 8
FF = 256
FH, FHD, FKV = 4, 16, 2
NE, HID = 8, 170
CH = -(-NE * HID // P)
UPBUF = 3


def experts_of(chunk):
    return range(chunk * P // HID, min((chunk * P + P - 1) // HID, NE - 1) + 1)


DOWN_AT = [D * sum(len(experts_of(ch)) for ch in range(n)) for n in range(CH + 1)]
EPS = 1e-5
EPS_RMS = 1e-6

PACK_A = dict(ident=P, conv=KCH * D, conv_b=1, centring=P, pos=N, ln_w=1, ln_b=1)
PACK_B = dict(ff1=FF, ff1_b=2, ff2=2 * D, ff2_b=1, wq=P, wk=P, wv=P, proj=P, bq=1, bk=1, bv=1, bp=1,
              head_mask=HEADS)
PACK_C = dict(aq=P, ak=P, av=P, abq=1, abk=1, abv=D, beta=2, cosines=2 * N,
              fq=P, fq_turned=P, fk=P, fk_turned=P, fv=2 * FKV * FHD, fo=P, router=NE, rope_cos=N, rope_sin=N,
              causal=2 * N, fhead_mask=FH // 2, rank=NE, ln1=1, ln2=1)
PACK_D = dict(up=2 * CH * P)
PACK_E = dict(down=DOWN_AT[CH])


def width(pack):
    return sum(pack.values())


def columns(pack, name):
    at = 0
    for key, n in pack.items():
        if key == name:
            return slice(at, at + n)
        at += n
    raise KeyError(name)


def build(nc, x, pack_a, pack_b, pack_c, pack_d, pack_e, out):
    with ExitStack() as ctx:
        def sb(name, shape, dt=F32):
            return ctx.enter_context(nc.sbuf_tensor(name, shape, dt))

        made = {}

        def sem(name):
            if name not in made:
                made[name] = ctx.enter_context(nc.semaphore(name))
            return made[name]

        idle_bf = sb("idle_bf", [P, 512], BF16)
        PS = ctx.enter_context(nc.psum_tensor("PS", [P, 8, 512], F32))

        A = sb("pack_a_sb", [P, width(PACK_A)])
        Bp = sb("pack_b_sb", [P, width(PACK_B)])
        Cp = sb("pack_c_sb", [P, width(PACK_C)])
        up_w = sb("up_w", [P, 2 * CH * P])
        up_hi = sb("up_hi", [P, 2 * CH * P], F32R)
        up_lo = sb("up_lo", [P, 2 * CH * P], F32R)
        down_w = sb("down_w", [P, DOWN_AT[CH]])

        def a(name):
            return A[:, columns(PACK_A, name)]

        def b(name):
            return Bp[:, columns(PACK_B, name)]

        def c(name):
            return Cp[:, columns(PACK_C, name)]

        shared_x = sb("shared_x", [P, KCH * 1024])
        shared_p = sb("shared_p", [P, 4 * COLS])
        shared_f = sb("shared_f", [P, 4 * COLS])
        shared_h = sb("shared_h", [P, CH * 2 * COLS])
        x_sb = shared_x[:, :].rearrange("q (k c) -> q k c", k=KCH)
        patches = shared_p[:, :].rearrange("q (k c) -> q k c", k=2)
        x_patches = shared_f[:, :].rearrange("q (k c) -> q k c", k=2)
        kf = sb("kf", [P, COLS])
        emb = kf
        means = sb("means", [P, DOWN_AT[CH] // D])
        squares = sb("squares", [P, COLS])
        normed = sb("normed", [P, COLS])
        sq_sums = sb("sq_sums", [P, 8])
        std = sb("std", [P, 8])
        rstd = sb("rstd", [P, 8])
        std_rms = sb("std_rms", [P, 8])
        rstd_rms = sb("rstd_rms", [P, 8])
        spare = sb("spare", [P, 1])
        consts = sb("consts", [P, 4])
        euler = sb("euler", [P, 8, NE])
        table_use = sb("table_use", [P, 1])
        pos_b = sb("pos_b", [P, N])
        proj_bias = sb("proj_bias", [P, 1])
        h0 = sb("h0", [P, COLS])
        hidden = shared_f[:, :].rearrange("q (m s c) -> q m s c", m=2, s=2)
        f1 = sb("f1", [P, COLS])
        h2 = sb("h2", [P, COLS])
        h3 = sb("h3", [P, COLS])
        qf = sb("qf", [P, COLS])
        k_heads = shared_h[:, 0:W8 * HEADS * N].rearrange("q (w h n) -> q w h n", w=W8, h=HEADS)
        vo = sb("vo", [P, 2, W8, 4, 2, HD + 1])
        r1 = sb("r1", [P, W8, HEADS])
        top = sb("top", [P, 2, HEADS])
        shifted = sb("shifted", [P, 2, COLS])
        probs = sb("probs", [P, 2, COLS])
        attended = sb("attended", [P, COLS])
        bias = sb("bias", [P, N])
        q2_bias = sb("q2_bias", [P, 1])
        q2 = qf
        k2 = sb("k2", [P, COLS])
        v2 = sb("v2", [P, W8, D + 1])
        s2 = sb("s2", [P, COLS])
        on = s2[:, :].rearrange("q (w d) -> q w d", d=D)
        s2_top = sb("s2_top", [P, W8])
        s2_shift = sb("s2_shift", [P, COLS])
        p2 = sb("p2", [P, 4, P])
        r2 = sb("r2", [P, W8])
        o2 = attended
        sum2 = h2
        h4 = sb("h4", [P, COLS])
        h4n = kf
        h4f = h0
        rope = shared_f[:, :].rearrange("q (k c) -> q k c", k=4)
        kr = sb("kr", [P, COLS])
        q3 = qf
        vo3 = sb("vo3", [P, 2, W8, FKV, 2, FHD + 1])
        k3_heads = shared_x[:, 0:W8 * 2 * N].rearrange("q (w h n) -> q w h n", w=W8, h=2)
        causal_bf = sb("causal_bf", [P, 8 * N], BF16)
        ident_bf = sb("ident_bf", [P, P], BF16)
        attended3 = attended
        h5 = f1
        h45 = attended
        h5n = normed
        parts = sb("parts", [P, W8, 2, N])
        xf = sb("xf", [P, 2, COLS], F32R)
        router_s = sb("router_s", [P, NE])
        router_parts = sb("router_parts", [P, 2, NE], F32R)
        gate = shared_f[:, 0:UPBUF * COLS].rearrange("q (k c) -> q k c", k=UPBUF)
        hh = shared_h[:, 0:CH * 2 * COLS].rearrange("q (c s t) -> q c s t", c=CH, s=2)
        small = {k: sb("r_" + k, [P, 8, NE]) for k in
                 ("low", "logits", "shift", "exp", "prob", "same1", "rank1", "one1", "prob2", "same2", "rank2", "one2",
                  "part1", "part2", "both", "weights")}
        few = {k: sb("r_" + k, [P, 8]) for k in
               ("top", "sum", "rsum", "first", "first_rank", "second", "second_rank", "total", "total_eps", "rtotal")}
        weighted = shared_p[:, 2 * COLS:].rearrange("q (k e d) -> q k e d", k=2, e=NE)
        mixed = s2[:, :].rearrange("q (u s d) -> q u s d", u=4, s=2)
        h6 = s2_shift[:, :].rearrange("q (n d) -> q n d", d=D)
        out_sb = k2[:, :].rearrange("q (n d) -> q n d", d=D)

        CONSTS = (1.0, EPS, EPS_RMS, EPS_RMS * EPS)

        def const(value):
            n = CONSTS.index(value)
            return consts[:, n:n + 1]

        def tiles(t):
            return t[:, :].rearrange("q (t d) -> q t d", d=D)

        def half(t, g):
            return t[:, g * HC:(g + 1) * HC]

        def vo_part(h2, p, g):
            return vo[HALF * h2:HALF * h2 + HALF, p, 4 * g:4 * g + 4, :, h2, 0:HD]

        def vo3_part(h2, p, g):
            return vo3[HALF * h2:HALF * h2 + HALF, p, 4 * g:4 * g + 4, :, h2, 0:FHD]

        TURNED_BANKS = ((1, 6), (5, 2))
        UP_BANKS = (6, 3, 0)
        DOWN_BANKS = (5, 2, 3, 4)
        LAST_BANK = 6
        ROUTE_FROM = 17
        LAST_TILES = (4, 2, 2)

        def n_before(group):
            return sum(LAST_TILES[:group])

        block = ctx.enter_context(nc.Block())

        @block.sync
        def _(sp):
            def load_x(k):
                ch, ph = k // 2, k % 2
                rows = x[:, ch].rearrange("b (i r) w -> b i (r w)", i=GRID)[:, :, ph * 1024:(ph + 1) * 1024]
                sp.dma_start(x_sb[:, k, :], rows).then_inc(sem(f"x_loaded{k}"), 16)

            load_x(0)
            sp.dma_start(a("ident"), pack_a[:, columns(PACK_A, "ident")]).then_inc(sem("ident_loaded"), 16)
            load_x(1)
            rest = slice(columns(PACK_A, "ident").stop, width(PACK_A))
            sp.dma_start(A[:, rest], pack_a[:, rest]).then_inc(sem("pack_a_loaded"), 16)
            for k in range(2, KCH):
                load_x(k)
            sp.dma_start(Bp[:, :], pack_b).then_inc(sem("pack_b_loaded"), 16)
            sp.dma_start(up_w[:, :], pack_d).then_inc(sem("up_w_loaded"), 16)
            sp.dma_start(Cp[:, :], pack_c).then_inc(sem("pack_c_loaded"), 16)
            sp.dma_start(down_w[:, :], pack_e).then_inc(sem("down_w_loaded"), 16)
            for first, last, groups in ((0, 4, 1), (4, 8, 3)):
                sp.wait_ge(sem("out_normed"), groups)
                rows = out.rearrange("(t p) n d -> t (p n) d", p=2)[first:last].rearrange("t q d -> q t d")
                sp.dma_start(rows, out_sb[:, first:last]).then_inc(sem("stored"), 16)
            sp.wait_ge(sem("stored"), 32)

        @block.tensor
        def _(pe):
            mm, tp = nc.tensor.matmul, nc.tensor.transpose
            ident = a("ident")

            def stay_awake(n, bank, cols=512):
                for _ in range(n):
                    mm(PS[:, bank, 0:cols], idle_bf[:, 0:P], idle_bf[:, 0:cols], start=True, stop=True)

            def conv_transposes(k):
                pe.wait_ge(sem("x_grouped"), k + 2 if k else 1)
                if k >= 2:
                    pe.wait_ge(sem("patches_copied_act"), k - 1)
                    pe.wait_ge(sem("patches_copied_dve"), k - 1)
                for j in range(GRID):
                    if k == 0 and j == 4:
                        pe.wait_ge(sem("x_grouped"), 2)
                    t = tp(PS[:, 2 * (k % 2) + j // 4, (j % 4) * P:(j % 4 + 1) * P], x_patches[:, k % 2, j * P:(j + 1) * P], ident)
                    if j % 4 == 3:
                        t.then_inc(sem("patches_turned"), 1)

            def conv_products(k):
                pe.wait_ge(sem("patches_copied_act"), k + 1)
                pe.wait_ge(sem("patches_copied_dve"), k + 1)
                if k == 0:
                    pe.wait_ge(sem("pack_a_loaded"), 16)
                w = a("conv")[:, k * D:(k + 1) * D]
                for q in range(2):
                    for jh in range(2):
                        first = (4 * jh + 2 * q) * P
                        m = mm(PS[HALF * jh:HALF * jh + HALF, 4 + q, 0:HC], w, patches[:, k % 2, first:first + 2 * P],
                               start=(k == 0), stop=(k == KCH - 1))
                    if (k, q) == (KCH - 1, 0):
                        m.then_inc(sem("first_conv_half"), 1)
                m.then_inc(sem("conv_summed"), 1)

            def ffn_up(name, src, u_banks, g):
                pe.wait_ge(sem(name + "_in"), g + 1)
                for m in range(2):
                    for s in range(2):
                        r = slice(HALF * s, HALF * s + HALF)
                        t = mm(PS[:, u_banks[g] + s, m * HC:(m + 1) * HC], b("ff1")[r, m * P:(m + 1) * P],
                               src[r, g * HC:(g + 1) * HC], start=True, stop=True)
                t.then_inc(sem(name + "_up"), 1)

            def ffn_down(name):
                for g in range(2):
                    for m in range(2):
                        pe.wait_ge(sem(name + "_gelu"), 2 * g + m + 1)
                        for s in range(2):
                            r = slice(HALF * s, HALF * s + HALF)
                            t = mm(PS[r, 6 + g, 0:HC], b("ff2")[:, m * D:(m + 1) * D],
                                   hidden[:, m, s, g * HC:(g + 1) * HC], start=(m == 0), stop=(m == 1))
                    t.then_inc(sem(name + "_down"), 1)

            def values(src, w, wide, bank, g):
                for u in (2 * g, 2 * g + 1):
                    at = (u % 2) * 2 * wide
                    t = mm(PS[:, bank, at:at + 2 * wide], src[:, u * P:(u + 1) * P], w, start=True, stop=True)
                return t

            pe.wait_ge(sem("idle_made"), 1)
            stay_awake(7, 7)
            pe.wait_ge(sem("ident_loaded"), 16)
            for k in range(KCH):
                conv_transposes(k)
                if k:
                    conv_products(k - 1)
            conv_products(KCH - 1)

            by_jh = PS[:, 6, :].rearrange("q (h j d) -> q h j d", h=2, j=4)
            for q in range(2):
                pe.wait_ge(sem(f"emb_ready{q}"), 1)
                for j4 in (2 * q, 2 * q + 1):
                    t = mm(by_jh[:, :, j4, :], emb[:, j4 * P:(j4 + 1) * P], a("centring"), start=True, stop=True)
            t.then_inc(sem("emb_centred"), 1)
            stay_awake(6, 7)
            for g in range(2):
                pe.wait_ge(sem("ln0_normed"), g + 1)
                for j in range(4 * g, 4 * g + 4):
                    for s in range(2):
                        r = slice(HALF * s, HALF * s + HALF)
                        t = mm(PS[r, 5, j * D:(j + 1) * D], normed[r, j * D:(j + 1) * D], ident[r, r],
                               start=True, stop=True)
            t.then_inc(sem("emb_turned"), 1)
            pe.wait_ge(sem("pack_b_loaded"), 16)
            mm(PS[:, 4, 0:1], b("proj"), b("bv"), start=True, stop=True).then_inc(sem("proj_bv"), 1)

            stay_awake(2, 7)
            for g in range(2):
                ffn_up("ffn1", h0, (0, 2), g)
            ffn_down("ffn1")

            for g in range(2):
                pe.wait_ge(sem("f1_ready"), g + 1)
                cols = slice(g * HC, (g + 1) * HC)
                mm(PS[:, 2 * g, 0:HC], b("wq"), f1[:, cols], start=True, stop=True).then_inc(sem("q1_mm"), 1)
                mm(PS[:, 2 * g + 1, 0:HC], b("wk"), f1[:, cols], start=True, stop=True).then_inc(sem("k1_mm"), 1)
                if g == 0:
                    pe.wait_ge(sem("proj_bias_made"), 1)
                values(f1, b("wv"), D, 4 + g, g).then_inc(sem("v1_mm"), 1)

            def scores1(w):
                if w % 4 == 0:
                    pe.wait_ge(sem("q1_act"), w // 4 + 1)
                    pe.wait_ge(sem("k1_act"), w // 4 + 1)
                    pe.wait_ge(sem("k1_dve"), 5 * (w // 4 + 1))
                if w >= 2:
                    pe.wait_ge(sem("att1_shifted"), w - 1)
                for s in range(2):
                    r = slice(HALF * s, HALF * s + HALF)
                    t = mm(PS[r, 6 + w % 2, :], qf[r, w * N:(w + 1) * N], k_heads[r, w].rearrange("q h n -> q (h n)"),
                           start=True, stop=True)
                t.then_inc(sem("att1_scores"), 1)

            def turn1(w):
                pe.wait_ge(sem("att1_shifted"), w + 1)
                if w >= 2:
                    pe.wait_ge(sem("att1_probs"), w - 1)
                for ch in range(4):
                    t = tp(PS[:, w % 2, ch * P:(ch + 1) * P], shifted[:, w % 2, ch * P:(ch + 1) * P], ident)
                t.then_inc(sem("att1_turned"), 1)

            def mix1(w):
                if w % 4 == 0:
                    pe.wait_ge(sem("v1_act"), w // 4 + 1)
                    pe.wait_ge(sem("v1_dve"), w // 4 + 1)
                pe.wait_ge(sem("att1_probs"), w + 1)
                wide = 2 * (HD + 1)
                for s in range(2):
                    r = slice(HALF * s, HALF * s + HALF)
                    for ch in range(4):
                        at = ((w % 4) * 4 + ch) * wide
                        t = mm(PS[r, 4 + w // 4, at:at + wide], probs[:, w % 2, ch * P + s * HALF:ch * P + (s + 1) * HALF],
                               vo[:, w % 2, (w // 2) * 2 + s, ch].rearrange("q e d -> q (e d)"), start=True, stop=True)
                t.then_inc(sem("att1_mixed"), 1)

            def mixed_to_features(name, bank, g):
                pe.wait_ge(sem(name + "_divided"), g + 1)
                for w in range(4 * g, 4 * g + 4):
                    for s in range(2):
                        r = slice(HALF * s, HALF * s + HALF)
                        t = mm(PS[r, bank, (w % 4) * N:(w % 4 + 1) * N], on[r, w, :], ident[r, r], start=True, stop=True)
                t.then_inc(sem(name + "_back"), 1)

            def project1(g):
                pe.wait_ge(sem("att1_ready"), g + 1)
                mm(PS[:, 2 + g, 0:HC], b("proj"), half(attended, g),
                   start=True, stop=True).then_inc(sem("proj_mm"), 1)

            pe.wait_ge(sem("vo_made"), 1)
            for w in range(W8):
                scores1(w)
                if w == 1:
                    stay_awake(2, 1)
                if w >= 1:
                    turn1(w - 1)
                if w >= 2:
                    mix1(w - 2)
            stay_awake(2, 6)
            turn1(W8 - 1)
            mix1(W8 - 2)
            mixed_to_features("att1", 0, 0)
            mix1(W8 - 1)
            project1(0)
            mixed_to_features("att1", 1, 1)
            stay_awake(1, 7)
            project1(1)
            ffn_up("ffn2", h2, (4, 0), 0)
            ffn_up("ffn2", h2, (4, 0), 1)
            ffn_down("ffn2")

            def turn2(g):
                pe.wait_ge(sem("att2_shifted"), g + 1)
                for u in (2 * g, 2 * g + 1):
                    t = tp(PS[:, 4 * g + 1, (u % 2) * P:(u % 2 + 1) * P], s2_shift[:, u * P:(u + 1) * P], ident)
                t.then_inc(sem("att2_turned"), 1)

            pe.wait_ge(sem("pack_c_loaded"), 16)
            for g in range(2):
                pe.wait_ge(sem("h3_ready"), g + 1)
                cols = slice(g * HC, (g + 1) * HC)
                mm(PS[:, 4 * g, 0:HC], c("aq"), h3[:, cols], start=True, stop=True).then_inc(sem("q2_mm"), 1)
                mm(PS[:, 4 * g + 1, 0:HC], c("ak"), h3[:, cols], start=True, stop=True).then_inc(sem("k2_mm"), 1)
            pe.wait_ge(sem("bias_made"), 1)
            for g in range(2):
                pe.wait_ge(sem("q2_act"), g + 1)
                mm(PS[:, 4 * g, 0:HC].rearrange("q (w n) -> q w n", n=N), ident, bias[:, :].unsqueeze(1).to_broadcast([P, 4, N]),
                   start=True, stop=True, skip_group_check=True)
                pe.wait_ge(sem("k2_dve"), g + 1)
                for w in range(4 * g, 4 * g + 4):
                    for s in range(2):
                        r = slice(HALF * s, HALF * s + HALF)
                        t = mm(PS[r, 4 * g, (w % 4) * N:(w % 4 + 1) * N], q2[r, w * N:(w + 1) * N],
                               k2[r, w * N:(w + 1) * N], start=False, stop=True, skip_group_check=True)
                t.then_inc(sem("att2_scores"), 1)
            turn2(0)
            pe.wait_ge(sem("v2_centred"), 2)
            for g in range(2):
                values(h3, c("av"), D, 4 * g + 2, g).then_inc(sem("v2_mm"), 1)
            turn2(1)
            for g in range(2):
                for u in (2 * g, 2 * g + 1):
                    t = mm(PS[:, 4 * g + 3, (u % 2) * P:(u % 2 + 1) * P], h3[:, u * P:(u + 1) * P], a("centring"),
                           start=True, stop=True)
                t.then_inc(sem("h3_turned"), 1)
            for g in range(2):
                pe.wait_ge(sem("v2_ready"), g + 1)
                pe.wait_ge(sem("att2_probs"), g + 1)
                for u in (2 * g, 2 * g + 1):
                    for s in range(2):
                        for p in range(2):
                            r = slice(HALF * p, HALF * p + HALF)
                            at = ((u % 2) * 2 + s) * (D + 1)
                            t = mm(PS[r, 4 * g + 2, at:at + D + 1], p2[r, u, s * HALF:(s + 1) * HALF],
                                   v2[r, 2 * u + s, :], start=True, stop=True)
                t.then_inc(sem("att2_mixed"), 1)

            stay_awake(15, 1)
            for g in range(2):
                pe.wait_ge(sem("h4n_ready"), g + 1)
                for u in (2 * g, 2 * g + 1):
                    t = tp(PS[:, 4 * g, (u % 2) * P:(u % 2 + 1) * P], h4n[:, u * P:(u + 1) * P], ident)
                t.then_inc(sem("h4_turned"), 1)
            for g in range(2):
                pe.wait_ge(sem("h4f_ready"), g + 1)
                cols = slice(g * HC, (g + 1) * HC)
                for n, name in enumerate(("fk", "fk_turned", "fq", "fq_turned")):
                    t = mm(PS[:, 1 + 4 * g + n // 2, (n % 2) * HC:(n % 2 + 1) * HC], c(name), h4f[:, cols],
                           start=True, stop=True)
                    if n % 2:
                        t.then_inc(sem("qk3_mm"), 1)

            def scores3(g, hg):
                if hg == 1:
                    pe.wait_ge(sem("q3_ready"), g + 1)
                if g == 0:
                    stay_awake(1, 4 * g + hg)
                mm(PS[:, 4 * g + hg, :], ident_bf[:, :], causal_bf[:, :], start=True, stop=True, skip_group_check=True)
                pe.wait_ge(sem("q3_ready"), g + 1)
                pe.wait_ge(sem("k3_ready"), g + 1)
                for w in range(4 * g, 4 * g + 4):
                    for s in range(2):
                        rows = slice(HALF * s + 32 * hg, HALF * s + 32 * hg + 32)
                        t = mm(PS[HALF * s:HALF * s + HALF, 4 * g + hg, (w % 4) * P:(w % 4 + 1) * P],
                               q3[rows, w * N:(w + 1) * N], k3_heads[rows, w].rearrange("q h n -> q (h n)"),
                               start=False, stop=True, skip_group_check=True)
                t.then_inc(sem("att3_scores"), 1)

            def turn3(i):
                if i >= 2:
                    pe.wait_ge(sem("att3_probs"), i - 1)
                pe.wait_ge(sem("att3_shifted"), i + 1)
                for n in range(4):
                    t = tp(PS[:, 2 + 4 * (i % 2), n * P:(n + 1) * P], shifted[:, i % 2, n * P:(n + 1) * P], ident)
                t.then_inc(sem("att3_turned"), 1)

            def mix3(i):
                g, ch = i // 2, i % 2
                if ch == 0:
                    pe.wait_ge(sem("v3_ready"), g + 1)
                pe.wait_ge(sem("att3_probs"), i + 1)
                wide = 2 * (FHD + 1)
                for w in range(4 * g, 4 * g + 4):
                    for s in range(2):
                        r = slice(HALF * s, HALF * s + HALF)
                        at = ((w % 4) * FKV + ch) * wide
                        t = mm(PS[r, 3 + 4 * g, at:at + wide],
                               probs[:, i % 2, (w % 4) * P + s * HALF:(w % 4) * P + (s + 1) * HALF],
                               vo3[:, w % 2, (w // 2) * 2 + s, ch].rearrange("q e d -> q (e d)"), start=True, stop=True)
                t.then_inc(sem("att3_mixed"), 1)

            def open3(g):
                mm(PS[:, 4 * g, 0:HC], ident, half(h4, g), start=True, stop=True, skip_group_check=True)

            pe.wait_ge(sem("causal_made"), 1)
            pe.wait_ge(sem("ident_bf_made"), 1)
            scores3(0, 0)
            scores3(0, 1)
            for g in range(2):
                values(h4f, c("fv"), FKV * FHD, 3 + 4 * g, g).then_inc(sem("v3_mm"), 1)
            turn3(0)
            scores3(1, 0)
            scores3(1, 1)
            turn3(1)
            mix3(0)
            open3(0)
            turn3(2)
            mix3(1)
            turn3(3)
            mix3(2)
            open3(1)
            mix3(3)
            mixed_to_features("att3", 2, 0)
            stay_awake(1, 3)
            mixed_to_features("att3", 6, 1)
            for g in range(2):
                pe.wait_ge(sem("att3_ready"), g + 1)
                for u in (2 * g, 2 * g + 1):
                    t = mm(PS[:, 4 * g, (u % 2) * P:(u % 2 + 1) * P], attended3[:, u * P:(u + 1) * P], c("fo"),
                           start=False, stop=True, skip_group_check=True)
                t.then_inc(sem("fo_mm"), 1)
                if g == 0:
                    stay_awake(1, 3)

            stay_awake(10, 3)
            for g in range(2):
                pe.wait_ge(sem("parts_ready"), g + 1)
                for s in range(2):
                    for u in (2 * g, 2 * g + 1):
                        t = tp(PS[:, TURNED_BANKS[s][g], (u % 2) * P:(u % 2 + 1) * P], parts[:, 2 * u + s].rearrange("q l d -> q (l d)"), ident)
                t.then_inc(sem("parts_turned"), 1)

            def router_products():
                pe.wait_ge(sem("router_made"), 1)
                for t8 in range(8):
                    u, s = t8 // 2, t8 % 2
                    t = mm(PS[:, 2, t8 * 2 * NE:(t8 + 1) * 2 * NE], xf[:, s, u * P:(u + 1) * P],
                           router_parts[:, :, :].rearrange("q l e -> q (l e)"), start=True, stop=True)
                t.then_inc(sem("logits_mm"), 1)

            pe.wait_ge(sem("xf_ready0"), 2)
            pe.wait_ge(sem("up_split"), 1)
            for s in range(2):
                for ch in range(CH):
                    n = s * CH + ch
                    if n == 1:
                        pe.wait_ge(sem("h45_ready"), 2)
                    if n >= UPBUF:
                        pe.wait_ge(sem("hh_ready"), n - UPBUF + 1)
                    for v in range(2):
                        at = (2 * ch + v) * P
                        mm(PS[:, UP_BANKS[n % UPBUF] + v, :], up_hi[:, at:at + P], xf[:, s, :], start=True, stop=False)
                        t = mm(PS[:, UP_BANKS[n % UPBUF] + v, :], up_lo[:, at:at + P], xf[:, s, :], start=False, stop=True)
                        t.then_inc(sem("up_mm"), 1)
                    if n == 1:
                        pe.wait_ge(sem("xf_ready1"), 2)
                        router_products()
            pe.wait_ge(sem("down_centred"), 1)
            for n in range(8):
                s, u = n // 4, n % 4
                if n % 4 == 0:
                    pe.wait_ge(sem("hh_ready"), CH * (s + 1))
                if n == 1:
                    pe.wait_ge(sem("logits_read"), 1)
                if n == 2:
                    pe.wait_ge(sem("hh_ready"), 2 * CH)
                if n >= 4:
                    pe.wait_ge(sem("tile_weighted"), n - 3)
                bank = DOWN_BANKS[n % 4]
                tok = slice(u * P, (u + 1) * P)
                for ch in range(CH):
                    groups = [experts_of(ch)]
                    if n == 7 and 3 in groups[0] and 4 in groups[0]:
                        groups = [range(3, 4), range(4, 5)]
                    for ex in groups:
                        last_half = n == 7 and ex[0] >= 4
                        if n == 7 and ex[0] == 4 and len(groups) == 2:
                            t.then_inc(sem("down_mm"), 1)
                        first = DOWN_AT[ch] + (ex[0] - experts_of(ch)[0]) * D
                        for r in (slice(0, HALF), slice(HALF, P)) if len(ex) == 1 else (slice(0, P),):
                            t = mm(PS[r, LAST_BANK if last_half else bank, ex[0] * D:(ex[-1] + 1) * D],
                                   hh[:, ch, s, u * P + r.start:u * P + r.stop],
                                   down_w[:, first:first + len(ex) * D], start=(ch == 0 or (last_half and len(groups) == 2)),
                                   stop=(ch == CH - 1), skip_group_check=True)
                t.then_inc(sem("down_mm"), 1)

        @block.scalar
        def _(act):
            f = nc.scalar.activation

            for k in range(KCH):
                act.wait_ge(sem("patches_turned"), 2 * k + 1)
                if k >= 2:
                    act.wait_ge(sem("conv_summed"), k - 1)
                f(patches[:, k % 2, 0:512], PS[:, 2 * (k % 2), :], ACT.Copy).then_inc(sem("patches_copied_act"), 1)

            def bring_table(func):
                f(table_use[:, :], const(1.0), func)

            def roots(name, dst, factor, eps):
                for g in range(2):
                    act.wait_ge(sem(name + "_sq_sum"), g + 1)
                    f(dst[:, 4 * g:4 * g + 4], sq_sums[:, 4 * g:4 * g + 4], ACT.Sqrt, scale=factor, bias=const(eps))\
                        .then_inc(sem(name + "_std"), 1)

            def squares_of(name, ready, count, src):
                for g in range(2):
                    act.wait_ge(sem(ready), count[g])
                    f(half(squares, g), half(src, g), ACT.Square).then_inc(sem(name + "_squared"), 1)

            def gelus(name, u_banks):
                for g in range(2):
                    act.wait_ge(sem(name + "_up"), g + 1)
                    for m in range(2):
                        f(hidden[:, m, :, g * HC:(g + 1) * HC],
                          PS[:, u_banks[g]:u_banks[g] + 2, m * HC:(m + 1) * HC],
                          ACT.Gelu_apprx_tanh, bias=b("ff1_b")[:, m:m + 1]).then_inc(sem(name + "_gelu"), 1)

            act.wait_ge(sem("consts_made"), 1)
            bring_table(ACT.Sqrt)
            act.wait_ge(sem("pack_a_loaded"), 16)
            act.wait_ge(sem("first_conv_half"), 1)
            f(half(emb, 0), PS[:, 4, 0:HC], ACT.Identity, bias=a("conv_b")).then_inc(sem("emb_ready0"), 1)
            squares_of("ln0", "emb_centred", (1, 1), PS[:, 6, :])
            roots("ln0", std, 1.0 / D, EPS)
            bring_table(ACT.Gelu_apprx_tanh)
            act.wait_ge(sem("pack_b_loaded"), 16)
            gelus("ffn1", (0, 2))
            for g in range(2):
                act.wait_ge(sem("ffn1_down"), g + 1)
                f(half(f1, g), PS[:, 6 + g, 0:HC], ACT.Identity, bias=b("ff2_b")).then_inc(sem("f1_ready"), 1)

            def queries1(g):
                act.wait_ge(sem("q1_mm"), g + 1)
                f(half(qf, g), PS[:, 2 * g, 0:HC], ACT.Identity, bias=b("bq")).then_inc(sem("q1_act"), 1)

            def last_heads1(g):
                act.wait_ge(sem("kf_ready"), g + 1)
                for h in range(5, 8):
                    t = f(k_heads[:, 4 * g:4 * g + 4, h, :], half(kf, g).rearrange("q (w n) -> q w n", n=N), ACT.Copy,
                          scale=b("head_mask")[:, h:h + 1])
                t.then_inc(sem("k1_act"), 1)

            def values1(g):
                act.wait_ge(sem("v1_mm"), g + 1)
                src = PS[HALF:P, 4 + g, 0:HC].rearrange("q (t c e d) -> q t c e d", t=4, c=4, e=2)
                for h2_ in range(2):
                    t = f(vo_part(h2_, 1, g), src[:, :, :, h2_, :], ACT.Copy)
                t.then_inc(sem("v1_act"), 1)

            queries1(0)
            last_heads1(0)
            act.wait_ge(sem("vo_made"), 1)
            values1(0)
            bring_table(ACT.Exp)
            scale1 = float(HD) ** -0.5
            between = [queries1, last_heads1, values1]
            for w in range(W8):
                act.wait_ge(sem("att1_turned"), w + 1)
                if w >= 2:
                    act.wait_ge(sem("att1_mixed"), w - 1)
                f(probs[:, w % 2, :], PS[:, w % 2, :], ACT.Exp, scale=scale1).then_inc(sem("att1_probs"), 1)
                if w < len(between):
                    between[w](1)

            for g in range(2):
                act.wait_ge(sem("att1_back"), g + 1)
                f(half(attended, g), PS[:, g, 0:HC], ACT.Copy).then_inc(sem("att1_ready"), 1)
            gelus("ffn2", (4, 0))

            act.wait_ge(sem("bias_made"), 1)
            for g in range(2):
                act.wait_ge(sem("q2_mm"), g + 1)
                f(half(q2, g), PS[:, 4 * g, 0:HC], ACT.Identity, scale=float(D) ** -0.5, bias=q2_bias[:, :])\
                    .then_inc(sem("q2_act"), 1)
            for g in range(2):
                act.wait_ge(sem("att2_turned"), g + 1)
                f(p2[:, 2 * g:2 * g + 2, :], PS[:, 4 * g + 1, 0:HC].rearrange("q (u n) -> q u n", n=P),
                  ACT.Exp).then_inc(sem("att2_probs"), 1)

            bring_table(ACT.Sqrt)
            squares_of("ln1", "ln1_in", (1, 2), sum2)
            for g in range(2):
                at = slice(4 * g, 4 * g + 4)
                act.wait_ge(sem("ln1_sq_sum"), g + 1)
                f(std_rms[:, at], sq_sums[:, at], ACT.Sqrt, scale=(1.0 + EPS_RMS) / D, bias=const(EPS_RMS * EPS))\
                    .then_inc(sem("rms1_std"), 1)
            roots("ln1", std, 1.0 / D, EPS)

            for g in range(2):
                act.wait_ge(sem("h4_turned"), g + 1)
                f(half(h4f, g), PS[:, 4 * g, 0:HC], ACT.Copy, scale=c("ln1")).then_inc(sem("h4f_ready"), 1)
            bring_table(ACT.Exp)
            for g in range(2):
                act.wait_ge(sem("kr_ready"), g + 1)
                for h in range(2):
                    t = f(k3_heads[:, 4 * g:4 * g + 4, h, :], half(kr, g).rearrange("q (w n) -> q w n", n=N),
                          ACT.Copy, scale=c("fhead_mask")[:, h:h + 1])
                t.then_inc(sem("k3_ready"), 1)
            act.wait_ge(sem("vo3_made"), 1)
            for g in range(2):
                act.wait_ge(sem("v3_mm"), g + 1)
                for h2_ in range(2):
                    for p in range(2):
                        src = PS[HALF * p:HALF * (p + 1), 3 + 4 * g, 0:P].rearrange(
                            "q (t c d) -> q t c d", t=4, c=FKV)
                        t = f(vo3_part(h2_, p, g), src, ACT.Copy)
                t.then_inc(sem("v3_ready"), 1)
            scale3 = float(FHD) ** -0.5
            for i in range(4):
                act.wait_ge(sem("att3_turned"), i + 1)
                if i >= 2:
                    act.wait_ge(sem("att3_mixed"), i - 1)
                f(probs[:, i % 2, :], PS[:, 2 + 4 * (i % 2), :], ACT.Exp, scale=scale3).then_inc(sem("att3_probs"), 1)

            bring_table(ACT.Sqrt)
            for g in range(2):
                act.wait_ge(sem("att3_back"), g + 1)
                f(half(attended3, g), PS[:, 2 + 4 * g, 0:HC], ACT.Copy).then_inc(sem("att3_ready"), 1)
            for g in range(2):
                act.wait_ge(sem("fo_mm"), g + 1)
                f(half(squares, g), PS[:, 4 * g, 0:HC], ACT.Square).then_inc(sem("rms2_squared"), 1)
            roots("rms2", std, 1.0 / D, EPS_RMS)
            for g in range(2):
                act.wait_ge(sem("rms2_normed"), g + 1)
                f(parts[:, 4 * g:4 * g + 4, 0, :].bitcast(F32R), tiles(h5n)[:, 4 * g:4 * g + 4], ACT.Copy)\
                    .then_inc(sem("high_ready"), 1)
            bring_table(ACT.Silu)
            for g in range(2):
                act.wait_ge(sem("parts_turned"), g + 1)
                f(half(xf[:, 1], g), PS[:, TURNED_BANKS[1][g], 0:HC], ACT.Copy).then_inc(sem("xf_ready1"), 1)
            for n in range(2 * CH):
                act.wait_ge(sem("up_mm"), 2 * n + 1)
                if n >= UPBUF:
                    act.wait_ge(sem("hh_ready"), n - UPBUF + 1)
                f(gate[:, n % UPBUF, :], PS[:, UP_BANKS[n % UPBUF], :], ACT.Silu).then_inc(sem("gated"), 1)

            bring_table(ACT.Sqrt)
            for n in range(len(LAST_TILES)):
                at = slice(n_before(n), n_before(n + 1))
                act.wait_ge(sem("lnf_sq_sum"), n + 1)
                f(std[:, at], sq_sums[:, at], ACT.Sqrt, scale=1.0 / D, bias=const(EPS)).then_inc(sem("lnf_std"), 1)

        @block.gpsimd
        def _(pool):
            g_ = nc.gpsimd
            g_.memset(idle_bf[:, :], 0.0).then_inc(sem("idle_made"), 1)
            for n, value in enumerate(CONSTS):
                t = g_.memset(consts[:, n:n + 1], value)
            t.then_inc(sem("consts_made"), 1)
            g_.memset(v2[:, :, D:D + 1], 1.0)
            g_.memset(euler[:, :, :], math.e).then_inc(sem("euler_made"), 1)
            g_.memset(vo[:, :, :, :, :, :], 0.0).then_inc(sem("vo_zero"), 1)
            for h2_ in range(2):
                pool.wait_ge(sem("vo_zero"), h2_ + 1)
                g_.memset(vo[HALF * h2_:HALF * h2_ + HALF, :, :, :, h2_, HD:HD + 1], 1.0).then_inc(sem("vo_zero"), 1)
            pool.wait_ge(sem("vo_zero"), 3)
            g_.memset(spare[:, 0:1], 0.0).then_inc(sem("vo_made"), 1)

            g_.memset(vo3[:, :, :, :, :, :], 0.0).then_inc(sem("vo3_zero"), 1)
            for h2_ in range(2):
                pool.wait_ge(sem("vo3_zero"), h2_ + 1)
                g_.memset(vo3[HALF * h2_:HALF * h2_ + HALF, :, :, :, h2_, FHD:FHD + 1], 1.0).then_inc(sem("vo3_zero"), 1)
            pool.wait_ge(sem("vo3_zero"), 3)
            g_.memset(spare[:, 0:1], 0.0).then_inc(sem("vo3_made"), 1)

            pool.wait_ge(sem("pack_c_loaded"), 16)
            g_.tensor_scalar(router_s[:, :], c("router"), c("ln2"), None, ALU.mult).then_inc(sem("router_s"), 1)
            pool.wait_ge(sem("router_s"), 1)
            g_.tensor_copy(router_parts[:, 0], router_s[:, :]).then_inc(sem("router_h"), 1)
            pool.wait_ge(sem("router_h"), 1)
            g_.tensor_tensor(router_parts[:, 1], router_s[:, :], router_parts[:, 0].bitcast(F32),
                             ALU.subtract).then_inc(sem("router_made"), 1)
            g_.tensor_copy(causal_bf[:, :].rearrange("q (t n) -> q t n", t=4),
                           c("causal").unsqueeze(1).to_broadcast([P, 4, 2 * N])).then_inc(sem("causal_made"), 1)
            g_.tensor_copy(ident_bf[:, :], a("ident")).then_inc(sem("ident_bf_made"), 1)
            pool.wait_ge(sem("up_w_loaded"), 16)
            g_.tensor_scalar(up_w[:, :], up_w[:, :], c("ln2"), None, ALU.mult).then_inc(sem("up_scaled"), 1)
            pool.wait_ge(sem("up_scaled"), 1)
            g_.tensor_copy(up_hi[:, :], up_w[:, :]).then_inc(sem("up_h"), 1)
            pool.wait_ge(sem("up_h"), 1)
            g_.tensor_tensor(up_lo[:, :], up_w[:, :], up_hi[:, :].bitcast(F32), ALU.subtract).then_inc(sem("up_split"), 1)

            for g in range(2):
                pool.wait_ge(sem("rope_q"), g + 1)
                g_.tensor_tensor(half(q3, g), half(rope[:, 2], g), half(rope[:, 3], g), ALU.add).then_inc(sem("q3_ready"), 1)
            pool.wait_ge(sem("euler_made"), 1)
            pool.wait_ge(sem("logits_read"), 1)
            g_.tensor_tensor(small["exp"][:, :, :], euler[:, :, :], small["shift"][:, :, :], ALU.pow).then_inc(sem("router_exp"), 1)

        @block.vector
        def _(ve):
            v = nc.vector

            def block_sums(name, w, n):
                v.reduce_sum(means[:, 0:n], w.rearrange("q (n d) -> q n d", d=D), AX).then_inc(sem(name + "_sum"), 1)

            def less_means(name, w, n):
                blocks = w.rearrange("q (n d) -> q n d", d=D)
                ve.wait_ge(sem(name + "_sum"), 1)
                return v.scalar_tensor_tensor(out=blocks, in0=means[:, 0:n].unsqueeze(2).to_broadcast([P, n, D]),
                                              scalar=-1.0 / D, in1=blocks, op0=ALU.mult, op1=ALU.add)

            def centre(name, w, n):
                block_sums(name, w, n)
                return less_means(name, w, n)

            def sum_squares(name, g):
                ve.wait_ge(sem(name + "_squared"), g + 1)
                v.reduce_sum(sq_sums[:, 4 * g:4 * g + 4], tiles(squares)[:, 4 * g:4 * g + 4], AX)\
                    .then_inc(sem(name + "_sq_sum"), 1)

            def invert(name, g, dst, src):
                ts = slice(4 * g, 4 * g + 4)
                ve.wait_ge(sem(name + "_std"), g + 1)
                v.reciprocal(dst[:, ts], src[:, ts]).then_inc(sem(name + "_rstd"), 1)

            def scale(name, g, dst, src, by):
                ts = slice(4 * g, 4 * g + 4)
                ve.wait_ge(sem(name + "_rstd"), g + 1)
                return v.tensor_tensor(tiles(dst)[:, ts], tiles(src)[:, ts], by[:, ts].unsqueeze(2).to_broadcast([P, 4, D]),
                                       ALU.mult)

            def group(k):
                ve.wait_ge(sem(f"x_loaded{k}"), 16)
                if k >= 2:
                    ve.wait_ge(sem("patches_turned"), 2 * k - 2)
                for js in (slice(0, 4), slice(4, 8)) if k == 0 else (slice(0, 8),):
                    v.tensor_copy(x_patches[:, k % 2, :].rearrange("q (j r w) -> q j r w", j=GRID, r=8)[:, js],
                                  x_sb[:, k, :].rearrange("q (r j w) -> q j r w", r=8, j=GRID)[:, js])\
                        .then_inc(sem("x_grouped"), 1)

            group(0)
            for k in range(KCH):
                if k + 1 < KCH:
                    group(k + 1)
                ve.wait_ge(sem("patches_turned"), 2 * k + 2)
                if k >= 2:
                    ve.wait_ge(sem("conv_summed"), k - 1)
                v.tensor_copy(patches[:, k % 2, 512:1024], PS[:, 2 * (k % 2) + 1, :]).then_inc(sem("patches_copied_dve"), 1)

            ve.wait_ge(sem("pack_a_loaded"), 16)
            ve.wait_ge(sem("conv_summed"), KCH)
            v.tensor_scalar(half(emb, 1), PS[:, 5, 0:HC], a("conv_b"), None, ALU.add).then_inc(sem("emb_ready1"), 1)
            v.tensor_scalar(pos_b[:, :], a("pos"), a("ln_b"), None, ALU.add).then_inc(sem("pos_b_made"), 1)
            for g in range(2):
                sum_squares("ln0", g)
            for g in range(2):
                invert("ln0", g, rstd, std)
                scale("ln0", g, normed, PS[:, 6, :], rstd).then_inc(sem("ln0_normed"), 1)
            ve.wait_ge(sem("emb_turned"), 1)
            ve.wait_ge(sem("pos_b_made"), 1)
            turned = PS[:, 5, :].rearrange("q (j w i) -> q w i j", j=GRID, w=W8)
            grid = pos_b[:, :].rearrange("q (i j) -> q i j", j=GRID).unsqueeze(1).to_broadcast([P, W8 // 2, GRID, GRID])
            for g in range(2):
                v.scalar_tensor_tensor(out=half(h0, g).rearrange("q (w i j) -> q w i j", i=GRID, j=GRID),
                                       in0=turned[:, 4 * g:4 * g + 4], scalar=a("ln_w"), in1=grid,
                                       op0=ALU.mult, op1=ALU.add).then_inc(sem("ffn1_in"), 1)
            ve.wait_ge(sem("pack_b_loaded"), 16)
            ve.wait_ge(sem("proj_bv"), 1)
            v.tensor_tensor(proj_bias[:, :], PS[:, 4, 0:1], b("bp"), ALU.add).then_inc(sem("proj_bias_made"), 1)
            ve.wait_ge(sem("pack_c_loaded"), 16)
            centre("av", c("av"), 2).then_inc(sem("v2_centred"), 1)
            ve.wait_ge(sem("v2_centred"), 1)
            centre("abv", c("abv"), 1).then_inc(sem("v2_centred"), 1)
            ve.wait_ge(sem("v2_centred"), 2)
            ve.wait_ge(sem("down_w_loaded"), 16)
            centre("down", down_w[:, :], DOWN_AT[CH] // D).then_inc(sem("down_centred"), 1)
            v.tensor_scalar(q2_bias[:, :], c("abq"), float(D) ** -0.5, None, ALU.mult)
            v.tensor_scalar(bias[:, :], c("cosines")[:, N:2 * N], c("beta")[:, 1:2], None, ALU.mult).then_inc(sem("bias_part"), 1)
            ve.wait_ge(sem("bias_part"), 1)
            v.scalar_tensor_tensor(out=bias[:, :], in0=c("cosines")[:, 0:N], scalar=c("beta")[:, 0:1], in1=bias[:, :],
                                   op0=ALU.mult, op1=ALU.add).then_inc(sem("bias_made"), 1)

            def keys1(g):
                ve.wait_ge(sem("k1_mm"), g + 1)
                v.tensor_scalar(half(kf, g), PS[:, 2 * g + 1, 0:HC], b("bk"), None, ALU.add).then_inc(sem("kf_ready"), 1)

            def first_heads1(g, heads):
                ve.wait_ge(sem("kf_ready"), g + 1)
                for h in heads:
                    t = v.tensor_scalar(k_heads[:, 4 * g:4 * g + 4, h, :], half(kf, g).rearrange("q (w n) -> q w n", n=N),
                                        b("head_mask")[:, h:h + 1], None, ALU.mult)
                t.then_inc(sem("k1_dve"), len(heads))

            def values1(g):
                ve.wait_ge(sem("v1_mm"), g + 1)
                src = PS[0:HALF, 4 + g, 0:HC].rearrange("q (t c e d) -> q t c e d", t=4, c=4, e=2)
                for h2_ in range(2):
                    t = v.tensor_copy(vo_part(h2_, 0, g), src[:, :, :, h2_, :])
                t.then_inc(sem("v1_dve"), 1)

            keys1(0)
            first_heads1(0, range(5))
            ve.wait_ge(sem("vo_made"), 1)
            values1(0)
            keys1(1)

            def shift(name, rows, n):
                ve.wait_ge(sem(name + "_scores"), n + 1)
                if n >= 2:
                    ve.wait_ge(sem(name + "_turned"), n - 1)
                tops = top[:, n % 2, :].rearrange("q (b h) -> q b h", b=2)
                v.reduce_max(tops, rows, AX).then_inc(sem(name + "_top"), 1)
                ve.wait_ge(sem(name + "_top"), n + 1)
                v.tensor_tensor(shifted[:, n % 2, :].rearrange("q (b h n) -> q b h n", b=2, n=N), rows,
                                tops.unsqueeze(3).to_broadcast([P, 2, 4, N]), ALU.subtract)\
                    .then_inc(sem(name + "_shifted"), 1)

            def divide(name, bank, g, heads, size):
                ve.wait_ge(sem(name + "_mixed"), (4 if name == "att1" else 2) * (g + 1))
                mix = PS[:, bank, 0:4 * heads * (size + 1)].rearrange("q (w h d) -> q w h d", w=4, h=heads)
                rec = r1[:, 4 * g:4 * g + 4, 0:heads]
                v.reciprocal(rec, mix[:, :, :, size]).then_inc(sem(name + "_recip"), 1)
                ve.wait_ge(sem(name + "_recip"), g + 1)
                v.tensor_tensor(on[:, 4 * g:4 * g + 4, :].rearrange("q w (h d) -> q w h d", h=heads), mix[:, :, :, 0:size],
                                rec.unsqueeze(3).to_broadcast([P, 4, heads, size]), ALU.mult)\
                    .then_inc(sem(name + "_divided"), 1)

            for w in range(W8):
                shift("att1", PS[:, 6 + w % 2, :].rearrange("q (b h n) -> q b h n", b=2, n=N), w)
                if w in (0, 1, 2):
                    first_heads1(1, (range(2), range(2, 4), range(4, 5))[w])
                if w == 3:
                    values1(1)
                if w == 6:
                    divide("att1", 4, 0, HEADS, HD)
            divide("att1", 5, 1, HEADS, HD)

            ve.wait_ge(sem("proj_bias_made"), 1)
            for g in range(2):
                ve.wait_ge(sem("proj_mm"), g + 1)
                v.scalar_tensor_tensor(out=half(h2, g), in0=PS[:, 2 + g, 0:HC], scalar=proj_bias[:, 0:1],
                                       in1=half(h0, g), op0=ALU.add, op1=ALU.add).then_inc(sem("ffn2_in"), 1)
            for g in range(2):
                ve.wait_ge(sem("ffn2_down"), g + 1)
                v.scalar_tensor_tensor(out=half(h3, g), in0=PS[:, 6 + g, 0:HC], scalar=b("ff2_b"),
                                       in1=half(h2, g), op0=ALU.add, op1=ALU.add).then_inc(sem("h3_ready"), 1)

            for g in range(2):
                ve.wait_ge(sem("k2_mm"), g + 1)
                v.tensor_scalar(half(k2, g), PS[:, 4 * g + 1, 0:HC], c("abk"), None, ALU.add).then_inc(sem("k2_dve"), 1)
            for g in range(2):
                ts = slice(4 * g, 4 * g + 4)
                rows = PS[:, 4 * g, 0:HC].rearrange("q (w n) -> q w n", n=N)
                ve.wait_ge(sem("att2_scores"), g + 1)
                v.reduce_max(s2_top[:, ts], rows, AX).then_inc(sem("att2_top"), 1)
                ve.wait_ge(sem("att2_top"), g + 1)
                v.tensor_tensor(tiles(s2_shift)[:, ts], rows, s2_top[:, ts].unsqueeze(2).to_broadcast([P, 4, N]),
                                ALU.subtract).then_inc(sem("att2_shifted"), 1)
            for g in range(2):
                ve.wait_ge(sem("v2_mm"), g + 1)
                v.tensor_tensor(v2[:, 4 * g:4 * g + 4, 0:D], PS[:, 4 * g + 2, 0:HC].rearrange("q (t d) -> q t d", d=D),
                                c("abv").unsqueeze(1).to_broadcast([P, 4, D]), ALU.add).then_inc(sem("v2_ready"), 1)
            for g in range(2):
                mixed2 = PS[:, 4 * g + 2, 0:4 * (D + 1)].rearrange("q (t d) -> q t d", d=D + 1)
                ve.wait_ge(sem("att2_mixed"), g + 1)
                v.reciprocal(r2[:, 4 * g:4 * g + 4], mixed2[:, :, D]).then_inc(sem("att2_recip"), 1)
            for g in range(2):
                ts = slice(4 * g, 4 * g + 4)
                mixed2 = PS[:, 4 * g + 2, 0:4 * (D + 1)].rearrange("q (t d) -> q t d", d=D + 1)
                ve.wait_ge(sem("att2_recip"), g + 1)
                v.tensor_tensor(tiles(o2)[:, ts], mixed2[:, :, 0:D], r2[:, ts].unsqueeze(2).to_broadcast([P, 4, D]),
                                ALU.mult).then_inc(sem("o2_ready"), 1)
            for g in range(2):
                ve.wait_ge(sem("h3_turned"), g + 1)
                ve.wait_ge(sem("o2_ready"), g + 1)
                v.tensor_tensor(half(sum2, g), PS[:, 4 * g + 3, 0:HC], half(o2, g), ALU.add).then_inc(sem("ln1_in"), 1)
            for g in range(2):
                sum_squares("ln1", g)
            for g in range(2):
                invert("rms1", g, rstd_rms, std_rms)
                scale("rms1", g, h4n, sum2, rstd_rms).then_inc(sem("h4n_ready"), 1)
            for g in range(2):
                invert("ln1", g, rstd, std)
            for g in range(2):
                scale("ln1", g, h4, sum2, rstd)
            cos = c("rope_cos").unsqueeze(1).to_broadcast([P, 4, N])
            sin = c("rope_sin").unsqueeze(1).to_broadcast([P, 4, N])
            for g in range(2):
                cols = slice(g * HC, (g + 1) * HC)
                for n in range(4):
                    ve.wait_ge(sem("qk3_mm"), 2 * g + n // 2 + 1)
                    t = v.tensor_tensor(rope[:, n, cols].rearrange("q (w n) -> q w n", n=N),
                                        PS[:, 1 + 4 * g + n // 2, (n % 2) * HC:(n % 2 + 1) * HC].rearrange(
                                            "q (w n) -> q w n", n=N),
                                        sin if n % 2 else cos, ALU.mult)
                    if n == 1:
                        t.then_inc(sem("rope_k"), 1)
                        ve.wait_ge(sem("rope_k"), g + 1)
                        v.tensor_tensor(half(kr, g), rope[:, 0, cols], rope[:, 1, cols], ALU.add).then_inc(sem("kr_ready"), 1)
                t.then_inc(sem("rope_q"), 1)
            for i in range(4):
                g, hg = i // 2, i % 2
                shift("att3", PS[:, 4 * g + hg, :].rearrange("q (b h n) -> q b h n", b=2, n=N), i)
            divide("att3", 3, 0, FH, FHD)
            divide("att3", 7, 1, FH, FHD)
            for g in range(2):
                sum_squares("rms2", g)

            def normalised(g):
                invert("rms2", g, rstd, std)
                ts = slice(4 * g, 4 * g + 4)
                ve.wait_ge(sem("rms2_rstd"), g + 1)
                v.tensor_tensor(tiles(h5n)[:, ts], PS[:, 4 * g, 0:HC].rearrange("q (t d) -> q t d", d=D),
                                rstd[:, ts].unsqueeze(2).to_broadcast([P, 4, D]), ALU.mult).then_inc(sem("rms2_normed"), 1)

            def low_part(g):
                ts = slice(4 * g, 4 * g + 4)
                ve.wait_ge(sem("high_ready"), g + 1)
                v.tensor_tensor(parts[:, ts, 1, :], tiles(h5n)[:, ts], parts[:, ts, 0, :], ALU.subtract)\
                    .then_inc(sem("parts_ready"), 1)

            normalised(0)
            normalised(1)
            low_part(0)
            low_part(1)
            for g in range(2):
                ve.wait_ge(sem("parts_turned"), g + 1)
                v.tensor_copy(half(xf[:, 0], g), PS[:, TURNED_BANKS[0][g], 0:HC]).then_inc(sem("xf_ready0"), 1)
            for g in range(2):
                v.tensor_tensor(half(h45, g), PS[:, 4 * g, 0:HC], half(h4, g), ALU.add).then_inc(sem("h45_ready"), 1)

            def spread(name):
                return few[name][:, :].unsqueeze(2).to_broadcast([P, 8, NE])

            rank = c("rank").unsqueeze(1).to_broadcast([P, 8, NE])
            logit_parts = PS[:, 2, 0:16 * NE].rearrange("q (t l e) -> q t l e", l=2, e=NE)
            logits = small["logits"][:, :, :]
            routed = sem("router_step")

            def top_of(dst, src):
                return lambda: v.reduce_max(few[dst][:, :], small[src][:, :, :], AX)

            def pair(dst, x0, x1, op):
                return lambda: v.tensor_tensor(small[dst][:, :, :], small[x0][:, :, :], x1, op)

            def few_pair(dst, x0, x1, op):
                return lambda: v.tensor_tensor(few[dst][:, :], few[x0][:, :], few[x1][:, :], op)

            router_steps = [
                lambda: v.reduce_sum(few["sum"][:, :], small["exp"][:, :, :], AX),
                lambda: v.reciprocal(few["rsum"][:, :], few["sum"][:, :]),
                pair("prob", "exp", spread("rsum"), ALU.mult),
                top_of("first", "prob"),
                pair("same1", "prob", spread("first"), ALU.is_equal),
                pair("rank1", "same1", rank, ALU.mult),
                top_of("first_rank", "rank1"),
                pair("one1", "rank1", spread("first_rank"), ALU.is_equal),
                lambda: v.scalar_tensor_tensor(out=small["prob2"][:, :, :], in0=small["one1"][:, :, :], scalar=-2.0,
                                               in1=small["prob"][:, :, :], op0=ALU.mult, op1=ALU.add),
                top_of("second", "prob2"),
                pair("same2", "prob2", spread("second"), ALU.is_equal),
                pair("rank2", "same2", rank, ALU.mult),
                top_of("second_rank", "rank2"),
                pair("one2", "rank2", spread("second_rank"), ALU.is_equal),
                pair("part1", "one1", spread("first"), ALU.mult),
                pair("part2", "one2", spread("second"), ALU.mult),
                pair("both", "part1", small["part2"][:, :, :], ALU.add),
                few_pair("total", "first", "second", ALU.add),
                lambda: v.tensor_scalar(few["total_eps"][:, :], few["total"][:, :], 1e-9, None, ALU.add),
                lambda: v.reciprocal(few["rtotal"][:, :], few["total_eps"][:, :]),
                pair("weights", "both", spread("rtotal"), ALU.mult),
            ]

            def route(first, last):
                for n in range(first, last):
                    if n == 0:
                        ve.wait_ge(sem("router_exp"), 1)
                    else:
                        ve.wait_ge(routed, n + 1)
                    router_steps[n]().then_inc(routed, 1)

            for n in range(2 * CH):
                s, ch = n // CH, n % CH
                ve.wait_ge(sem("gated"), n + 1)
                ve.wait_ge(sem("up_mm"), 2 * n + 2)
                v.tensor_tensor(hh[:, ch, s, :], PS[:, UP_BANKS[n % UPBUF] + 1, :], gate[:, n % UPBUF, :], ALU.mult)\
                    .then_inc(sem("hh_ready"), 1)
                if n == 2:
                    ve.wait_ge(sem("logits_mm"), 1)
                    v.tensor_copy(small["low"][:, :, :], logit_parts[:, :, 1]).then_inc(sem("logits_step"), 1)
                    ve.wait_ge(sem("logits_step"), 1)
                    v.tensor_tensor(logits, logit_parts[:, :, 0], small["low"][:, :, :], ALU.add).then_inc(sem("logits_step"), 1)
                if n == 3:
                    ve.wait_ge(sem("logits_step"), 2)
                    v.reduce_max(few["top"][:, :], logits, AX).then_inc(routed, 1)
                    ve.wait_ge(routed, 1)
                    v.tensor_tensor(small["shift"][:, :, :], logits, spread("top"), ALU.subtract).then_inc(sem("logits_read"), 1)
                if n == 9:
                    ve.wait_ge(sem("h45_ready"), 2)
                    ve.wait_ge(sem("down_centred"), 1)
                    block_sums("h45", h45[:, :], 8)
                if n == 13:
                    less_means("h45", h45[:, :], 8).then_inc(sem("h45_centred"), 1)
                if n >= ROUTE_FROM:
                    route(n - ROUTE_FROM, n - ROUTE_FROM + 1)
            route(2 * CH - ROUTE_FROM, len(router_steps))

            ve.wait_ge(routed, len(router_steps) + 1)
            ve.wait_ge(sem("h45_centred"), 1)
            def sum_last(n):
                at = slice(n_before(n), n_before(n + 1))
                ve.wait_ge(sem("h6_ready"), parts_done)
                v.tensor_tensor(tiles(squares)[:, at], h6[:, at], h6[:, at], ALU.mult).then_inc(sem("lnf_squared"), 1)
                ve.wait_ge(sem("lnf_squared"), n + 1)
                v.reduce_sum(sq_sums[:, at], tiles(squares)[:, at], AX).then_inc(sem("lnf_sq_sum"), 1)

            def finish(n):
                at = slice(n_before(n), n_before(n + 1))
                ve.wait_ge(sem("lnf_std"), n + 1)
                v.reciprocal(rstd[:, at], std[:, at]).then_inc(sem("lnf_rstd"), 1)
                ve.wait_ge(sem("lnf_rstd"), n + 1)
                v.tensor_tensor(out_sb[:, at], h6[:, at], rstd[:, at].unsqueeze(2).to_broadcast([P, at.stop - at.start, D]),
                                ALU.mult).then_inc(sem("out_normed"), 1)

            group, parts_done = 0, 0
            for n in range(8):
                s, u = n // 4, n % 4
                for k in range(2 if n == 7 else 1):
                    ex = slice(4 * k, 4 * k + 4) if n == 7 else slice(0, NE)
                    bank = LAST_BANK if k else DOWN_BANKS[n % 4]
                    ve.wait_ge(sem("down_mm"), parts_done + 1)
                    w = weighted[:, parts_done % 2, ex]
                    v.tensor_tensor(w, PS[:, bank, ex.start * D:ex.stop * D].rearrange("q (e d) -> q e d", d=D),
                                    small["weights"][:, 2 * u + s, ex].unsqueeze(2).to_broadcast([P, ex.stop - ex.start, D]),
                                    ALU.mult).then_inc(sem("tile_weighted"), 1)
                    ve.wait_ge(sem("tile_weighted"), parts_done + 1)
                    v.reduce_sum(mixed[:, u, s, :], w.rearrange("q e d -> q d e"), AX).then_inc(sem("tile_mixed"), 1)
                    ve.wait_ge(sem("tile_mixed"), parts_done + 1)
                    base = h6[:, n] if k else h45[:, (2 * u + s) * D:(2 * u + s + 1) * D]
                    v.tensor_tensor(h6[:, n], mixed[:, u, s, :], base, ALU.add).then_inc(sem("h6_ready"), 1)
                    parts_done += 1
                if n + 1 in (n_before(1), n_before(2), n_before(3)):
                    sum_last(group)
                    group += 1
                if n == n_before(1):
                    finish(0)
            finish(1)
            finish(2)


def layouts(np, t):
    def w(name):
        return np.asarray(t[name])

    def both(m):
        return np.concatenate([m, m], axis=0)

    def diag(m):
        n = m.shape[1]
        z = np.zeros((P, 2 * n), np.float32)
        z[:D, :n] = m
        z[D:, n:] = m
        return z

    def col(vec):
        return both(vec.reshape(D, 1))

    def row(vec):
        return np.broadcast_to(vec.reshape(1, -1), (P, vec.size))

    def pack(names, parts):
        assert {k: v.shape[1] for k, v in parts.items()} == names, \
            {k: v.shape for k, v in parts.items() if v.shape[1] != names.get(k)}
        return np.ascontiguousarray(np.concatenate([parts[k] for k in names], axis=1))

    pos = np.arange(N, dtype=np.float32)[:, None]
    i = np.arange(0, D, 2, dtype=np.float32)
    ang = pos * np.exp(-np.log(np.float32(10000.0)) * i / np.float32(D)).astype(np.float32)
    pe = np.stack([np.sin(ang), np.cos(ang)], axis=-1).reshape(N, D).astype(np.float32)
    conv = w("L0_tok_conv_w").reshape(D, KCH, P).transpose(2, 1, 0).reshape(P, KCH * D)
    pack_a = pack(PACK_A, dict(
        ident=np.eye(P, dtype=np.float32), conv=conv, conv_b=col(w("L0_tok_conv_b")),
        centring=np.kron(np.eye(2), np.eye(D) - 1.0 / D).astype(np.float32), pos=both(pe.T),
        ln_w=col(w("L0_tok_ln_w")), ln_b=col(w("L0_tok_ln_b"))))

    qkv, qkv_b = w("L0_tok_qkv_w"), w("L0_tok_qkv_b")
    feature = np.arange(P)[:, None] % D
    pack_b = pack(PACK_B, dict(
        ff1=both(w("L0_tok_ff_w1").T), ff1_b=w("L0_tok_ff_b1").reshape(2, P).T,
        ff2=w("L0_tok_ff_w2").T.reshape(2, P, D).transpose(1, 0, 2).reshape(P, 2 * D), ff2_b=col(w("L0_tok_ff_b2")),
        wq=diag(qkv[0:D].T), wk=diag(qkv[D:2 * D].T), wv=diag(qkv[2 * D:].T), proj=diag(w("L0_tok_proj_w").T),
        bq=col(qkv_b[0:D]), bk=col(qkv_b[D:2 * D]), bv=col(qkv_b[2 * D:]), bp=col(w("L0_tok_proj_b")),
        head_mask=(feature // HD == np.arange(HEADS)[None, :]).astype(np.float32)))

    n = np.arange(N, dtype=np.float32)
    dist = np.abs(n[:, None] - n[None, :])
    two_pi = np.float32(2.0 * np.pi)
    cosines = np.concatenate([np.cos(two_pi * dist / np.float32(period)) for period in (24.0, 720.0)], axis=1)
    inv_freq = 1.0 / 10000.0 ** (np.arange(0, FHD, 2, dtype=np.float32) / FHD)
    freqs = np.outer(n, inv_freq)
    emb = np.concatenate([freqs, freqs], axis=-1)
    cos, sin = np.cos(emb).T.astype(np.float32), np.sin(emb).T.astype(np.float32)
    sign = np.where(np.arange(FHD) < FHD // 2, -1.0, 1.0)[:, None].astype(np.float32)
    turned = (np.arange(FHD) + FHD // 2) % FHD
    wq = w("L0_ffn_wq").reshape(FH, FHD, D)
    wk = w("L0_ffn_wk").reshape(FKV, FHD, D)[[h // (FH // FKV) for h in range(FH)]]
    causal = np.where(n[:, None] >= n[None, :], 0.0, -1e30).astype(np.float32)
    pack_c = pack(PACK_C, dict(
        aq=diag(w("L0_attn_Wq").T), ak=diag(w("L0_attn_Wk").T), av=diag(w("L0_attn_Wv").T),
        abq=col(w("L0_attn_bq")), abk=col(w("L0_attn_bk")), abv=row(w("L0_attn_bv")), beta=row(w("L0_attn_beta")),
        cosines=both(cosines.astype(np.float32)),
        fq=diag(wq.reshape(D, D).T), fq_turned=diag(wq[:, turned].reshape(D, D).T),
        fk=diag(wk.reshape(D, D).T), fk_turned=diag(wk[:, turned].reshape(D, D).T),
        fv=diag(w("L0_ffn_wv").T), fo=diag(w("L0_ffn_wo").T), router=both(w("L0_ffn_router_w").T),
        rope_cos=both(np.tile(cos, (FH, 1))), rope_sin=both(np.tile(sign * sin, (FH, 1))),
        causal=both(np.tile(causal, (1, 2))),
        fhead_mask=(feature // FHD % (FH // 2) == np.arange(FH // 2)[None, :]).astype(np.float32),
        rank=row(np.arange(NE, 0, -1).astype(np.float32)), ln1=col(w("L0_ffn_ln1_w")), ln2=col(w("L0_ffn_ln2_w"))))

    up = np.zeros((2, CH * P, D), np.float32)
    down = np.zeros((P, DOWN_AT[CH]), np.float32)
    w2 = w("L0_ffn_w2").transpose(0, 2, 1)
    for v, name in enumerate(("L0_ffn_w1", "L0_ffn_w3")):
        up[v, :NE * HID] = w(name).reshape(NE * HID, D)
    up = up.reshape(2, CH, P, D).transpose(1, 0, 2, 3)
    for ch in range(CH):
        for n, ex in enumerate(experts_of(ch)):
            r0, r1 = max(ch * P, ex * HID), min((ch + 1) * P, (ex + 1) * HID)
            down[r0 - ch * P:r1 - ch * P, DOWN_AT[ch] + n * D:DOWN_AT[ch] + (n + 1) * D] = w2[ex, r0 - ex * HID:r1 - ex * HID]
    pack_d = np.ascontiguousarray(both(up.reshape(2 * CH * P, D).T))
    return dict(x=np.ascontiguousarray(w("x")), pack_a=pack_a, pack_b=pack_b, pack_c=pack_c, pack_d=pack_d, pack_e=down)


def kernel(**inputs):
    import numpy as np
    import concourse.bacc as bacc
    from concourse.bass_utils import run_bass_kernel_spmd

    nc = bacc.Bacc("TRN2", target_bir_lowering=False, num_devices=1)
    arrays, args = {}, []
    for name, arr in layouts(np, inputs).items():
        arrays[name + "_dram"] = arr
        args.append(nc.dram_tensor(name + "_dram", arr.shape, mybir.dt.from_np(arr.dtype), kind="ExternalInput").ap())
    args.append(nc.dram_tensor("out_dram", (B, N, D), F32, kind="ExternalOutput").ap())
    build(nc, *args)
    r = run_bass_kernel_spmd(nc, [arrays], core_ids=[0])
    return r.results[0]["out_dram"]
```
